# Optimizing a Trainium2 kernel written in Bass

```python
import numpy as np
import jax
import jax.numpy as jnp

def _softmax(x, axis=-1):
    return jax.nn.softmax(x, axis=axis)

def _gelu(x):
    return jax.nn.gelu(x, approximate=True)

def _silu(x):
    return jax.nn.silu(x)

def _sigmoid(x):
    return jax.nn.sigmoid(x)

def _layernorm(x, axis=-1, eps=1e-05):
    m = jnp.mean(x, axis=axis, keepdims=True)
    v = jnp.var(x, axis=axis, keepdims=True)
    return (x - m) / jnp.sqrt(v + eps)

def _scatter_add(tgt, idx, src, axis=0):
    return tgt.at[idx].add(src)

def _segment_sum(src, seg, n):
    return jax.ops.segment_sum(src, seg, n)
kernel_name = 'mk_prb_d2_jaxref_r8_796616'

def setup_inputs(seed: int=0):
    np.random.seed(seed)
    _w = jnp.asarray

    def _L0_attn_setup():
        import jax, jax.numpy as jnp
        import numpy as np
        import math
        D_MODEL = 128
        N_HEAD = 16
        HEAD_DIM = D_MODEL // N_HEAD

        def _split_heads(t):
            B, S, _ = t.shape
            return t.reshape(B, S, N_HEAD, HEAD_DIM).transpose(0, 2, 1, 3)
        key = jax.random.key(seed)
        ks = jax.random.split(key, 9)
        B, S = (2, 256)
        x = jax.random.normal(ks[0], (B, S, D_MODEL), dtype=jnp.float32)
        w = lambda k, std: jax.random.normal(k, (D_MODEL, D_MODEL), dtype=jnp.float32) * std
        return {'x': x, 'Wq_amp': w(ks[1], 0.02), 'Wk_amp': w(ks[2], 0.02), 'Wq_phi': w(ks[3], 0.005), 'Wk_phi': w(ks[4], 0.005), 'Wv': w(ks[5], 0.02), 'Wo': w(ks[6], 0.02), 'score_log_scale': jnp.zeros((N_HEAD,), dtype=jnp.float32)}
    _L0_attn_in = _L0_attn_setup()

    def _L0_ffn_setup():
        import jax, jax.numpy as jnp
        import numpy as np
        D = 128
        H = 4
        DF = 512
        E = 8
        EPS = 1e-05

        def _layer_norm(x, g, b):
            mu = jnp.mean(x, axis=-1, keepdims=True)
            var = jnp.mean(jnp.square(x - mu), axis=-1, keepdims=True)
            return (x - mu) * jax.lax.rsqrt(var + EPS) * g + b

        def _mha(x, Wqkv, bqkv, Wo, bo):
            S, B, _ = x.shape
            hd = D // H
            qkv = x @ Wqkv.T + bqkv
            q, k, v = jnp.split(qkv, 3, axis=-1)
            to_heads = lambda t: t.reshape(S, B, H, hd).transpose(1, 2, 0, 3)
            q, k, v = (to_heads(q), to_heads(k), to_heads(v))
            scores = jnp.einsum('bhqd,bhkd->bhqk', q, k) * (1.0 / np.sqrt(hd))
            att = jax.nn.softmax(scores, axis=-1)
            o = jnp.einsum('bhqk,bhkd->bhqd', att, v)
            o = o.transpose(2, 0, 1, 3).reshape(S, B, D)
            return o @ Wo.T + bo

        def _moe(x, Wg, W1, b1, W2, b2):
            S, B, _ = x.shape
            xf = x.reshape(S * B, D)
            logits = xf @ Wg.T
            idx = jnp.argmax(logits, axis=-1)
            out = jnp.zeros_like(xf)
            for e in range(E):
                m = (idx == e)[:, None].astype(xf.dtype)
                h = jax.nn.relu(xf @ W1[e] + b1[e])
                out = out + m * (h @ W2[e] + b2[e])
            return out.reshape(S, B, D)
        key = jax.random.key(seed)
        ks = jax.random.split(key, 16)
        S, B = (64, 8)
        s = lambda k, shape, fan: jax.random.normal(k, shape, jnp.float32) * (1.0 / np.sqrt(fan))
        return {'x': jax.random.normal(ks[0], (S, B, D), jnp.float32), 'Wqkv': s(ks[1], (3 * D, D), D), 'bqkv': jnp.zeros((3 * D,), jnp.float32), 'Wo': s(ks[2], (D, D), D), 'bo': jnp.zeros((D,), jnp.float32), 'g1': jnp.ones((D,), jnp.float32), 'be1': jnp.zeros((D,), jnp.float32), 'g2': jnp.ones((D,), jnp.float32), 'be2': jnp.zeros((D,), jnp.float32), 'Wg': s(ks[3], (E, D), D), 'W1': s(ks[4], (E, D, DF), D), 'b1': jnp.zeros((E, DF), jnp.float32), 'W2': s(ks[5], (E, DF, D), DF), 'b2': jnp.zeros((E, D), jnp.float32)}
    _L0_ffn_in = _L0_ffn_setup()

    def _L1_attn_setup():
        import jax, jax.numpy as jnp
        import numpy as np
        B, S, H, NH = (2, 256, 128, 16)
        HD = H // NH
        key = jax.random.key(seed)
        ks = jax.random.split(key, 9)
        sc = 0.02
        return {'hidden_states': jax.random.normal(ks[0], (B, S, H), jnp.float32), 'Wq': jax.random.normal(ks[1], (H, H), jnp.float32) * sc, 'bq': jax.random.normal(ks[2], (H,), jnp.float32) * sc, 'Wk': jax.random.normal(ks[3], (H, H), jnp.float32) * sc, 'bk': jax.random.normal(ks[4], (H,), jnp.float32) * sc, 'Wv': jax.random.normal(ks[5], (H, H), jnp.float32) * sc, 'bv': jax.random.normal(ks[6], (H,), jnp.float32) * sc, 'Wo': jax.random.normal(ks[7], (H, H), jnp.float32) * sc, 'bo': jax.random.normal(ks[8], (H,), jnp.float32) * sc}
    _L1_attn_in = _L1_attn_setup()

    def _L1_ffn_setup():
        import jax, jax.numpy as jnp
        import numpy as np
        TOP_K = 2

        def _route(x2d, gate_w, num_experts, top_k):
            scores = jax.nn.softmax((x2d @ gate_w.T).astype(jnp.float32), axis=1)
            top_scores, sel = jax.lax.top_k(scores, top_k)
            sel_flat = sel.reshape(-1)
            counts = jnp.bincount(sel_flat, length=num_experts)
            order = jnp.argsort(sel_flat, stable=True)
            top_scores_sorted = top_scores.reshape(-1)[order]
            token_idx = order // top_k
            return (top_scores_sorted, token_idx, counts)

        def _grouped_swiglu(xr, w1, w2, w3, eid):
            out = jnp.zeros((xr.shape[0], w2.shape[-1]), dtype=xr.dtype)
            for e in range(w1.shape[0]):
                xe = jnp.where((eid == e)[:, None], xr, 0.0)
                h = jax.nn.silu(xe @ w1[e]) * (xe @ w3[e])
                out = out + h @ w2[e]
            return out
        key = jax.random.key(seed)
        ks = jax.random.split(key, 5)
        bs, slen, dim, hidden, E = (2, 256, 128, 352, 8)
        x = jax.random.normal(ks[0], (bs, slen, dim), dtype=jnp.float32)
        gate_w = jax.random.normal(ks[1], (E, dim), dtype=jnp.float32) * 0.02
        w1 = jax.random.normal(ks[2], (E, dim, hidden), dtype=jnp.float32) * 0.02
        w2 = jax.random.normal(ks[3], (E, hidden, dim), dtype=jnp.float32) * 0.02
        w3 = jax.random.normal(ks[4], (E, dim, hidden), dtype=jnp.float32) * 0.02
        return {'x': x, 'gate_w': gate_w, 'w1': w1, 'w2': w2, 'w3': w3}
    _L1_ffn_in = _L1_ffn_setup()
    _d = {'L0_attn_x': _L0_attn_in['x'], 'L0_attn_Wq_amp': _L0_attn_in['Wq_amp'], 'L0_attn_Wk_amp': _L0_attn_in['Wk_amp'], 'L0_attn_Wq_phi': _L0_attn_in['Wq_phi'], 'L0_attn_Wk_phi': _L0_attn_in['Wk_phi'], 'L0_attn_Wv': _L0_attn_in['Wv'], 'L0_attn_Wo': _L0_attn_in['Wo'], 'L0_attn_score_log_scale': _L0_attn_in['score_log_scale'], 'L0_ffn_Wqkv': _L0_ffn_in['Wqkv'], 'L0_ffn_bqkv': _L0_ffn_in['bqkv'], 'L0_ffn_Wo': _L0_ffn_in['Wo'], 'L0_ffn_bo': _L0_ffn_in['bo'], 'L0_ffn_g1': _L0_ffn_in['g1'], 'L0_ffn_be1': _L0_ffn_in['be1'], 'L0_ffn_g2': _L0_ffn_in['g2'], 'L0_ffn_be2': _L0_ffn_in['be2'], 'L0_ffn_Wg': _L0_ffn_in['Wg'], 'L0_ffn_W1': _L0_ffn_in['W1'], 'L0_ffn_b1': _L0_ffn_in['b1'], 'L0_ffn_W2': _L0_ffn_in['W2'], 'L0_ffn_b2': _L0_ffn_in['b2'], 'L1_attn_Wq': _L1_attn_in['Wq'], 'L1_attn_bq': _L1_attn_in['bq'], 'L1_attn_Wk': _L1_attn_in['Wk'], 'L1_attn_bk': _L1_attn_in['bk'], 'L1_attn_Wv': _L1_attn_in['Wv'], 'L1_attn_bv': _L1_attn_in['bv'], 'L1_attn_Wo': _L1_attn_in['Wo'], 'L1_attn_bo': _L1_attn_in['bo'], 'L1_ffn_gate_w': _L1_ffn_in['gate_w'], 'L1_ffn_w1': _L1_ffn_in['w1'], 'L1_ffn_w2': _L1_ffn_in['w2'], 'L1_ffn_w3': _L1_ffn_in['w3']}
    _x0 = _d['L0_attn_x']
    _d['L0_attn_x'] = jax.random.normal(jax.random.fold_in(jax.random.key(seed), 1), (8, 512, 128), dtype=_x0.dtype)
    del _x0
    return _d

def reference(L0_attn_x, L0_attn_Wq_amp, L0_attn_Wk_amp, L0_attn_Wq_phi, L0_attn_Wk_phi, L0_attn_Wv, L0_attn_Wo, L0_attn_score_log_scale, L0_ffn_Wqkv, L0_ffn_bqkv, L0_ffn_Wo, L0_ffn_bo, L0_ffn_g1, L0_ffn_be1, L0_ffn_g2, L0_ffn_be2, L0_ffn_Wg, L0_ffn_W1, L0_ffn_b1, L0_ffn_W2, L0_ffn_b2, L1_attn_Wq, L1_attn_bq, L1_attn_Wk, L1_attn_bk, L1_attn_Wv, L1_attn_bv, L1_attn_Wo, L1_attn_bo, L1_ffn_gate_w, L1_ffn_w1, L1_ffn_w2, L1_ffn_w3):

    def _L0_attn_ref(x, Wq_amp, Wk_amp, Wq_phi, Wk_phi, Wv, Wo, score_log_scale):
        import jax, jax.numpy as jnp
        import numpy as np
        import math
        D_MODEL = 128
        N_HEAD = 16
        HEAD_DIM = D_MODEL // N_HEAD

        def _split_heads(t):
            B, S, _ = t.shape
            return t.reshape(B, S, N_HEAD, HEAD_DIM).transpose(0, 2, 1, 3)
        B, S, _ = x.shape
        eps = 1e-06
        q_amp = _split_heads(jax.nn.softplus(x @ Wq_amp.T))
        k_amp = _split_heads(jax.nn.softplus(x @ Wk_amp.T))
        q_phi = _split_heads(math.pi * jnp.tanh(x @ Wq_phi.T))
        k_phi = _split_heads(math.pi * jnp.tanh(x @ Wk_phi.T))
        q_amp = q_amp / jnp.sqrt(jnp.mean(q_amp * q_amp, axis=-1, keepdims=True) + eps)
        k_amp = k_amp / jnp.sqrt(jnp.mean(k_amp * k_amp, axis=-1, keepdims=True) + eps)
        q_cos = q_amp * jnp.cos(q_phi)
        q_sin = q_amp * jnp.sin(q_phi)
        k_cos = k_amp * jnp.cos(k_phi)
        k_sin = k_amp * jnp.sin(k_phi)
        scores = (jnp.einsum('bhqd,bhkd->bhqk', q_cos, k_cos) + jnp.einsum('bhqd,bhkd->bhqk', q_sin, k_sin)) / math.sqrt(HEAD_DIM)
        scores = scores * jnp.exp(score_log_scale)[None, :, None, None]
        mask = jnp.tril(jnp.ones((S, S), dtype=bool))
        scores = jnp.where(mask[None, None], scores, -jnp.inf)
        attn = jax.nn.softmax(scores, axis=-1)
        v = _split_heads(x @ Wv.T)
        out = jnp.einsum('bhqk,bhkd->bhqd', attn, v)
        out = out.transpose(0, 2, 1, 3).reshape(B, S, D_MODEL)
        return out @ Wo.T

    def _L0_ffn_ref(x, Wqkv, bqkv, Wo, bo, g1, be1, g2, be2, Wg, W1, b1, W2, b2):
        import jax, jax.numpy as jnp
        import numpy as np
        D = 128
        H = 4
        DF = 512
        E = 8
        EPS = 1e-05

        def _layer_norm(x, g, b):
            mu = jnp.mean(x, axis=-1, keepdims=True)
            var = jnp.mean(jnp.square(x - mu), axis=-1, keepdims=True)
            return (x - mu) * jax.lax.rsqrt(var + EPS) * g + b

        def _mha(x, Wqkv, bqkv, Wo, bo):
            S, B, _ = x.shape
            hd = D // H
            qkv = x @ Wqkv.T + bqkv
            q, k, v = jnp.split(qkv, 3, axis=-1)
            to_heads = lambda t: t.reshape(S, B, H, hd).transpose(1, 2, 0, 3)
            q, k, v = (to_heads(q), to_heads(k), to_heads(v))
            scores = jnp.einsum('bhqd,bhkd->bhqk', q, k) * (1.0 / np.sqrt(hd))
            att = jax.nn.softmax(scores, axis=-1)
            o = jnp.einsum('bhqk,bhkd->bhqd', att, v)
            o = o.transpose(2, 0, 1, 3).reshape(S, B, D)
            return o @ Wo.T + bo

        def _moe(x, Wg, W1, b1, W2, b2):
            S, B, _ = x.shape
            xf = x.reshape(S * B, D)
            logits = xf @ Wg.T
            idx = jnp.argmax(logits, axis=-1)
            out = jnp.zeros_like(xf)
            for e in range(E):
                m = (idx == e)[:, None].astype(xf.dtype)
                h = jax.nn.relu(xf @ W1[e] + b1[e])
                out = out + m * (h @ W2[e] + b2[e])
            return out.reshape(S, B, D)
        y = _layer_norm(x + _mha(x, Wqkv, bqkv, Wo, bo), g1, be1)
        z = _layer_norm(y + _moe(y, Wg, W1, b1, W2, b2), g2, be2)
        return z

    def _L1_attn_ref(hidden_states, Wq, bq, Wk, bk, Wv, bv, Wo, bo):
        import jax, jax.numpy as jnp
        import numpy as np
        B, S, H, NH = (2, 256, 128, 16)
        HD = H // NH
        b, s, h = hidden_states.shape
        q = hidden_states @ Wq.T + bq
        k = hidden_states @ Wk.T + bk
        v = hidden_states @ Wv.T + bv
        q = q.reshape(b, s, NH, HD).transpose(0, 2, 1, 3)
        k = k.reshape(b, s, NH, HD).transpose(0, 2, 1, 3)
        v = v.reshape(b, s, NH, HD).transpose(0, 2, 1, 3)
        scores = jnp.einsum('bhqd,bhkd->bhqk', q, k) / jnp.sqrt(jnp.float32(HD))
        causal = jnp.triu(jnp.ones((s, s), dtype=bool), k=1)
        scores = jnp.where(causal, -jnp.inf, scores)
        attn = jax.nn.softmax(scores, axis=-1)
        ctx = jnp.einsum('bhqk,bhkd->bhqd', attn, v)
        ctx = ctx.transpose(0, 2, 1, 3).reshape(b, s, h)
        return ctx @ Wo.T + bo

    def _L1_ffn_ref(x, gate_w, w1, w2, w3):
        import jax, jax.numpy as jnp
        import numpy as np
        TOP_K = 2

        def _route(x2d, gate_w, num_experts, top_k):
            scores = jax.nn.softmax((x2d @ gate_w.T).astype(jnp.float32), axis=1)
            top_scores, sel = jax.lax.top_k(scores, top_k)
            sel_flat = sel.reshape(-1)
            counts = jnp.bincount(sel_flat, length=num_experts)
            order = jnp.argsort(sel_flat, stable=True)
            top_scores_sorted = top_scores.reshape(-1)[order]
            token_idx = order // top_k
            return (top_scores_sorted, token_idx, counts)

        def _grouped_swiglu(xr, w1, w2, w3, eid):
            out = jnp.zeros((xr.shape[0], w2.shape[-1]), dtype=xr.dtype)
            for e in range(w1.shape[0]):
                xe = jnp.where((eid == e)[:, None], xr, 0.0)
                h = jax.nn.silu(xe @ w1[e]) * (xe @ w3[e])
                out = out + h @ w2[e]
            return out
        bs, slen, dim = x.shape
        E, top_k = (gate_w.shape[0], TOP_K)
        x2d = x.reshape(bs * slen, dim)
        top_scores, token_idx, counts = _route(x2d, gate_w, E, top_k)
        routed_in = (x2d[token_idx].astype(jnp.float32) * top_scores[:, None]).astype(x.dtype)
        Tr = bs * slen * top_k
        eid = jnp.repeat(jnp.arange(E), counts, total_repeat_length=Tr)
        routed_out = _grouped_swiglu(routed_in, w1, w2, w3, eid)
        out = jnp.zeros((bs * slen, dim), dtype=x.dtype).at[token_idx].add(routed_out)
        return out.reshape(bs, slen, dim)
    x = L0_attn_x
    xn = _layernorm(x, axis=-1)
    x = x + _L0_attn_ref(xn, L0_attn_Wq_amp, L0_attn_Wk_amp, L0_attn_Wq_phi, L0_attn_Wk_phi, L0_attn_Wv, L0_attn_Wo, L0_attn_score_log_scale) + _L0_ffn_ref(xn, L0_ffn_Wqkv, L0_ffn_bqkv, L0_ffn_Wo, L0_ffn_bo, L0_ffn_g1, L0_ffn_be1, L0_ffn_g2, L0_ffn_be2, L0_ffn_Wg, L0_ffn_W1, L0_ffn_b1, L0_ffn_W2, L0_ffn_b2)
    xn = _layernorm(x, axis=-1)
    x = x + _L1_attn_ref(xn, L1_attn_Wq, L1_attn_bq, L1_attn_Wk, L1_attn_bk, L1_attn_Wv, L1_attn_bv, L1_attn_Wo, L1_attn_bo) + _L1_ffn_ref(xn, L1_ffn_gate_w, L1_ffn_w1, L1_ffn_w2, L1_ffn_w3)
    return x

_drawn_inputs = setup_inputs


def setup_inputs(seed=0):
    import zlib

    import numpy as np

    out = dict(_drawn_inputs(seed))
    spreads = {'L0_attn_score_log_scale': (0.0, 0.8),
     'L0_ffn_bqkv': (0.0, 0.1),
     'L0_ffn_bo': (0.0, 0.1),
     'L0_ffn_g1': (1.0, 0.2),
     'L0_ffn_be1': (0.0, 0.1),
     'L0_ffn_g2': (1.0, 0.2),
     'L0_ffn_be2': (0.0, 0.1),
     'L0_ffn_b1': (0.0, 0.268),
     'L0_ffn_b2': (0.0, 0.1)}
    factors = {'L0_attn_Wq_amp': 8.0,
     'L0_attn_Wk_amp': 8.0,
     'L0_attn_Wq_phi': 8.0,
     'L0_attn_Wk_phi': 8.0,
     'L0_attn_Wv': 8.0,
     'L0_attn_Wo': 8.0,
     'L1_attn_Wq': 8.0,
     'L1_attn_bq': 8.0,
     'L1_attn_Wk': 8.0,
     'L1_attn_bk': 8.0,
     'L1_attn_Wv': 8.0,
     'L1_attn_bv': 8.0,
     'L1_attn_Wo': 8.0,
     'L1_attn_bo': 5.065,
     'L1_ffn_gate_w': 8.0,
     'L1_ffn_w1': 8.0,
     'L1_ffn_w2': 8.0,
     'L1_ffn_w3': 8.0}
    for name, (base, spread) in spreads.items():
        noise = np.random.default_rng([zlib.crc32(name.encode()), seed]).standard_normal(out[name].shape)
        drawn = base * np.exp(spread * noise) if base else spread * noise
        out[name] = jnp.asarray(drawn.astype(out[name].dtype))
    for name, factor in factors.items():
        out[name] = (out[name] * factor).astype(out[name].dtype)
    return out
```

```python
from contextlib import ExitStack

import numpy as np

import concourse.bass as bass
from concourse import mybir

F32 = mybir.dt.float32
BF16 = mybir.dt.bfloat16
I32 = mybir.dt.int32
U32 = mybir.dt.uint32
ALU = mybir.AluOpType
ACT = mybir.ActivationFunctionType
X_AXIS = mybir.AxisListType.X

P = 128
B, S, D = 8, 512, 128
T = B * S
NT = T // P
NH = 16
HD = D // NH
MH = 4
MD = D // MH
E = 8
DF = 512
HID = 352
QT = S // P
GH = 4
NG = NH // GH
ROWS = 2 * P
TILES = (T // ROWS + E - 1, 2 * T // ROWS + E - 1)
POS = P // B
LN_EPS = 1e-5
AMP_EPS = 1e-6
NEG = -1e30
PI = float(np.pi)

Q_PARTS = (0, 1, 0, 2, 0, 1)
K_PARTS = (0, 0, 1, 0, 2, 1)
SLOTS = len(Q_PARTS)
K0, K1 = SLOTS * 2 * HD, SLOTS * HD

(W_QA, W_KA, W_QP, W_KP, W_V0, W_O0, W_MQ, W_MK, W_MV, W_MO, W_Q1, W_K1, W_V1, W_O1) = range(14)
C_MQ, C_MK, C_Q1, C_K1, C_HS, C_PIH, C_EPS = range(7)
R_MV, R_MO, R_G1, R_BE1, R_G2, R_BE2, R_V1, R_O1 = range(8)


class Kept:
    pass


class Signal:

    def __init__(self, sem, per=1, by=1):
        self.sem, self.per, self.by = sem, per, by

    def after(self, unit, k=0):
        return (n_of(unit) * self.per + k + 1) * self.by

    def done(self, unit):
        return (n_of(unit) + 1) * self.per * self.by


def n_of(unit):
    return unit.n if isinstance(unit, Unit) else unit


class Unit:

    def __init__(self, turn, phase, cycle=2):
        self.turn, self.phase, self.cycle = turn, phase, cycle

    @property
    def n(self):
        return self.turn * self.cycle + self.phase

    @property
    def par(self):
        return self.phase % 2

    @property
    def pair(self):
        return self.turn * (self.cycle // 2) + self.phase // 2

    @property
    def group(self):
        return self.phase % NG

    @property
    def row(self):
        return self.turn * (self.cycle // NG) + self.phase // NG

    @property
    def row_par(self):
        return self.phase // NG % 2

    def __sub__(self, k):
        return Unit(self.turn + (self.phase - k) // self.cycle, (self.phase - k) % self.cycle, self.cycle)

    def __add__(self, k):
        return self - (-k)

    def past(self, k):
        return not isinstance(self.turn, int) or self.n >= k


def in_steps(eng, units, depth, step, cycle=2):
    first = max(4, cycle)
    turns = (units - first) // cycle
    for t in range(first):
        step(Unit(t // cycle, t % cycle, cycle))
    with eng.Fori(0, turns) as i:
        for phase in range(cycle):
            step(Unit(i + first // cycle, phase, cycle))
    for t in range(first + cycle * turns, units + depth - 1):
        step(Unit(t // cycle, t % cycle, cycle))


def active(t, k, units):
    return not isinstance(t.turn, int) or 0 <= t.n - k < units


def wide(row):
    return row.unsqueeze(1).broadcast_to([P, QT, D])


def phase_resources(nc, ctx, phase):
    def sb(name, shape, dtype=F32):
        return ctx.enter_context(nc.sbuf_tensor(f"{phase}_{name}", shape, dtype))

    def banks(name, n):
        return ctx.enter_context(nc.psum_tensor(f"{phase}_{name}", [P, n, 512], F32))

    numbers = []

    def clear():
        with nc.Block() as block:
            @block.sync
            def _(sp):
                for n in sorted(numbers):
                    if n - 1 not in numbers:
                        end = n
                        while end in numbers:
                            end += 1
                        sp.sem_clear(range(n, end))

    ctx.callback(clear)

    def signal(name, per=1, by=1):
        sem = ctx.enter_context(nc.semaphore(f"{phase}_{name}"))
        numbers.append(sem.num)
        return Signal(sem, per, by)

    return sb, banks, signal




def setup(nc, k):
    with ExitStack() as ctx:
        sb, banks, signal = phase_resources(nc, ctx, "setup")
        wraw = sb("wraw", [P, 14, D])
        graw = sb("graw", [E, 2, D])
        zeros = sb("zeros", [P, 2, ROWS * D // P])
        turned_ps = banks("turned_ps", 4)
        raw_in = [signal(f"raw_in{i}", by=16) for i in range(14)]
        gate_in = signal("gate_in", per=2, by=16)
        rows_in = signal("rows_in", per=8, by=16)
        cols_in = signal("cols_in", per=6, by=16)
        base_set = signal("base_set")
        ident_ready = signal("ident_ready")
        turned = signal("turned")
        copied = signal("copied")
        zero_set = signal("zero_set")
        zero_out = signal("zero_out", by=16)
        scale_exp = signal("scale_exp")
        scale_ready = signal("scale_ready")
        block = ctx.enter_context(nc.Block())
        squares = [k.arg["L0_attn_Wq_amp"], k.arg["L0_attn_Wk_amp"], k.arg["L0_attn_Wq_phi"], k.arg["L0_attn_Wk_phi"], k.arg["L0_attn_Wv"],
                   k.arg["L0_attn_Wo"], k.arg["L0_ffn_Wqkv"][0:D], k.arg["L0_ffn_Wqkv"][D:2 * D], k.arg["L0_ffn_Wqkv"][2 * D:3 * D],
                   k.arg["L0_ffn_Wo"], k.arg["L1_attn_Wq"], k.arg["L1_attn_Wk"], k.arg["L1_attn_Wv"], k.arg["L1_attn_Wo"]]

        @block.sync
        def _(sp):
            for n in range(0, 14, 2):
                sp.dma_start(wraw[:, n, :], squares[n]).then_inc(raw_in[n].sem, 16)
            sp.dma_start(graw[:, 0, :], k.arg["L0_ffn_Wg"]).then_inc(gate_in.sem, 16)
            sp.dma_start(graw[:, 1, :], k.arg["L1_ffn_gate_w"]).then_inc(gate_in.sem, 16)
            sp.wait_ge(zero_set.sem, 1)
            n = 0
            for layer, dst in enumerate((k.sorted0, k.sorted1)):
                for a in range(0, TILES[layer], 2):
                    m = min(2, TILES[layer] - a)
                    sp.dma_start(dst[a * ROWS:(a + m) * ROWS, :].rearrange("(a p r) d -> p a (r d)", a=m, p=P),
                                 zeros[:, 0:m, :]).then_inc(zero_out.sem, 16)
                    n += 1
            sp.wait_ge(zero_out.sem, 16 * n)

        @block.scalar
        def _(act):
            for n in range(1, 14, 2):
                act.dma_start(wraw[:, n, :], squares[n]).then_inc(raw_in[n].sem, 16)
            rows = [k.arg["L0_ffn_bqkv"][2 * D:3 * D], k.arg["L0_ffn_bo"], k.arg["L0_ffn_g1"], k.arg["L0_ffn_be1"], k.arg["L0_ffn_g2"],
                    k.arg["L0_ffn_be2"], k.arg["L1_attn_bv"], k.arg["L1_attn_bo"]]
            for n, row in enumerate(rows):
                act.dma_start(k.row[:, n, :], row.rearrange("(o d) -> o d", o=1).partition_broadcast(P))\
                   .then_inc(rows_in.sem, 16)
            cols = [k.arg["L0_ffn_bqkv"][0:D], k.arg["L0_ffn_bqkv"][D:2 * D], k.arg["L1_attn_bq"], k.arg["L1_attn_bk"]]
            for n, col in enumerate(cols):
                act.dma_start(k.col[:, n:n + 1], col.rearrange("(d o) -> d o", o=1)).then_inc(cols_in.sem, 16)
            act.dma_start(k.col[:, C_HS:C_HS + 1],
                          k.arg["L0_attn_score_log_scale"].rearrange("(h o) -> h o", o=1).broadcast_to([NH, HD]))\
               .then_inc(cols_in.sem, 16)
            act.wait_ge(cols_in.sem, 5 * 16)
            act.activation(k.hscale[:, :], k.col[:, C_HS:C_HS + 1], ACT.Exp).then_inc(scale_exp.sem, 1)
            for n in range(4):
                act.wait_ge(turned.sem, min(4 * n + 4, 14))
                m = min(4, 14 - 4 * n)
                act.copy(k.wT[:, 4 * n:4 * n + m, :], turned_ps[:, n, 0:m * D]).then_inc(copied.sem, 1)
            act.wait_ge(turned.sem, 15)
            act.copy(k.gateT[:, :, :], turned_ps[:, 3, 256:256 + 2 * E]).then_inc(copied.sem, 1)
            act.wait_ge(rows_in.sem, 8 * 16)

        @block.gpsimd
        def _(pool):
            pool.memset(k.ident[:, :], 0.0).then_inc(base_set.sem, 1)
            pool.wait_ge(base_set.sem, 1)
            pool.affine_select(out=k.ident[:, :], in_=k.ident[:, :], compare_op=ALU.not_equal, fill=1.0, base=0,
                               pattern=[[-1, P]], channel_multiplier=1).then_inc(ident_ready.sem, 1)
            pool.memset(zeros[:, :, :], 0.0).then_inc(zero_set.sem, 1)
            pool.memset(k.causal_q[:, :], 0.0).then_inc(base_set.sem, 1)
            pool.memset(k.causal_k[:, :], 0.0).then_inc(base_set.sem, 1)
            pool.memset(k.batch_mask[:, :], NEG).then_inc(base_set.sem, 1)
            pool.memset(k.before[:, :], 1.0).then_inc(base_set.sem, 1)
            pool.memset(k.ones[:, :], 1.0).then_inc(base_set.sem, 1)
            pool.memset(k.head_mean[:, :], 1.0 / HD).then_inc(base_set.sem, 1)
            pool.memset(k.half[:, :], -0.5).then_inc(base_set.sem, 1)
            pool.memset(k.ln_eps[:, :], LN_EPS).then_inc(base_set.sem, 1)
            pool.memset(k.col[:, C_PIH:C_PIH + 1], PI / 2).then_inc(base_set.sem, 1)
            pool.memset(k.col[:, C_EPS:C_EPS + 1], AMP_EPS).then_inc(base_set.sem, 1)
            pool.wait_ge(ident_ready.sem, 1)
            pool.tensor_copy(k.identb[:, :], k.ident[:, :]).then_inc(ident_ready.sem, 1)
            pool.wait_ge(base_set.sem, 11)
            pool.affine_select(out=k.causal_q[:, :], in_=k.causal_q[:, :], compare_op=ALU.is_ge, fill=NEG, base=0,
                               pattern=[[-1, P]], channel_multiplier=1).then_inc(base_set.sem, 1)
            pool.affine_select(out=k.causal_k[:, :], in_=k.causal_k[:, :], compare_op=ALU.is_ge, fill=NEG, base=0,
                               pattern=[[1, P]], channel_multiplier=-1).then_inc(base_set.sem, 1)
            pool.affine_select(out=k.before[:, :], in_=k.before[:, :], compare_op=ALU.is_gt, fill=0.0, base=0,
                               pattern=[[1, P]], channel_multiplier=-1).then_inc(base_set.sem, 1)
            head = k.head_mean[:, :].rearrange("p (h d) -> p h d", d=HD)
            pool.affine_select(out=head, in_=head, compare_op=ALU.is_ge, fill=0.0, base=0,
                               pattern=[[-HD, NH], [0, HD]], channel_multiplier=1).then_inc(base_set.sem, 1)
            pool.wait_ge(base_set.sem, 15)
            pool.affine_select(out=head, in_=head, compare_op=ALU.is_ge, fill=0.0, base=HD - 1,
                               pattern=[[HD, NH], [0, HD]], channel_multiplier=-1).then_inc(base_set.sem, 1)
            for n, m in enumerate(range(-(B - 1), B)):
                pool.wait_ge(base_set.sem, 16 + n)
                pool.affine_select(out=k.batch_mask[:, :], in_=k.batch_mask[:, :], compare_op=ALU.not_equal,
                                   fill=0.0, base=-POS * m, pattern=[[-1, P]], channel_multiplier=1)\
                    .then_inc(base_set.sem, 1)
            pool.iota(k.counted_i[:, :], pattern=[[1, 64]], base=0, channel_multiplier=0)\
                .then_inc(base_set.sem, 1)
            pool.wait_ge(base_set.sem, 32)
            pool.tensor_copy(k.counted[:, :], k.counted_i[:, :]).then_inc(base_set.sem, 1)
            pool.wait_ge(base_set.sem, 33)

        @block.tensor
        def _(pe):
            pe.wait_ge(ident_ready.sem, 1)
            for n in range(14):
                pe.wait_ge(raw_in[n].sem, 16)
                pe.transpose(turned_ps[:, n // 4, n % 4 * D:(n % 4 + 1) * D], wraw[:, n, :], k.ident[:, :])\
                  .then_inc(turned.sem, 1)
            pe.wait_ge(gate_in.sem, 32)
            pe.wait_ge(copied.sem, 4)
            pe.transpose(turned_ps[:, 3, 256:256 + E], graw[:, 0, :], k.ident[0:E, 0:E])
            pe.transpose(turned_ps[:, 3, 256 + E:256 + 2 * E], graw[:, 1, :], k.ident[0:E, 0:E])\
              .then_inc(turned.sem, 1)

        @block.vector
        def _(dve):
            dve.wait_ge(scale_exp.sem, 1)
            dve.tensor_scalar(k.hscale[:, :], k.hscale[:, :], float(HD) ** -0.5, None, ALU.mult)\
               .then_inc(scale_ready.sem, 1)
            dve.wait_ge(scale_ready.sem, 1)




def ln_stats(dve, src, stats, mv, stats_done, mv_done, unit, src_ready=None):
    if src_ready:
        dve.wait_ge(src_ready.sem, src_ready.done(unit))
    for j in range(QT):
        dve.bn_stats(stats[:, j, 0:6], src[:, j, :]).then_inc(stats_done.sem, 1)
    dve.wait_ge(stats_done.sem, stats_done.done(unit))
    dve.tensor_copy(stats[:, 0, 6:7], stats[:, 0, 0:1])
    for j in range(QT):
        dve.bn_aggr(mv[:, j, :], stats[:, j, 0:6]).then_inc(mv_done.sem, 1)


def ln_rstd(pool, k, mv, var_eps, rstd, mv_done, eps_done, rstd_done, unit):
    pool.wait_ge(mv_done.sem, mv_done.done(unit))
    pool.tensor_tensor(var_eps[:, :], mv[:, :, 1], k.ln_eps[:, :], ALU.add).then_inc(eps_done.sem, 1)
    pool.wait_ge(eps_done.sem, eps_done.done(unit))
    pool.tensor_tensor(rstd[:, :], var_eps[:, :], k.half[:, :], ALU.pow).then_inc(rstd_done.sem, 1)


def ln_apply(dve, dst, src, mv, rstd, rstd_done, xn_done, unit):
    dve.wait_ge(rstd_done.sem, rstd_done.done(unit))
    for j in range(QT):
        dve.tensor_scalar(dst[:, j, :], src[:, j, :], mv[:, j, 0:1], rstd[:, j:j + 1], ALU.subtract, ALU.mult)\
           .then_inc(xn_done.sem, 1)




def mix0(nc, k):
    UNITS = T // (QT * P)
    with ExitStack() as ctx:
        sb, banks, signal = phase_resources(nc, ctx, "mix0")
        x_tile = sb("x_tile", [P, 2, QT, D])
        xn = sb("xn", [P, 2, QT, D])
        xnT = sb("xnT", [P, QT * P])
        qT = sb("qT", [P, 2, QT * P])
        k_heads = sb("k_heads", [P, 2, QT, MH, P])
        v = sb("v", [P, 2, QT, D])
        probs = sb("probs", [P, 2, MH, P])
        probsT = sb("probsT", [P, 2, MH, P])
        neg_max = sb("neg_max", [P, 2, MH])
        sums = sb("sums", [P, 2, MH])
        rsums = sb("rsums", [P, 2, MH])
        mixedT = sb("mixedT", [P, QT * P])
        res = sb("res", [P, 2, QT, D])
        res_n = sb("res_n", [P, QT, D])
        res_g = sb("res_g", [P, QT, D])
        y = sb("y", [P, 2, QT, D])
        yT = sb("yT", [P, QT * P])
        stats_a, stats_c = sb("stats_a", [P, QT, 7]), sb("stats_c", [P, QT, 7])
        mv_a, mv_c = sb("mv_a", [P, QT, 2]), sb("mv_c", [P, QT, 2])
        ve_a, ve_c = sb("ve_a", [P, QT]), sb("ve_c", [P, QT])
        rstd_a, rstd_c = sb("rstd_a", [P, QT]), sb("rstd_c", [P, QT])
        ps = banks("mix_ps", 8)
        XV, Q, K_, SC, PT, MX, OUT = 0, 1, 2, 3, 5, 6, 7

        x_in = [signal(f"x_in{i}", B, 16) for i in range(2)]
        heads_zero = signal("heads_zero")
        stats_a_done, mv_a_done = signal("stats_a_done", QT), signal("mv_a_done", QT)
        eps_a_done, rstd_a_done = signal("eps_a_done"), signal("rstd_a_done")
        xn_done = signal("xn_done", QT)
        x_turned, xT_ready = signal("x_turned"), signal("xT_ready")
        q_proj, k_proj, v_proj = signal("q_proj"), signal("k_proj"), signal("v_proj")
        q_ready, v_ready = signal("q_ready"), signal("v_ready")
        k_ready_act, k_ready_dve = signal("k_ready_act", 2), signal("k_ready_dve", 2)
        scored, maxed = signal("scored", QT), signal("maxed", QT)
        exped, sums_inv, normed = signal("exped", QT * MH), signal("sums_inv", QT), signal("normed", QT)
        p_turned, pT_ready, mixed = signal("p_turned", QT), signal("pT_ready", QT), signal("mixed", QT)
        mixT_ready, projected, res_done, res_bias = (signal(x) for x in ("mixT_ready", "projected", "res_done", "res_bias"))
        stats_c_done, mv_c_done = signal("stats_c_done", QT), signal("mv_c_done", QT)
        eps_c_done, rstd_c_done = signal("eps_c_done"), signal("rstd_c_done")
        res_n_done, res_g_done, y_ready = signal("res_n_done", QT), signal("res_g_done"), signal("y_ready")
        y_kept = [signal(f"y_kept{i}", 1, 16) for i in range(2)]
        y_turned, yT_ready, logits_ps, logits_done = (signal(x) for x in ("y_turned", "yT_ready", "logits_ps", "logits_done"))
        DEPTH = 4
        block = ctx.enter_context(nc.Block())

        @block.sync
        def _(sp):
            def load(u):
                if u.past(2):
                    sp.wait_ge(xn_done.sem, xn_done.done(u - 2))
                for b in range(B):
                    src = k.x_flat[b, bass.ds(u.n * (QT * POS), QT * POS), :]
                    sp.dma_start(x_tile[b * POS:(b + 1) * POS, u.par, :, :],
                                 src.rearrange("(j s) d -> s j d", j=QT)).then_inc(x_in[u.par].sem, 16)

            def keep(u):
                sp.wait_ge(y_ready.sem, y_ready.done(u))
                sp.dma_start(k.y[:, bass.ds(u.n * QT, QT), :], y[:, u.par, :, :]).then_inc(y_kept[u.par].sem, 16)

            def step(t):
                if active(t, 0, UNITS):
                    load(t)
                if active(t, 3, UNITS):
                    keep(t - 3)

            in_steps(sp, UNITS, DEPTH, step)
            for i in range(2):
                sp.wait_ge(y_kept[i].sem, 16 * UNITS // 2)

        @block.gpsimd
        def _(pool):
            for half in range(2):
                pool.memset(k_heads[:, half, :, :, :], 0.0).then_inc(heads_zero.sem, 1)

            def step(t):
                if active(t, 2, UNITS):
                    u = t - 2
                    pool.wait_ge(res_done.sem, res_done.done(u))
                    pool.tensor_tensor(res[:, u.par, :, :], res[:, u.par, :, :], wide(k.row[:, R_MO, :]), ALU.add)\
                        .then_inc(res_bias.sem, 1)
                if active(t, 0, UNITS):
                    ln_rstd(pool, k, mv_a, ve_a, rstd_a, mv_a_done, eps_a_done, rstd_a_done, t)
                if active(t, 2, UNITS):
                    ln_rstd(pool, k, mv_c, ve_c, rstd_c, mv_c_done, eps_c_done, rstd_c_done, u)
                    pool.wait_ge(res_n_done.sem, res_n_done.done(u))
                    pool.tensor_tensor(res_g[:, :, :], res_n[:, :, :], wide(k.row[:, R_G1, :]), ALU.mult)\
                        .then_inc(res_g_done.sem, 1)
                    pool.wait_ge(res_g_done.sem, res_g_done.done(u))
                    if u.past(2):
                        pool.wait_ge(y_turned.sem, y_turned.done(u - 2))
                        pool.wait_ge(y_kept[u.par].sem, (u - 2).pair * 16 + 16)
                    pool.tensor_tensor(y[:, u.par, :, :], res_g[:, :, :], wide(k.row[:, R_BE1, :]), ALU.add)\
                        .then_inc(y_ready.sem, 1)
                if active(t, 1, UNITS):
                    u = t - 1
                    for j in range(QT):
                        pool.wait_ge(sums_inv.sem, sums_inv.after(u, j))
                        p = probs[:, j % 2, :, :]
                        pool.tensor_tensor(p, p, rsums[:, j % 2, :].unsqueeze(2).broadcast_to([P, MH, P]), ALU.mult)\
                            .then_inc(normed.sem, 1)

            in_steps(pool, UNITS, DEPTH, step)

        @block.scalar
        def _(act):
            def step(t):
                if active(t, 3, UNITS):
                    u = t - 3
                    act.wait_ge(y_turned.sem, y_turned.done(u))
                    if u.past(1):
                        act.wait_ge(logits_ps.sem, logits_ps.done(u - 1))
                    act.copy(yT[:, :], ps[:, PT, :]).then_inc(yT_ready.sem, 1)
                if active(t, 0, UNITS):
                    act.wait_ge(x_turned.sem, x_turned.done(t))
                    if t.past(1):
                        act.wait_ge(v_proj.sem, v_proj.done(t - 1))
                    act.copy(xnT[:, :], ps[:, XV, :]).then_inc(xT_ready.sem, 1)
                    act.wait_ge(k_proj.sem, k_proj.done(t))
                    act.wait_ge(heads_zero.sem, 2)
                    for h in range(2):
                        rows = slice(MD * h, MD * (h + 1))
                        act.activation(k_heads[rows, t.par, :, h, :],
                                       ps[rows, K_, :].rearrange("p (j t) -> p j t", j=QT), ACT.Identity,
                                       bias=k.col[rows, C_MK:C_MK + 1]).then_inc(k_ready_act.sem, 1)
                if active(t, 1, UNITS):
                    u = t - 1
                    for j in range(QT + 1):
                        if j < QT:
                            act.wait_ge(maxed.sem, maxed.after(u, j))
                            if u.past(1) or j >= 2:
                                act.wait_ge(p_turned.sem, p_turned.after(u, j - 2))
                            for h in range(MH):
                                act.activation(probs[:, j % 2, h, :], ps[:, SC + j % 2, h * P:(h + 1) * P], ACT.Exp,
                                               bias=neg_max[:, j % 2, h:h + 1], accum_out=sums[:, j % 2, h:h + 1])\
                                   .then_inc(exped.sem, 1)
                        if j >= 1:
                            act.wait_ge(p_turned.sem, p_turned.after(u, j - 1))
                            if u.past(1) or j >= 3:
                                act.wait_ge(mixed.sem, mixed.after(u, j - 3))
                            act.copy(probsT[:, (j - 1) % 2, :, :], ps[:, PT, :]).then_inc(pT_ready.sem, 1)
                    act.wait_ge(mixed.sem, mixed.done(u))
                    if u.past(1):
                        act.wait_ge(projected.sem, projected.done(u - 1))
                    act.copy(mixedT[:, :], ps[:, MX, :]).then_inc(mixT_ready.sem, 1)

            in_steps(act, UNITS, DEPTH, step)

        @block.tensor
        def _(pe):
            def turn_y(u):
                pe.wait_ge(y_ready.sem, y_ready.done(u))
                after = u + 1 if active(u, -1, UNITS) else u
                pe.wait_ge(pT_ready.sem, pT_ready.done(after))
                if u.past(1):
                    pe.wait_ge(logits_done.sem, logits_done.done(u - 1))
                for j in range(QT):
                    mm = pe.transpose(ps[:, PT, j * P:(j + 1) * P], y[:, u.par, j, :], k.ident[:, :])
                mm.then_inc(y_turned.sem, 1)

            def logits(u):
                pe.wait_ge(yT_ready.sem, yT_ready.done(u))
                for j in range(QT):
                    mm = pe.matmul(ps[:, PT, j * E:(j + 1) * E], yT[:, j * P:(j + 1) * P], k.gateT[:, 0, :],
                                   start=True, stop=True)
                mm.then_inc(logits_ps.sem, 1)

            def project_out(u):
                pe.wait_ge(mixT_ready.sem, mixT_ready.done(u))
                if u.past(1):
                    pe.wait_ge(res_done.sem, res_done.done(u - 1))
                for j in range(QT):
                    mm = pe.matmul(ps[:, OUT, j * P:(j + 1) * P], mixedT[:, j * P:(j + 1) * P], k.wT[:, W_MO, :],
                                   start=True, stop=True)
                mm.then_inc(projected.sem, 1)

            def turn_x(u):
                pe.wait_ge(xn_done.sem, xn_done.done(u))
                if u.past(1):
                    pe.wait_ge(v_ready.sem, v_ready.done(u - 1))
                for j in range(QT):
                    mm = pe.transpose(ps[:, XV, j * P:(j + 1) * P], xn[:, u.par, j, :], k.ident[:, :])
                mm.then_inc(x_turned.sem, 1)

            def project_qkv(u):
                pe.wait_ge(xT_ready.sem, xT_ready.done(u))
                if u.past(1):
                    pe.wait_ge(q_ready.sem, q_ready.done(u - 1))
                    pe.wait_ge(k_ready_act.sem, k_ready_act.done(u - 1))
                    pe.wait_ge(k_ready_dve.sem, k_ready_dve.done(u - 1))
                pe.matmul(ps[:, K_, :], k.wT[:, W_MK, :], xnT[:, :], start=True, stop=True).then_inc(k_proj.sem, 1)
                pe.matmul(ps[:, Q, :], k.wT[:, W_MQ, :], xnT[:, :], start=True, stop=True).then_inc(q_proj.sem, 1)
                for j in range(QT):
                    mm = pe.matmul(ps[:, XV, j * P:(j + 1) * P], xnT[:, j * P:(j + 1) * P], k.wT[:, W_MV, :],
                                   start=True, stop=True)
                mm.then_inc(v_proj.sem, 1)

            def attend(u):
                pe.wait_ge(q_ready.sem, q_ready.done(u))
                pe.wait_ge(k_ready_act.sem, k_ready_act.done(u))
                pe.wait_ge(k_ready_dve.sem, k_ready_dve.done(u))
                pe.wait_ge(v_ready.sem, v_ready.done(u))
                for j in range(QT + 2):
                    if j < QT:
                        if u.past(1) or j >= 2:
                            pe.wait_ge(exped.sem, exped.after(u, MH * (j - 1) - 1))
                        pe.matmul(ps[:, SC + j % 2, :], qT[:, u.par, j * P:(j + 1) * P], k_heads[:, u.par, j, :, :],
                                  start=True, stop=False)
                        pe.matmul(ps[:, SC + j % 2, :], k.identb[:, :],
                                  k.batch_mask[:, :].unsqueeze(1).broadcast_to([P, MH, P]), start=False, stop=True)\
                          .then_inc(scored.sem, 1)
                    if 1 <= j <= QT:
                        i = j - 1
                        pe.wait_ge(normed.sem, normed.after(u, i))
                        if i >= 1:
                            pe.wait_ge(pT_ready.sem, pT_ready.after(u, i - 1))
                        elif u.past(1):
                            pe.wait_ge(pT_ready.sem, pT_ready.done(u - 1))
                            if u.past(2):
                                pe.wait_ge(logits_done.sem, logits_done.done(u - 2))
                        for h in range(MH):
                            mm = pe.transpose(ps[:, PT, h * P:(h + 1) * P], probs[:, i % 2, h, :], k.ident[:, :])
                        mm.then_inc(p_turned.sem, 1)
                    if j >= 2:
                        i = j - 2
                        pe.wait_ge(pT_ready.sem, pT_ready.after(u, i))
                        if i == 0 and (u.past(1)):
                            pe.wait_ge(mixT_ready.sem, mixT_ready.done(u - 1))
                        for h in range(MH):
                            mm = pe.matmul(ps[MD * h:MD * (h + 1), MX, i * P:(i + 1) * P],
                                           v[:, u.par, i, MD * h:MD * (h + 1)], probsT[:, i % 2, h, :],
                                           start=True, stop=True)
                        mm.then_inc(mixed.sem, 1)

            def step(t):
                if active(t, 3, UNITS):
                    turn_y(t - 3)
                if active(t, 2, UNITS):
                    project_out(t - 2)
                if active(t, 0, UNITS):
                    turn_x(t)
                if active(t, 3, UNITS):
                    logits(t - 3)
                if active(t, 0, UNITS):
                    project_qkv(t)
                if active(t, 1, UNITS):
                    attend(t - 1)

            in_steps(pe, UNITS, DEPTH, step)

        @block.vector
        def _(dve):
            def evacuate(u):
                dve.wait_ge(k_proj.sem, k_proj.done(u))
                for h in range(2, MH):
                    rows = slice(MD * h, MD * (h + 1))
                    dve.wait_ge(heads_zero.sem, 2)
                    dve.tensor_scalar(k_heads[rows, u.par, :, h, :], ps[rows, K_, :].rearrange("p (j t) -> p j t", j=QT),
                                      k.col[rows, C_MK:C_MK + 1], None, ALU.add).then_inc(k_ready_dve.sem, 1)
                dve.wait_ge(q_proj.sem, q_proj.done(u))
                dve.tensor_scalar(qT[:, u.par, :], ps[:, Q, :], k.col[:, C_MQ:C_MQ + 1], float(MD) ** -0.5,
                                  ALU.add, ALU.mult).then_inc(q_ready.sem, 1)
                dve.wait_ge(v_proj.sem, v_proj.done(u))
                if u.past(2):
                    dve.wait_ge(mixed.sem, mixed.done(u - 2))
                dve.tensor_tensor(v[:, u.par, :, :], ps[:, XV, :].rearrange("p (j d) -> p j d", j=QT),
                                  wide(k.row[:, R_MV, :]), ALU.add).then_inc(v_ready.sem, 1)

            def softmax(u):
                for j in range(QT + 1):
                    if j < QT:
                        dve.wait_ge(scored.sem, scored.after(u, j))
                        dve.tensor_reduce(neg_max[:, j % 2, :], ps[:, SC + j % 2, :].rearrange("p (h t) -> p h t", h=MH),
                                          X_AXIS, ALU.max, negate=True).then_inc(maxed.sem, 1)
                    if j >= 1:
                        i = j - 1
                        dve.wait_ge(exped.sem, exped.after(u, MH * j - 1))
                        dve.reciprocal(rsums[:, i % 2, :], sums[:, i % 2, :]).then_inc(sums_inv.sem, 1)

            def step(t):
                if active(t, 2, UNITS):
                    u = t - 2
                    dve.wait_ge(projected.sem, projected.done(u))
                    dve.tensor_tensor(res[:, u.par, :, :], ps[:, OUT, :].rearrange("p (j d) -> p j d", j=QT),
                                      xn[:, u.par, :, :], ALU.add).then_inc(res_done.sem, 1)
                if active(t, 0, UNITS):
                    dve.wait_ge(x_in[t.par].sem, (t.pair + 1) * (16 * B))
                    ln_stats(dve, x_tile[:, t.par, :, :], stats_a, mv_a, stats_a_done, mv_a_done, t)
                if active(t, 2, UNITS):
                    dve.wait_ge(res_bias.sem, res_bias.done(u))
                    ln_stats(dve, res[:, u.par, :, :], stats_c, mv_c, stats_c_done, mv_c_done, u)
                if active(t, 0, UNITS):
                    ln_apply(dve, xn[:, t.par, :, :], x_tile[:, t.par, :, :], mv_a, rstd_a, rstd_a_done, xn_done, t)
                if active(t, 2, UNITS):
                    if u.past(1):
                        dve.wait_ge(res_g_done.sem, res_g_done.done(u - 1))
                    ln_apply(dve, res_n, res[:, u.par, :, :], mv_c, rstd_c, rstd_c_done, res_n_done, u)
                if active(t, 3, UNITS):
                    dve.wait_ge(logits_ps.sem, logits_ps.done(t - 3))
                    dve.tensor_copy(k.logits[:, bass.ds((t - 3).n * QT, QT), :],
                                    ps[:, PT, 0:QT * E].rearrange("p (j e) -> p j e", j=QT))\
                       .then_inc(logits_done.sem, 1)
                if active(t, 0, UNITS):
                    evacuate(t)
                if active(t, 1, UNITS):
                    softmax(t - 1)

            in_steps(dve, UNITS, DEPTH, step)




def prepare(nc, k, layer):
    COMP = 2 - layer
    x_in_dram = (k.x_flat, k.z)[layer]
    stacks = ((k.q_stack, k.k_stack), (k.q_stack1, k.k_stack1))[layer]
    w_q, w_k, w_v = ((W_QA, W_KA, W_V0), (W_Q1, W_K1, W_V1))[layer]
    with ExitStack() as ctx:
        sb, banks, signal = phase_resources(nc, ctx, f"prepare{layer}")
        x_tile = sb("x_tile", [P, 2, QT, D])
        xn = sb("xn", [P, 2, QT, D])
        xnT = sb("xnT", [P, QT * P])
        stats, mv = sb("stats", [P, QT, 7]), sb("mv", [P, QT, 2])
        var_eps, rstd = sb("var_eps", [P, QT]), sb("rstd", [P, QT])
        vals = sb("vals", [P, 2, COMP, S])
        rest = sb("rest", [P, 2, COMP, S])
        parts = sb("parts", [P, 2, 2, 3, COMP, S], BF16)
        if layer == 0:
            turn = sb("turn", [P, 2, S])
            turn_abs = sb("turn_abs", [P, 2, S])
            sine, cosine = sb("sine", [P, 2, S]), sb("cosine", [P, 2, S])
            mag, logs = sb("mag", [P, 2, S]), sb("logs", [P, 2, S])
            amp, square = sb("amp", [P, 2, S]), sb("square", [P, 2, S])
            inv, amp_n = sb("inv", [P, 2, S]), sb("amp_n", [P, 2, S])
        ps = banks("prep_ps", 8)
        XV, AMP, PHI, MS, LOG = 0, 1, 3, 5, 7

        x_in = [signal(f"x_in{i}", by=16) for i in range(2)]
        stats_done, mv_done, eps_done, rstd_done = signal("stats_done", QT), signal("mv_done", QT), signal("eps_done"), signal("rstd_done")
        xn_done = signal("xn_done", QT)
        x_turned, xT_ready = signal("x_turned"), signal("xT_ready")
        projected, v_proj, v_ready = signal("projected"), signal("v_proj"), signal("v_ready")
        phases_ps, tanh_done, sine_done, turn_abs_done, cosine_done = (signal(x) for x in ("phases_ps", "tanh_done", "sine_done", "turn_abs_done", "cosine_done"))
        mag_done, exp_done, log_done, amp_done, square_done = (signal(x) for x in ("mag_done", "exp_done", "log_done", "amp_done", "square_done"))
        mean_ps, mean_log, inv_done, amp_n_done = signal("mean_ps"), signal("mean_log"), signal("inv_done"), signal("amp_n_done", 2)
        vals_done, high_done, rest_done, mid_done, low_done = signal("vals_done", 2 if layer == 0 else 1), signal("high_done"), signal("rest_done"), signal("mid_done"), signal("low_done")
        stacked = [signal(f"stacked{i}", 2 * SLOTS, 16) for i in range(2)]
        logits_ps, logits_done = signal("logits_ps"), signal("logits_done")
        xn_kept = [signal(f"xn_kept{i}", by=16) for i in range(2)]
        q_vals_done, summed = signal("q_vals_done"), signal("summed")
        sum_kept = [signal(f"sum_kept{i}", by=16) for i in range(2)]
        DEPTH = 2
        block = ctx.enter_context(nc.Block())

        @block.sync
        def _(sp):
            def load(u):
                if u.past(2):
                    sp.wait_ge(xn_done.sem, xn_done.done(u - 2))
                    if layer == 1:
                        sp.wait_ge(sum_kept[u.par].sem, u.pair * 16)
                sp.dma_start(x_tile[:, u.par, :, :], x_in_dram[bass.ds(u.n, 1), :, :].rearrange("b (j p) d -> p (b j) d", p=P))\
                  .then_inc(x_in[u.par].sem, 16)

            def store(u):
                for side, which in enumerate((Q_PARTS, K_PARTS)):
                    for slot in sorted(range(SLOTS), key=lambda s: which[s]):
                        done = (high_done, mid_done, low_done)[which[slot]]
                        sp.wait_ge(done.sem, done.done(u))
                        rows = stacks[side][bass.ds(u.n, 1), :, slot * COMP * HD:(slot + 1) * COMP * HD, :]
                        sp.dma_start(rows.rearrange("b h (d c) t -> (b h) d (c t)", d=HD), parts[:, u.par, side, which[slot], :, :].rearrange("p c t -> p (c t)"))\
                          .then_inc(stacked[u.par].sem, 16)

            def step(t):
                if active(t, 0, B):
                    load(t)
                    if layer == 1:
                        sp.wait_ge(xn_done.sem, xn_done.done(t))
                        sp.dma_start(k.x_sum[:, bass.ds(t.n * QT, QT), :], x_tile[:, t.par, :, :])\
                          .then_inc(sum_kept[t.par].sem, 16)
                        sp.dma_start(k.y[:, bass.ds(t.n * QT, QT), :], xn[:, t.par, :, :]).then_inc(xn_kept[t.par].sem, 16)
                if active(t, 1, B):
                    store(t - 1)

            in_steps(sp, B, DEPTH, step)
            for i in range(2):
                sp.wait_ge(stacked[i].sem, stacked[i].done(B // 2 - 1))
                if layer == 1:
                    sp.wait_ge(xn_kept[i].sem, 16 * B // 2)
                    sp.wait_ge(sum_kept[i].sem, 16 * B // 2)

        @block.gpsimd
        def _(pool):
            def step(t):
                if active(t, 0, B):
                    ln_rstd(pool, k, mv, var_eps, rstd, mv_done, eps_done, rstd_done, t)

            in_steps(pool, B, DEPTH, step)

        @block.scalar
        def _(act):
            def amplitudes(u):
                act.wait_ge(phases_ps.sem, phases_ps.done(u))
                act.activation(turn[:, :, :], ps[:, PHI:PHI + 2, :], ACT.Tanh).then_inc(tanh_done.sem, 1)
                act.wait_ge(tanh_done.sem, tanh_done.done(u))
                act.activation(sine[:, :, :], turn[:, :, :], ACT.Sin, scale=PI).then_inc(sine_done.sem, 1)
                act.wait_ge(turn_abs_done.sem, turn_abs_done.done(u))
                act.activation(cosine[:, :, :], turn_abs[:, :, :], ACT.Sin, bias=k.col[:, C_PIH:C_PIH + 1], scale=-PI)\
                   .then_inc(cosine_done.sem, 1)
                act.wait_ge(projected.sem, projected.done(u))
                act.activation(mag[:, :, :], ps[:, AMP:AMP + 2, :], ACT.Abs).then_inc(mag_done.sem, 1)
                act.wait_ge(mag_done.sem, mag_done.done(u))
                act.activation(mag[:, :, :], mag[:, :, :], ACT.Exp, scale=-1.0).then_inc(exp_done.sem, 1)
                act.wait_ge(exp_done.sem, exp_done.done(u))
                act.activation(logs[:, :, :], mag[:, :, :], ACT.Ln, bias=1.0).then_inc(log_done.sem, 1)
                act.wait_ge(amp_done.sem, amp_done.done(u))
                act.activation(square[:, :, :], amp[:, :, :], ACT.Square).then_inc(square_done.sem, 1)

            def inverse(u):
                act.wait_ge(mean_ps.sem, mean_ps.done(u))
                act.activation(inv[:, :, :], ps[:, MS:MS + 2, :], ACT.Ln, bias=k.col[:, C_EPS:C_EPS + 1])\
                   .then_inc(mean_log.sem, 1)
                act.wait_ge(mean_log.sem, mean_log.done(u))
                act.activation(inv[:, :, :], inv[:, :, :], ACT.Exp, scale=-0.5).then_inc(inv_done.sem, 1)

            def step(t):
                if active(t, 0, B):
                    act.wait_ge(x_turned.sem, x_turned.done(t))
                    if t.past(1):
                        act.wait_ge(v_proj.sem, v_proj.done(t - 1))
                        if layer == 1:
                            act.wait_ge(logits_ps.sem, logits_ps.done(t - 1))
                    act.copy(xnT[:, :], ps[:, XV, :]).then_inc(xT_ready.sem, 1)
                if active(t, 1, B):
                    u = t - 1
                    if layer == 0:
                        amplitudes(u)
                        inverse(u)
                    else:
                        act.wait_ge(projected.sem, projected.done(u))
                        act.activation(vals[:, 1, 0, :], ps[:, AMP + 1, :], ACT.Identity, bias=k.col[:, C_K1:C_K1 + 1])\
                           .then_inc(vals_done.sem, 1)
                        act.wait_ge(q_vals_done.sem, q_vals_done.done(u))
                    act.wait_ge(vals_done.sem, vals_done.done(u))
                    if u.past(2):
                        act.wait_ge(stacked[u.par].sem, (u - 2).pair * (2 * SLOTS * 16) + 2 * SLOTS * 16)
                    act.copy(parts[:, u.par, :, 0, :, :], vals[:, :, :, :]).then_inc(high_done.sem, 1)
                    act.wait_ge(rest_done.sem, rest_done.done(u))
                    act.copy(parts[:, u.par, :, 1, :, :], rest[:, :, :, :]).then_inc(mid_done.sem, 1)

            in_steps(act, B, DEPTH, step)

        @block.tensor
        def _(pe):
            def step(t):
                if active(t, 0, B):
                    pe.wait_ge(xn_done.sem, xn_done.done(t))
                    if t.past(1):
                        pe.wait_ge(v_ready.sem, v_ready.done(t - 1))
                    for j in range(QT):
                        mm = pe.transpose(ps[:, XV, j * P:(j + 1) * P], xn[:, t.par, j, :], k.ident[:, :])
                    mm.then_inc(x_turned.sem, 1)
                    pe.wait_ge(xT_ready.sem, xT_ready.done(t))
                    for j in range(QT):
                        mm = pe.matmul(ps[:, XV, j * P:(j + 1) * P], xnT[:, j * P:(j + 1) * P], k.wT[:, w_v, :],
                                       start=True, stop=True)
                    mm.then_inc(v_proj.sem, 1)
                    if layer == 0:
                        if t.past(1):
                            pe.wait_ge(tanh_done.sem, tanh_done.done(t - 1))
                        pe.matmul(ps[:, PHI, :], k.wT[:, W_QP, :], xnT[:, :], start=True, stop=True)
                        pe.matmul(ps[:, PHI + 1, :], k.wT[:, W_KP, :], xnT[:, :], start=True, stop=True)\
                          .then_inc(phases_ps.sem, 1)
                    else:
                        if t.past(1):
                            pe.wait_ge(logits_done.sem, logits_done.done(t - 1))
                        for j in range(QT):
                            mm = pe.matmul(ps[:, LOG, j * E:(j + 1) * E], xnT[:, j * P:(j + 1) * P], k.gateT[:, 1, :],
                                           start=True, stop=True)
                        mm.then_inc(logits_ps.sem, 1)
                if active(t, 1, B) and layer == 0:
                    u = t - 1
                    pe.wait_ge(square_done.sem, square_done.done(u))
                    for side in range(2):
                        mm = pe.matmul(ps[:, MS + side, :], k.head_mean[:, :], square[:, side, :], start=True, stop=True)
                    mm.then_inc(mean_ps.sem, 1)
                if active(t, 0, B):
                    if t.past(1):
                        if layer == 0:
                            pe.wait_ge(amp_done.sem, amp_done.done(t - 1))
                        else:
                            pe.wait_ge(vals_done.sem, vals_done.done(t - 1))
                            pe.wait_ge(q_vals_done.sem, q_vals_done.done(t - 1))
                    pe.matmul(ps[:, AMP, :], k.wT[:, w_q, :], xnT[:, :], start=True, stop=True)
                    pe.matmul(ps[:, AMP + 1, :], k.wT[:, w_k, :], xnT[:, :], start=True, stop=True)\
                      .then_inc(projected.sem, 1)

            in_steps(pe, B, DEPTH, step)

        @block.vector
        def _(dve):
            def values(u):
                if layer == 1:
                    dve.wait_ge(projected.sem, projected.done(u))
                    dve.tensor_scalar(vals[:, 0, 0, :], ps[:, AMP, :], k.col[:, C_Q1:C_Q1 + 1], float(HD) ** -0.5,
                                      ALU.add, ALU.mult).then_inc(q_vals_done.sem, 1)
                    return
                dve.wait_ge(tanh_done.sem, tanh_done.done(u))
                dve.scalar_tensor_tensor(out=turn_abs[:, :, :], in0=turn[:, :, :], scalar=-1.0, in1=turn[:, :, :],
                                         op0=ALU.mult, op1=ALU.max).then_inc(turn_abs_done.sem, 1)
                dve.wait_ge(log_done.sem, log_done.done(u))
                dve.scalar_tensor_tensor(out=amp[:, :, :], in0=ps[:, AMP:AMP + 2, :], scalar=0.0, in1=logs[:, :, :],
                                         op0=ALU.max, op1=ALU.add).then_inc(amp_done.sem, 1)
                dve.wait_ge(inv_done.sem, inv_done.done(u))
                dve.scalar_tensor_tensor(out=amp_n[:, 0, :], in0=amp[:, 0, :], scalar=k.hscale[:, :], in1=inv[:, 0, :],
                                         op0=ALU.mult, op1=ALU.mult).then_inc(amp_n_done.sem, 1)
                dve.tensor_tensor(amp_n[:, 1, :], amp[:, 1, :], inv[:, 1, :], ALU.mult).then_inc(amp_n_done.sem, 1)
                dve.wait_ge(amp_n_done.sem, amp_n_done.done(u))
                dve.wait_ge(cosine_done.sem, cosine_done.done(u))
                dve.tensor_tensor(vals[:, :, 0, :], amp_n[:, :, :], cosine[:, :, :], ALU.mult).then_inc(vals_done.sem, 1)
                dve.tensor_tensor(vals[:, :, 1, :], amp_n[:, :, :], sine[:, :, :], ALU.mult).then_inc(vals_done.sem, 1)

            def split(u):
                dve.wait_ge(high_done.sem, high_done.done(u))
                flat = "p s c t -> p s (c t)"
                dve.tensor_tensor(rest[:, :, :, :].rearrange(flat), vals[:, :, :, :].rearrange(flat),
                                  parts[:, u.par, :, 0, :, :].rearrange(flat), ALU.subtract).then_inc(rest_done.sem, 1)
                dve.wait_ge(mid_done.sem, mid_done.done(u))
                dve.tensor_tensor(parts[:, u.par, :, 2, :, :].rearrange(flat), rest[:, :, :, :].rearrange(flat),
                                  parts[:, u.par, :, 1, :, :].rearrange(flat), ALU.subtract).then_inc(low_done.sem, 1)

            def step(t):
                if active(t, 0, B):
                    dve.wait_ge(x_in[t.par].sem, (t.pair + 1) * 16)
                    if layer == 1:
                        here = bass.ds(t.n * QT, QT)
                        dve.tensor_tensor(x_tile[:, t.par, :, :], x_tile[:, t.par, :, :], k.x_sum[:, here, :], ALU.add)\
                           .then_inc(summed.sem, 1)
                        dve.wait_ge(summed.sem, summed.done(t))
                    ln_stats(dve, x_tile[:, t.par, :, :], stats, mv, stats_done, mv_done, t)
                    if layer == 1 and t.past(2):
                        dve.wait_ge(xn_kept[t.par].sem, t.pair * 16)
                    ln_apply(dve, xn[:, t.par, :, :], x_tile[:, t.par, :, :], mv, rstd, rstd_done, xn_done, t)
                if active(t, 1, B):
                    values(t - 1)
                if active(t, 0, B):
                    dve.wait_ge(v_proj.sem, v_proj.done(t))
                    v_out = k.v_all[:, bass.ds(t.n, 1), :, :].rearrange("p b j d -> p (b j) d")
                    v_ps = ps[:, XV, :].rearrange("p (j d) -> p j d", j=QT)
                    if layer == 0:
                        dve.tensor_copy(v_out, v_ps).then_inc(v_ready.sem, 1)
                    else:
                        dve.tensor_tensor(v_out, v_ps, wide(k.row[:, R_V1, :]), ALU.add).then_inc(v_ready.sem, 1)
                        dve.wait_ge(logits_ps.sem, logits_ps.done(t))
                        dve.tensor_copy(k.logits[:, bass.ds(t.n * QT, QT), :],
                                        ps[:, LOG, 0:QT * E].rearrange("p (j e) -> p j e", j=QT))\
                           .then_inc(logits_done.sem, 1)
                if active(t, 1, B):
                    split(t - 1)

            in_steps(dve, B, DEPTH, step)


def prepare0(nc, k):
    prepare(nc, k, 0)


def prepare1(nc, k):
    prepare(nc, k, 1)




def route(nc, k, layer):
    COPIES = layer + 1
    W = COPIES * NT
    TL = TILES[layer]
    MOST = T // ROWS
    dst = (k.sorted0, k.sorted1)[layer]
    with ExitStack() as ctx:
        sb, banks, signal = phase_resources(nc, ctx, f"route{layer}")
        best = sb("best", [P, NT])
        ties = sb("ties", [P, NT, E])
        first = sb("first", [P, NT])
        left = sb("left", [P, NT, E])
        second = sb("second", [P, NT])
        onehot = sb("onehot", [P, W, E])
        weight = sb("weight", [P, E])
        counts = sb("counts", [P, E, W])
        keep = sb("keep", [P, E, W])
        prefix = sb("prefix", [P, E, W])
        total = sb("total", [P, E])
        filled = sb("filled", [P, E, MOST])
        tiles = sb("tiles", [P, E])
        tiles_to = sb("tiles_to", [P, E])
        start = sb("start", [P, E])
        offset = sb("offset", [P, E, W])
        row_of = sb("row_of", [P, W, E])
        row_f = sb("row_f", [P, W])
        passed = sb("passed", [P, TL, E])
        expert_f = sb("expert_f", [P, TL])
        probs = sb("probs", [P, NT, E])
        denom = sb("denom", [P, NT])
        share = sb("share", [P, COPIES, NT])
        scaled = sb("scaled", [P, 2, NT, D]) if layer == 1 else None
        ps = banks("route_ps", 2)
        exp_ready, dve_step = signal("exp_ready"), signal("dve_step")
        onehot_done, ranked, rows_ready = signal("onehot_done"), signal("ranked"), signal("rows_ready")
        scaled_done = signal("scaled_done")
        scattered = k.scattered[layer]
        minus_best, probs_exp = signal("minus_best"), signal("probs_exp")
        block = ctx.enter_context(nc.Block())

        def per_token(column):
            return column.unsqueeze(2).broadcast_to([P, NT, E])

        @block.tensor
        def _(pe):
            pe.wait_ge(onehot_done.sem, 1)
            flat = onehot[:, :, :].rearrange("p w e -> p (w e)")
            pe.matmul(ps[:, 0, 0:W * E], k.before[:, :], flat, start=True, stop=True)
            pe.matmul(ps[:, 1, 0:W * E], k.ones[:, :], flat, start=True, stop=True).then_inc(ranked.sem, 1)

        @block.scalar
        def _(act):
            if layer == 1:
                act.wait_ge(minus_best.sem, 1)
                act.activation(probs[:, :, :], probs[:, :, :], ACT.Exp).then_inc(probs_exp.sem, 1)

        @block.vector
        def _(dve):
            steps = [0]

            def then(instruction):
                steps[0] += 1
                instruction.then_inc(dve_step.sem, 1)
                dve.wait_ge(dve_step.sem, steps[0])

            def choose(logits, best_, hot):
                then(dve.tensor_reduce(best_, logits, X_AXIS, ALU.max))
                then(dve.tensor_tensor(ties[:, :, :], logits, per_token(best_), ALU.is_equal))
                then(dve.tensor_tensor(ties[:, :, :], ties[:, :, :], weight[:, :].unsqueeze(1).broadcast_to([P, NT, E]),
                                       ALU.mult))
                then(dve.tensor_reduce(first[:, :], ties[:, :, :], X_AXIS, ALU.max))
                return dve.tensor_tensor(hot, ties[:, :, :], per_token(first[:, :]), ALU.is_equal)

            then(dve.tensor_scalar(weight[:, :], k.counted[:, 0:E], -1.0, float(E), ALU.mult, ALU.add))
            if layer == 0:
                choose(k.logits[:, :, :], best[:, :], onehot[:, 0:NT, :]).then_inc(onehot_done.sem, 1)
                dve.wait_ge(onehot_done.sem, 1)
            else:
                then(choose(k.logits[:, :, :], best[:, :], onehot[:, 0:NT, :]))
                dve.tensor_tensor(probs[:, :, :], k.logits[:, :, :], per_token(best[:, :]), ALU.subtract)\
                   .then_inc(minus_best.sem, 1)
                then(dve.scalar_tensor_tensor(out=left[:, :, :], in0=onehot[:, 0:NT, :], scalar=NEG, in1=k.logits[:, :, :],
                                              op0=ALU.mult, op1=ALU.add))
                choose(left[:, :, :], second[:, :], onehot[:, NT:W, :]).then_inc(onehot_done.sem, 1)
                dve.wait_ge(probs_exp.sem, 1)
                dve.wait_ge(onehot_done.sem, 1)
                then(dve.tensor_reduce(denom[:, :], probs[:, :, :], X_AXIS, ALU.add))
                then(dve.reciprocal(denom[:, :], denom[:, :]))
                for c in range(2):
                    then(dve.tensor_tensor(ties[:, :, :], probs[:, :, :], onehot[:, c * NT:(c + 1) * NT, :], ALU.mult))
                    then(dve.tensor_reduce(share[:, c, :], ties[:, :, :], X_AXIS, ALU.add))
                    then(dve.tensor_tensor(share[:, c, :], share[:, c, :], denom[:, :], ALU.mult))
            then(dve.memset(keep[:, :, :], 1.0))
            then(dve.memset(keep[:, :, 0:1], 0.0))
            dve.wait_ge(ranked.sem, 1)
            then(dve.tensor_copy(counts[:, :, :], ps[:, 1, 0:W * E].rearrange("p (w e) -> p e w", e=E)))
            then(dve.tensor_tensor_scan(prefix[:, :, :].rearrange("p e w -> p (e w)"),
                                        keep[:, :, :].rearrange("p e w -> p (e w)"),
                                        counts[:, :, :].rearrange("p e w -> p (e w)"), 0.0, ALU.mult, ALU.add))
            then(dve.tensor_copy(total[:, :], prefix[:, :, W - 1]))
            then(dve.scalar_tensor_tensor(out=filled[:, :, :], in0=k.counted[:, 0:MOST].unsqueeze(1).broadcast_to([P, E, MOST]),
                                          scalar=float(ROWS), in1=total[:, :].unsqueeze(2).broadcast_to([P, E, MOST]),
                                          op0=ALU.mult, op1=ALU.is_lt))
            then(dve.tensor_reduce(tiles[:, :], filled[:, :, :], X_AXIS, ALU.add))
            then(dve.tensor_tensor_scan(tiles_to[:, :], k.ones[:, 0:E], tiles[:, :], 0.0, ALU.mult, ALU.add))
            then(dve.tensor_tensor(start[:, :], tiles_to[:, :], tiles[:, :], ALU.subtract))
            then(dve.tensor_tensor(offset[:, :, :], prefix[:, :, :], counts[:, :, :], ALU.subtract))
            then(dve.scalar_tensor_tensor(out=offset[:, :, :], in0=start[:, :].unsqueeze(2).broadcast_to([P, E, W]),
                                          scalar=float(ROWS), in1=offset[:, :, :], op0=ALU.mult, op1=ALU.add))
            then(dve.tensor_tensor(row_of[:, :, :], ps[:, 0, 0:W * E].rearrange("p (w e) -> p w e", e=E),
                                   offset[:, :, :].rearrange("p e w -> p w e"), ALU.add))
            then(dve.tensor_tensor(row_of[:, :, :], row_of[:, :, :], onehot[:, :, :], ALU.mult))
            then(dve.tensor_reduce(row_f[:, :], row_of[:, :, :], X_AXIS, ALU.add))
            dve.tensor_copy(k.rank_row[:, 0:W], row_f[:, :]).then_inc(rows_ready.sem, 1)
            if layer == 1:
                for c in range(2):
                    dve.tensor_tensor(scaled[:, c, :, :], k.y[:, :, :], share[:, c, :].unsqueeze(2).broadcast_to([P, NT, D]),
                                      ALU.mult).then_inc(scaled_done.sem, 1)
            then(dve.tensor_tensor(passed[:, :, :], tiles_to[:, :].unsqueeze(1).broadcast_to([P, TL, E]),
                                   k.counted[:, 0:TL].unsqueeze(2).broadcast_to([P, TL, E]), ALU.is_le))
            then(dve.tensor_reduce(expert_f[:, :], passed[:, :, :], X_AXIS, ALU.add))
            then(dve.tensor_scalar(expert_f[:, :], expert_f[:, :], float(E - 1), None, ALU.min))
            then(dve.tensor_copy(k.tile_expert[:, 0:TL], expert_f[:, :]))

        @block.gpsimd
        def _(pool):
            pool.wait_ge(rows_ready.sem, 1)
            for c in range(COPIES):
                if layer == 1:
                    pool.wait_ge(scaled_done.sem, c + 1)
                for t in range(NT):
                    n = c * NT + t
                    src = k.y[:, t, :] if layer == 0 else scaled[:, c, t, :]
                    if n >= 4:
                        pool.wait_ge(scattered[n % 4].sem, n // 4 * 16)
                    pool.indirect_dma_start(dst, bass.IndirectOffsetOnAxis(ap=k.rank_row[:, n:n + 1], axis=0), src, None)\
                        .then_inc(scattered[n % 4].sem, 16)
            for i in range(4):
                pool.wait_ge(scattered[i].sem, W // 4 * 16)


def route0(nc, k):
    route(nc, k, 0)


def route1(nc, k):
    route(nc, k, 1)




def experts(nc, k, layer):
    TL = TILES[layer]
    HC = DF // P if layer == 0 else 3
    size = [P] * HC if layer == 0 else [P, P, HID - 2 * P]
    src, dst = ((k.sorted0, k.done0), (k.sorted1, k.done1))[layer]
    LOADS = 5
    with ExitStack() as ctx:
        sb, banks, signal = phase_resources(nc, ctx, f"experts{layer}")
        rows = sb("rows", [P, 2, 2, D])
        rowsT = sb("rowsT", [P, 2, ROWS])
        w_in = sb("w_in", [P, 2, DF if layer == 0 else 2 * HID])
        w_out = sb("w_out", [P, 2, HC, D])
        b_in = sb("b_in", [P, 2, HC])
        b_out = sb("b_out", [P, 2, D])
        hidden = sb("hidden", [P, 2, HC, ROWS])
        gate = sb("gate", [P, HC, ROWS])
        result = sb("result", [P, 2, 2, D])
        ps = banks("experts_ps", 8)
        TURN, HID_A, HID_B, OUT = 0, 1, 3, 5
        loaded = [signal(f"loaded{i}", LOADS, 16) for i in range(2)]
        turned, rowsT_ready, hidden_ps, out_ps, result_done = (signal(x) for x in ("turned", "rowsT_ready", "hidden_ps", "out_ps", "result_done"))
        hidden_act, hidden_dve = signal("hidden_act", 2), signal("hidden_dve", 2)
        stored = [signal(f"stored{i}", by=16) for i in range(2)]
        DEPTH = 3
        block = ctx.enter_context(nc.Block())

        @block.sync
        def _(sp):
            def load(u):
                if u.past(2):
                    sp.wait_ge(out_ps.sem, out_ps.done(u - 2))
                    if layer == 0:
                        sp.wait_ge(result_done.sem, result_done.done(u - 2))
                e = sp.value_load(k.tile_expert[0:1, bass.ds(u.n, 1)], min_val=0, max_val=E - 1)
                done = loaded[u.par].sem
                sp.dma_start(rows[:, u.par, :, :], src[bass.ds(u.n * ROWS, ROWS), :].rearrange("(a p) d -> p a d", p=P))\
                  .then_inc(done, 16)
                one = bass.ds(e, 1)
                if layer == 0:
                    sp.dma_start(w_in[:, u.par, :], k.arg["L0_ffn_W1"][one, :, :].rearrange("e d f -> (e d) f")).then_inc(done, 16)
                    sp.dma_start(b_in[:, u.par, :], k.arg["L0_ffn_b1"][one, :].rearrange("e (p c) -> (e p) c", p=P))\
                      .then_inc(done, 16)
                    sp.dma_start(w_out[:, u.par, :, :], k.arg["L0_ffn_W2"][one, :, :].rearrange("e (p c) d -> (e p) c d", p=P))\
                      .then_inc(done, 16)
                    sp.dma_start(b_out[:, u.par, :], k.arg["L0_ffn_b2"][one, :].rearrange("e d -> (e d)").rearrange("(o d) -> o d", o=1)
                                 .partition_broadcast(P)).then_inc(done, 16)
                else:
                    sp.dma_start(w_in[:, u.par, 0:HID], k.arg["L1_ffn_w1"][one, :, :].rearrange("e d f -> (e d) f")).then_inc(done, 16)
                    sp.dma_start(w_in[:, u.par, HID:2 * HID], k.arg["L1_ffn_w3"][one, :, :].rearrange("e d f -> (e d) f"))\
                      .then_inc(done, 16)
                    sp.dma_start(w_out[:, u.par, 0:2, :], k.arg["L1_ffn_w2"][one, 0:2 * P, :].rearrange("e (c p) d -> p (e c) d", p=P))\
                      .then_inc(done, 16)
                    sp.dma_start(w_out[0:size[2], u.par, 2, :], k.arg["L1_ffn_w2"][one, 2 * P:HID, :].rearrange("e f d -> (e f) d"))\
                      .then_inc(done, 16)

            def store(u):
                sp.wait_ge(result_done.sem, result_done.done(u))
                sp.dma_start(dst[bass.ds(u.n * ROWS, ROWS), :].rearrange("(a p) d -> p a d", p=P), result[:, u.par, :, :])\
                  .then_inc(stored[u.par].sem, 16)

            def step(t):
                if active(t, 0, TL):
                    load(t)
                if active(t, 3, TL):
                    store(t - 3)

            in_steps(sp, TL, DEPTH + 1, step)
            for i in range(2):
                sp.wait_ge(stored[i].sem, (TL + 1 - i) // 2 * 16)

        @block.scalar
        def _(act):
            def step(t):
                if active(t, 0, TL):
                    act.wait_ge(turned.sem, turned.done(t))
                    if t.past(2):
                        act.wait_ge(hidden_ps.sem, hidden_ps.done(t - 2))
                    act.copy(rowsT[:, t.par, :], ps[:, TURN, 0:ROWS]).then_inc(rowsT_ready.sem, 1)
                if active(t, 1, TL):
                    u = t - 1
                    act.wait_ge(hidden_ps.sem, hidden_ps.done(u))
                    if layer == 0:
                        if u.past(2):
                            act.wait_ge(out_ps.sem, out_ps.done(u - 2))
                        for c in range(2):
                            act.activation(hidden[:, u.par, c, :], ps[:, HID_A, c * ROWS:(c + 1) * ROWS], ACT.Relu,
                                           bias=b_in[:, u.par, c:c + 1]).then_inc(hidden_act.sem, 1)
                    else:
                        if u.past(1):
                            act.wait_ge(hidden_dve.sem, hidden_dve.done(u - 1))
                        act.activation(gate[:, 0:2, :], ps[:, HID_A, :].rearrange("p (c r) -> p c r", c=2), ACT.Silu)\
                           .then_inc(hidden_act.sem, 1)
                        act.activation(gate[0:size[2], 2, :], ps[0:size[2], HID_A + 1, 0:ROWS], ACT.Silu)\
                           .then_inc(hidden_act.sem, 1)

            in_steps(act, TL, DEPTH, step)

        @block.vector
        def _(dve):
            def step(t):
                if active(t, 1, TL):
                    u = t - 1
                    dve.wait_ge(hidden_ps.sem, hidden_ps.done(u))
                    if u.past(2):
                        dve.wait_ge(out_ps.sem, out_ps.done(u - 2))
                    if layer == 0:
                        for c in range(2, 4):
                            dve.tensor_scalar(hidden[:, u.par, c, :], ps[:, HID_B - 1, (c - 2) * ROWS:(c - 1) * ROWS],
                                              b_in[:, u.par, c:c + 1], 0.0, ALU.add, ALU.max).then_inc(hidden_dve.sem, 1)
                    else:
                        dve.wait_ge(hidden_act.sem, hidden_act.after(u, 0))
                        dve.tensor_tensor(hidden[:, u.par, 0:2, :], ps[:, HID_B, :].rearrange("p (c r) -> p c r", c=2),
                                          gate[:, 0:2, :], ALU.mult).then_inc(hidden_dve.sem, 1)
                        dve.wait_ge(hidden_act.sem, hidden_act.after(u, 1))
                        dve.tensor_tensor(hidden[0:size[2], u.par, 2, :], ps[0:size[2], HID_B + 1, 0:ROWS],
                                          gate[0:size[2], 2, :], ALU.mult).then_inc(hidden_dve.sem, 1)
                if active(t, 2, TL):
                    u = t - 2
                    dve.wait_ge(out_ps.sem, out_ps.done(u))
                    if u.past(2):
                        dve.wait_ge(stored[u.par].sem, u.pair * 16)
                    out = ps[:, OUT + u.par, 0:2 * D].rearrange("p (a d) -> p a d", a=2)
                    if layer == 0:
                        dve.tensor_tensor(result[:, u.par, :, :], out, b_out[:, u.par, :].unsqueeze(1).broadcast_to([P, 2, D]),
                                          ALU.add).then_inc(result_done.sem, 1)
                    else:
                        dve.tensor_copy(result[:, u.par, :, :], out).then_inc(result_done.sem, 1)

            in_steps(dve, TL, DEPTH, step)

        @block.tensor
        def _(pe):
            def turn(u):
                pe.wait_ge(loaded[u.par].sem, (u.pair + 1) * (LOADS * 16))
                if u.past(1):
                    pe.wait_ge(rowsT_ready.sem, rowsT_ready.done(u - 1))
                for a in range(2):
                    mm = pe.transpose(ps[:, TURN, a * P:(a + 1) * P], rows[:, u.par, a, :], k.ident[:, :])
                mm.then_inc(turned.sem, 1)

            def into_hidden(u):
                pe.wait_ge(rowsT_ready.sem, rowsT_ready.done(u))
                if u.past(1):
                    pe.wait_ge(hidden_act.sem, hidden_act.done(u - 1))
                    pe.wait_ge(hidden_dve.sem, hidden_dve.done(u - 1))
                if layer == 0:
                    for c in range(HC):
                        mm = pe.matmul(ps[:, HID_A + c // 2, c % 2 * ROWS:(c % 2 + 1) * ROWS],
                                       w_in[:, u.par, c:DF:HC], rowsT[:, u.par, :], start=True, stop=True)
                else:
                    for w, bank in ((0, HID_A), (HID, HID_B)):
                        for c in range(HC):
                            mm = pe.matmul(ps[0:size[c], bank + c // 2, c % 2 * ROWS:(c % 2 + 1) * ROWS],
                                           w_in[:, u.par, w + c * P:w + c * P + size[c]], rowsT[:, u.par, :],
                                           start=True, stop=True)
                mm.then_inc(hidden_ps.sem, 1)

            def out_of_hidden(u):
                pe.wait_ge(hidden_act.sem, hidden_act.done(u))
                pe.wait_ge(hidden_dve.sem, hidden_dve.done(u))
                if u.past(2):
                    pe.wait_ge(result_done.sem, result_done.done(u - 2))
                for a in range(2):
                    for c in range(HC):
                        mm = pe.matmul(ps[:, OUT + u.par, a * D:(a + 1) * D], hidden[0:size[c], u.par, c, a * P:(a + 1) * P],
                                       w_out[0:size[c], u.par, c, :], start=(c == 0), stop=(c == HC - 1))
                mm.then_inc(out_ps.sem, 1)

            def step(t):
                if active(t, 2, TL):
                    out_of_hidden(t - 2)
                if active(t, 1, TL):
                    into_hidden(t - 1)
                if active(t, 0, TL):
                    turn(t)

            in_steps(pe, TL, DEPTH, step)


def experts0(nc, k):
    experts(nc, k, 0)


def experts1(nc, k):
    experts(nc, k, 1)




def attend(nc, k, layer):
    ROWS_K = (K0, K1)[layer]
    ROWS_A = ROWS_K + 3
    UNITS = B * NG
    RING = 4
    MCH, SCH = 10, 5
    stacks = ((k.q_stack, k.k_stack), (k.q_stack1, k.k_stack1))[layer]
    w_o = (W_O0, W_O1)[layer]
    with ExitStack() as ctx:
        sb, banks, signal = phase_resources(nc, ctx, f"attend{layer}")
        q = sb("q", [P, RING, GH, S], BF16)
        ks = sb("ks", [P, RING, GH, S], BF16)
        neg_max = sb("neg_max", [P, 2, GH, QT])
        rest = sb("rest", [P, GH * QT])
        max_parts = sb("max_parts", [P, 2, 3, GH * QT], BF16)
        maxT = sb("maxT", [3 * GH * QT, 2, P], BF16)
        probs = sb("probs", [P, 2, 2 * SCH, S])
        vals = sb("vals", [P, 2, QT * GH, 32])
        mixT = sb("mixT", [P, S])
        inv = sb("inv", [P, QT * GH])
        context = sb("context", [P, 2, QT, D])
        contextT = sb("contextT", [P, S])
        x_tile = sb("x_tile", [P, 2, QT, D]) if layer == 0 else None
        out_tile = sb("out_tile", [P, 2, QT, D]) if layer == 1 else None
        ps = banks("attend_ps", 8)
        MAXB, PROB, MIX, TURN = 0, 2, 6, 7

        loaded = [signal(f"loaded{i}", 2, 16) for i in range(RING)]
        preset = signal("preset")
        vals_ready = signal("vals_ready")
        scored, maxed = signal("scored", MCH), signal("maxed", MCH)
        high_done, rest_done, mid_done, parts_done = (signal(x) for x in ("high_done", "rest_done", "mid_done", "parts_done"))
        max_turned, maxT_ready = signal("max_turned"), signal("maxT_ready")
        max_in = [signal(f"max_in{i}", by=16) for i in range(2)]
        prob_ps, exped = signal("prob_ps", SCH), signal("exped", SCH)
        mixed, mixT_ready, mix_turned, inv_done, context_done = (signal(x) for x in ("mixed", "mixT_ready", "mix_turned", "inv_done", "context_done"))
        context_turned, contextT_ready, projected, added = (signal(x) for x in ("context_turned", "contextT_ready", "projected", "added"))
        x_in = [signal(f"x_in{i}", by=16) for i in range(2)]
        biased, first_added, summed = signal("biased"), signal("first_added"), signal("summed")
        if layer == 0:
            z_sum, z_norm, z_gain = sb("z_sum", [P, QT, D]), sb("z_norm", [P, QT, D]), sb("z_gain", [P, QT, D])
            z_tile = sb("z_tile", [P, QT, D])
            z_stats, z_mv, z_ve, z_rstd = sb("z_stats", [P, QT, 7]), sb("z_mv", [P, QT, 2]), sb("z_ve", [P, QT]), sb("z_rstd", [P, QT])
            z_summed, z_stats_done, z_mv_done, z_eps_done = signal("z_summed"), signal("z_stats_done", QT), signal("z_mv_done", QT), signal("z_eps_done")
            z_rstd_done, z_normed, z_scaled, z_ready = signal("z_rstd_done"), signal("z_normed", QT), signal("z_scaled"), signal("z_ready")
            z_stored = signal("z_stored", B, 16)
        gathered = k.gathered[layer]
        stored = [signal(f"stored{i}", by=16) for i in range(2)]
        DEPTH = 6
        block = ctx.enter_context(nc.Block())

        def max_chunk(c):
            pair, kind = divmod(c, 5)
            h = 2 * pair + kind // 2
            if kind == 4:
                return [(2 * pair, 1, 0), (2 * pair + 1, 1, 256)]
            return [(h, 3, 0)] if kind % 2 == 0 else [(h, 2, 0), (h, 0, 384)]

        def prob_bank(n):
            pair, kind = divmod(n, 5)
            h = 2 * pair + kind // 2
            if kind == 4:
                return [(2 * pair, 2, 0), (2 * pair + 1, 2, 256)]
            return [(h, 0, 0)] if kind % 2 == 0 else [(h, 1, 0), (h, 3, 384)]

        prob_place = {(h, kt): (n, col) for n in range(2 * SCH) for h, kt, col in prob_bank(n)}

        @block.sync
        def _(sp):
            def step(t):
                if active(t, 0, UNITS):
                    if t.past(RING):
                        sp.wait_ge(prob_ps.sem, prob_ps.done(t - RING))
                    else:
                        sp.wait_ge(preset.sem, 2)
                    for side, dst in enumerate((q, ks)):
                        src = stacks[side][bass.ds(t.row, 1), t.group * GH:(t.group + 1) * GH, :, :]
                        sp.dma_start(dst[0:ROWS_K, t.group, :, :], src.rearrange("b h r t -> r (b h) t"))\
                          .then_inc(loaded[t.group].sem, 16)
                    if t.group == 0 and layer == 0:
                        if t.past(2 * NG):
                            sp.wait_ge(added.sem, added.done(t.row - 2))
                        sp.dma_start(x_tile[:, t.row_par, :, :],
                                     k.x_flat[bass.ds(t.row, 1), :, :].rearrange("b (j p) d -> p (b j) d", p=P))\
                          .then_inc(x_in[t.row_par].sem, 16)
                if active(t, 1, UNITS):
                    u = t - 1
                    sp.wait_ge(maxT_ready.sem, maxT_ready.done(u))
                    sp.dma_start(q[ROWS_K:ROWS_A, u.group, :, :], maxT[:, u.par, :]).then_inc(max_in[u.par].sem, 16)
                if active(t, 5, UNITS) and (t - 5).group == NG - 1 and layer == 0:
                    r = (t - 5).row
                    sp.wait_ge(z_ready.sem, z_ready.done(r))
                    for b in range(B):
                        sp.dma_start(k.z[b, bass.ds(r * (QT * POS), QT * POS), :].rearrange("(j s) d -> s j d", j=QT),
                                     z_tile[b * POS:(b + 1) * POS, :, :]).then_inc(z_stored.sem, 16)
                if layer == 1 and active(t, 5, UNITS) and (t - 5).group == NG - 1:
                    u = t - 5
                    sp.wait_ge(summed.sem, summed.done(u.row))
                    sp.dma_start(k.out[bass.ds(u.row, 1), :, :].rearrange("b (j p) d -> p (b j) d", p=P),
                                 out_tile[:, u.row_par, :, :]).then_inc(stored[u.row_par].sem, 16)

            in_steps(sp, UNITS, DEPTH, step, 2 * NG)
            if layer == 1:
                for i in range(2):
                    sp.wait_ge(stored[i].sem, B // 2 * 16)
            else:
                sp.wait_ge(z_stored.sem, z_stored.done(B - 1))

        @block.gpsimd
        def _(pool):
            pool.memset(ks[0:ROWS_A, :, :, :], 1.0).then_inc(preset.sem, 1)
            pool.memset(vals[:, :, :, :], 0.0).then_inc(preset.sem, 1)
            pool.wait_ge(preset.sem, 2)
            pool.memset(vals[:, :, :, HD:HD + 1], 1.0).then_inc(preset.sem, 1)
            pool.wait_ge(preset.sem, 3)
            src = (k.done0, k.done1)[layer]

            def second_norm(r):
                here = slice(r * QT, (r + 1) * QT)
                for i in range(4):
                    pool.wait_ge(gathered[i].sem, (r + 1) * 16)
                if r >= 1:
                    pool.wait_ge(z_normed.sem, z_normed.done(r - 1))
                pool.tensor_tensor(z_sum[:, :, :], k.y[:, here, :], k.moe[:, here, :], ALU.add).then_inc(z_summed.sem, 1)
                ln_rstd(pool, k, z_mv, z_ve, z_rstd, z_mv_done, z_eps_done, z_rstd_done, r)
                pool.wait_ge(z_normed.sem, z_normed.done(r))
                pool.tensor_tensor(z_gain[:, :, :], z_norm[:, :, :], wide(k.row[:, R_G2, :]), ALU.mult).then_inc(z_scaled.sem, 1)
                pool.wait_ge(z_scaled.sem, z_scaled.done(r))
                if r >= 1:
                    pool.wait_ge(z_stored.sem, z_stored.done(r - 1))
                pool.tensor_tensor(z_tile[:, :, :], z_gain[:, :, :], wide(k.row[:, R_BE2, :]), ALU.add).then_inc(z_ready.sem, 1)

            for n in range(UNITS + NG):
                if layer == 0 and n >= 7 and (n - 7) % NG == 0:
                    second_norm((n - 7) // NG)
                if n >= UNITS:
                    continue
                if n >= 2:
                    pool.wait_ge(mixed.sem, mixed.done(n - 2))
                b, g = divmod(n, NG)
                pool.tensor_copy(vals[:, n % 2, :, 0:HD].rearrange("p (j h) d -> p j h d", j=QT),
                                 k.v_all[:, b, :, g * GH * HD:(g + 1) * GH * HD].rearrange("p j (h d) -> p j h d", h=GH))\
                    .then_inc(vals_ready.sem, 1)
                for c in range(layer + 1):
                    m = n * (layer + 1) + c
                    if m >= 4:
                        pool.wait_ge(gathered[m % 4].sem, m // 4 * 16)
                    pool.indirect_dma_start(k.moe[:, c * NT + n, :], None, src,
                                            bass.IndirectOffsetOnAxis(ap=k.rank_row[:, c * NT + n:c * NT + n + 1], axis=0))\
                        .then_inc(gathered[m % 4].sem, 16)
            for i in range(4):
                pool.wait_ge(gathered[i].sem, UNITS * (layer + 1) // 4 * 16)

        @block.scalar
        def _(act):
            def exponentials(u, c):
                act.wait_ge(prob_ps.sem, prob_ps.after(u, c))
                if c == 0 and u.past(2):
                    act.wait_ge(mixed.sem, mixed.done(u - 2))
                bank = PROB + 2 * ((u.par + c) % 2)
                act.activation(probs[:, u.par, 2 * c:2 * c + 2, :], ps[:, bank:bank + 2, :], ACT.Exp)\
                   .then_inc(exped.sem, 1)

            def step(t):
                row_ends = active(t, 5, UNITS) and (t - 5).group == NG - 1
                for c in range(SCH):
                    if active(t, 2, UNITS):
                        exponentials(t - 2, c)
                    if c == 2 and row_ends:
                        r = (t - 5).row
                        act.wait_ge(context_turned.sem, context_turned.done(r))
                        if (t - 5).past(NG):
                            act.wait_ge(projected.sem, projected.done(r - 1))
                        act.copy(contextT[:, :], ps[:, TURN, :]).then_inc(contextT_ready.sem, 1)
                if active(t, 3, UNITS):
                    u = t - 3
                    act.wait_ge(mixed.sem, mixed.done(u))
                    if u.past(1):
                        act.wait_ge(mix_turned.sem, mix_turned.done(u - 1))
                    act.copy(mixT[:, :], ps[:, MIX, :]).then_inc(mixT_ready.sem, 1)

            in_steps(act, UNITS, DEPTH, step, 2 * NG)

        @block.tensor
        def _(pe):
            def maxima(u, c):
                if c == 0:
                    pe.wait_ge(loaded[u.group].sem, (u.row + 1) * 32)
                if u.past(1) or c >= 2:
                    pe.wait_ge(maxed.sem, maxed.after(u, c - 2))
                g = u.group
                for h, qt, col in max_chunk(c):
                    last = col + (qt + 1) * P
                    pe.matmul(ps[:, MAXB + c % 2, col:last], q[0:ROWS_K, g, h, qt * P:(qt + 1) * P],
                              ks[0:ROWS_K, g, h, 0:(qt + 1) * P], start=True, stop=False)
                    mm = pe.matmul(ps[:, MAXB + c % 2, last - P:last], k.identb[:, :], k.causal_q[:, :],
                                   start=False, stop=True)
                mm.then_inc(scored.sem, 1)

            def turn_maxima(u):
                pe.wait_ge(parts_done.sem, parts_done.done(u))
                pe.matmul(ps[0:3 * GH * QT, TURN, 0:P], max_parts[:, u.par, :, :].rearrange("p a b -> p (a b)"), k.identb[:, :],
                          start=True, stop=True)\
                  .then_inc(max_turned.sem, 1)

            def probabilities(u, c):
                if c == 0:
                    pe.wait_ge(max_in[u.par].sem, (u.pair + 1) * 16)
                if u.past(1) or c >= 2:
                    pe.wait_ge(exped.sem, exped.after(u, c - 2))
                g = u.group
                for n in (2 * c, 2 * c + 1):
                    bank = PROB + 2 * ((u.par + c) % 2) + n % 2
                    for h, kt, col in prob_bank(n):
                        pe.matmul(ps[:, bank, col:col + S - kt * P], ks[0:ROWS_A, g, h, kt * P:(kt + 1) * P],
                                  q[0:ROWS_A, g, h, kt * P:S], start=True, stop=False)
                        mm = pe.matmul(ps[:, bank, col:col + P], k.identb[:, :], k.causal_k[:, :], start=False, stop=True)
                mm.then_inc(prob_ps.sem, 1)

            def mix(u, kt):
                if kt == 0:
                    pe.wait_ge(exped.sem, exped.done(u))
                    pe.wait_ge(vals_ready.sem, vals_ready.done(u))
                    if u.past(1):
                        pe.wait_ge(mixT_ready.sem, mixT_ready.done(u - 1))
                for h in range(GH):
                    n, col = prob_place[h, kt]
                    mm = pe.matmul(ps[32 * h:32 * h + 32, MIX, kt * P:S], vals[:, u.par, kt * GH + h, :],
                                   probs[:, u.par, n, col:col + S - kt * P], start=(kt == 0), stop=(kt == QT - 1))
                if kt == QT - 1:
                    mm.then_inc(mixed.sem, 1)

            def turn_mix(u):
                pe.wait_ge(mixT_ready.sem, mixT_ready.done(u))
                for j in range(QT):
                    mm = pe.transpose(ps[:, TURN, j * P:(j + 1) * P], mixT[:, j * P:(j + 1) * P], k.ident[:, :])
                mm.then_inc(mix_turned.sem, 1)

            def turn_context(u):
                for j in range(QT):
                    mm = pe.transpose(ps[:, TURN, j * P:(j + 1) * P], context[:, u.row_par, j, :], k.ident[:, :])
                mm.then_inc(context_turned.sem, 1)

            def project(u):
                pe.wait_ge(contextT_ready.sem, contextT_ready.done(u.row))
                for j in range(QT):
                    mm = pe.matmul(ps[:, TURN, j * P:(j + 1) * P], contextT[:, j * P:(j + 1) * P], k.wT[:, w_o, :],
                                   start=True, stop=True)
                mm.then_inc(projected.sem, 1)

            def turn_free(t, use):
                if use == 2 and active(t, 4, UNITS):
                    pe.wait_ge(context_done.sem, context_done.done(t - 4))
                elif active(t, 5, UNITS):
                    pe.wait_ge(context_done.sem, context_done.done(t - 5))
                if use and active(t, 1, UNITS):
                    pe.wait_ge(maxT_ready.sem, maxT_ready.done(t - 1))
                if active(t, 6, UNITS) and (t - 6).group == NG - 1:
                    pe.wait_ge(added.sem, added.done((t - 6).row))

            def step(t):
                row_ends = active(t, 5, UNITS) and (t - 5).group == NG - 1
                for c in range(MCH):
                    if active(t, 0, UNITS):
                        maxima(t, c)
                    if c % 2 and active(t, 2, UNITS):
                        probabilities(t - 2, c // 2)
                    if c % 2 == 0 and c < 2 * QT and active(t, 3, UNITS):
                        mix(t - 3, c // 2)
                    if c == 1 and active(t, 1, UNITS):
                        turn_free(t, 0)
                        turn_maxima(t - 1)
                    if c == 4 and active(t, 4, UNITS):
                        turn_free(t, 1)
                        turn_mix(t - 4)
                    if c == 7 and row_ends:
                        turn_free(t, 2)
                        turn_context(t - 5)
                    if c == 9 and row_ends:
                        project(t - 5)

            in_steps(pe, UNITS, DEPTH, step, 2 * NG)

        @block.vector
        def _(dve):
            def reduce(u, c):
                dve.wait_ge(scored.sem, scored.after(u, c))
                bank = ps[:, MAXB + c % 2, :]
                blocks = max_chunk(c)
                if c % 5 == 4:
                    h, qt, _ = blocks[0]
                    out = neg_max[:, u.par, h:h + 2, qt]
                    dve.tensor_reduce(out, bank.rearrange("p (h t) -> p h t", h=2), X_AXIS, ALU.max, negate=True)\
                       .then_inc(maxed.sem, 1)
                    return
                for n, (h, qt, col) in enumerate(blocks):
                    ins = dve.tensor_reduce(neg_max[:, u.par, h, qt:qt + 1], bank[:, col:col + (qt + 1) * P], X_AXIS,
                                            ALU.max, negate=True)
                ins.then_inc(maxed.sem, 1)

            def split_maxima(u):
                flat = neg_max[:, u.par, :, :].rearrange("p h j -> p (h j)")
                parts = max_parts[:, u.par, :, :]
                if u.past(2):
                    dve.wait_ge(max_turned.sem, max_turned.done(u - 2))
                dve.wait_ge(maxed.sem, maxed.done(u))
                dve.tensor_copy(parts[:, 0, :], flat).then_inc(high_done.sem, 1)
                dve.wait_ge(high_done.sem, high_done.done(u))
                dve.tensor_tensor(rest[:, :], flat, parts[:, 0, :], ALU.subtract).then_inc(rest_done.sem, 1)
                dve.wait_ge(rest_done.sem, rest_done.done(u))
                dve.tensor_copy(parts[:, 1, :], rest[:, :]).then_inc(mid_done.sem, 1)
                dve.wait_ge(mid_done.sem, mid_done.done(u))
                dve.tensor_tensor(parts[:, 2, :], rest[:, :], parts[:, 1, :], ALU.subtract).then_inc(parts_done.sem, 1)

            def copy_maxima(u):
                dve.wait_ge(max_turned.sem, max_turned.done(u))
                if u.past(2):
                    dve.wait_ge(max_in[u.par].sem, u.pair * 16)
                dve.tensor_copy(maxT[:, u.par, :], ps[0:3 * GH * QT, TURN, 0:P])\
                   .then_inc(maxT_ready.sem, 1)

            def divide(u):
                dve.wait_ge(mix_turned.sem, mix_turned.done(u))
                turned = ps[:, TURN, :].rearrange("p (n f) -> p n f", f=32)
                dve.reciprocal(inv[:, :], turned[:, :, HD]).then_inc(inv_done.sem, 1)
                dve.wait_ge(inv_done.sem, inv_done.done(u))
                if u.group == 0 and u.past(2 * NG):
                    dve.wait_ge(context_turned.sem, context_turned.done(u.row - 2))
                out = context[:, u.row_par, :, u.group * GH * HD:(u.group + 1) * GH * HD]
                dve.tensor_tensor(out.rearrange("p j (h d) -> p j h d", h=GH),
                                  turned[:, :, 0:HD].rearrange("p (j h) d -> p j h d", h=GH),
                                  inv[:, :].rearrange("p (j h) -> p j h", h=GH).unsqueeze(3).broadcast_to([P, QT, GH, HD]),
                                  ALU.mult).then_inc(context_done.sem, 1)

            def add_row(u):
                r = u.row
                dve.wait_ge(projected.sem, projected.done(r))
                proj = ps[:, TURN, :].rearrange("p (j d) -> p j d", j=QT)
                here = bass.ds(r * QT, QT)
                if layer == 0:
                    dve.wait_ge(x_in[u.row_par].sem, (r - u.row_par) * 8 + 16)
                    dve.tensor_tensor(k.x_sum[:, here, :], proj, x_tile[:, u.row_par, :, :], ALU.add).then_inc(added.sem, 1)
                    return
                if u.past(2 * NG):
                    dve.wait_ge(stored[u.row_par].sem, (r - u.row_par) * 8)
                out = out_tile[:, u.row_par, :, :]
                dve.tensor_tensor(out, proj, k.x_sum[:, here, :], ALU.add).then_inc(added.sem, 1)
                dve.wait_ge(added.sem, added.done(r))
                dve.tensor_tensor(out, out, wide(k.row[:, R_O1, :]), ALU.add).then_inc(biased.sem, 1)
                for i in range(4):
                    dve.wait_ge(gathered[i].sem, (r + 1) * 32)
                dve.wait_ge(biased.sem, biased.done(r))
                dve.tensor_tensor(out, out, k.moe[:, here, :], ALU.add).then_inc(first_added.sem, 1)
                dve.wait_ge(first_added.sem, first_added.done(r))
                dve.tensor_tensor(out, out, k.moe[:, bass.ds(r * QT + NT, QT), :], ALU.add).then_inc(summed.sem, 1)

            def step(t):
                row_ends = active(t, 5, UNITS) and (t - 5).group == NG - 1
                for c in range(MCH):
                    if active(t, 0, UNITS):
                        reduce(t, c)
                    if c == 1 and active(t, 1, UNITS):
                        copy_maxima(t - 1)
                    if c == 3 and layer == 0 and row_ends:
                        ln_stats(dve, z_sum, z_stats, z_mv, z_stats_done, z_mv_done, (t - 5).row, z_summed)
                    if c == 5 and active(t, 4, UNITS):
                        divide(t - 4)
                    if c == 7 and layer == 0 and row_ends:
                        if (t - 5).past(NG):
                            dve.wait_ge(z_scaled.sem, z_scaled.done((t - 5).row - 1))
                        ln_apply(dve, z_norm, z_sum, z_mv, z_rstd, z_rstd_done, z_normed, (t - 5).row)
                if active(t, 0, UNITS):
                    split_maxima(t)
                if row_ends:
                    add_row(t - 5)

            in_steps(dve, UNITS, DEPTH, step, 2 * NG)


def attend0(nc, k):
    attend(nc, k, 0)


def attend1(nc, k):
    attend(nc, k, 1)




def program(nc, names, args, out, phases=None):
    k = Kept()
    k.arg, k.out = dict(zip(names, args)), out
    with ExitStack() as ctx:
        def dram(name, shape, dtype=F32):
            return nc.dram_tensor(name, shape, dtype).ap()

        def sb(name, shape, dtype=F32):
            return ctx.enter_context(nc.sbuf_tensor(name, shape, dtype))

        k.x_flat = k.arg["L0_attn_x"]
        k.sorted0, k.sorted1 = (dram(f"sorted{i}", [TILES[i] * ROWS, D]) for i in range(2))
        k.done0, k.done1 = (dram(f"done{i}", [TILES[i] * ROWS, D]) for i in range(2))
        k.z = dram("z", [B, S, D])
        k.q_stack, k.k_stack = (dram(f"{n}_stack", [B, NH, K0, S], BF16) for n in "qk")
        k.q_stack1, k.k_stack1 = (dram(f"{n}_stack1", [B, NH, K1, S], BF16) for n in "qk")
        k.wT = sb("wT", [P, 14, D])
        k.gateT = sb("gateT", [P, 2, E])
        k.row = sb("row", [P, 8, D])
        k.col = sb("col", [P, 7])
        k.hscale = sb("hscale", [P, 1])
        k.ident, k.identb = sb("ident", [P, P]), sb("identb", [P, P], BF16)
        k.causal_q, k.causal_k = sb("causal_q", [P, P], BF16), sb("causal_k", [P, P], BF16)
        k.batch_mask = sb("batch_mask", [P, P], BF16)
        k.before, k.ones, k.head_mean = sb("before", [P, P]), sb("ones", [P, P]), sb("head_mean", [P, P])
        k.half, k.ln_eps = sb("half", [P, QT]), sb("ln_eps", [P, QT])
        k.counted_i, k.counted = sb("counted_i", [P, 64], I32), sb("counted", [P, 64])
        k.logits = sb("logits", [P, NT, E])
        k.v_all = sb("v_all", [P, B, QT, D])
        k.rank_row = sb("rank_row", [P, 2 * NT], U32)
        k.tile_expert = sb("tile_expert", [P, 64], I32)
        k.y = sb("y_all", [P, NT, D])
        k.x_sum = sb("x_sum", [P, NT, D])
        k.moe = sb("moe", [P, 2 * NT, D])
        k.scattered, k.gathered = ([[Signal(ctx.enter_context(nc.semaphore(f"{name}{layer}_{i}")), by=16) for i in range(4)]
                                    for layer in range(2)] for name in ("scattered", "gathered"))
        for phase in phases or PHASES:
            phase(nc, k)


PHASES = (setup, mix0, route0, prepare0, experts0, attend0, prepare1, route1, experts1, attend1)

_INS = ['L0_attn_x', 'L0_attn_Wq_amp', 'L0_attn_Wk_amp', 'L0_attn_Wq_phi', 'L0_attn_Wk_phi', 'L0_attn_Wv',
        'L0_attn_Wo', 'L0_attn_score_log_scale', 'L0_ffn_Wqkv', 'L0_ffn_bqkv', 'L0_ffn_Wo', 'L0_ffn_bo',
        'L0_ffn_g1', 'L0_ffn_be1', 'L0_ffn_g2', 'L0_ffn_be2', 'L0_ffn_Wg', 'L0_ffn_W1', 'L0_ffn_b1', 'L0_ffn_W2',
        'L0_ffn_b2', 'L1_attn_Wq', 'L1_attn_bq', 'L1_attn_Wk', 'L1_attn_bk', 'L1_attn_Wv', 'L1_attn_bv',
        'L1_attn_Wo', 'L1_attn_bo', 'L1_ffn_gate_w', 'L1_ffn_w1', 'L1_ffn_w2', 'L1_ffn_w3']
_OUTS = [((8, 512, 128), 'float32')]


def kernel(**inputs):
    import numpy as _np
    import concourse.bacc as _bacc
    from concourse import mybir as _mybir
    from concourse.bass_utils import run_bass_kernel_spmd as _run

    nc = _bacc.Bacc("TRN2", target_bir_lowering=False, num_devices=1)
    arrays, args = {}, []
    for name in _INS:
        a = _np.ascontiguousarray(inputs[name])
        arrays[f"in_{name}_dram"] = a
        args.append(nc.dram_tensor(f"in_{name}_dram", a.shape, _mybir.dt.from_np(a.dtype), kind="ExternalInput").ap())
    for i, (shape, dtype) in enumerate(_OUTS):
        dt = _mybir.dt.from_np(_np.dtype(dtype))
        args.append(nc.dram_tensor(f"out_{i}_dram", shape, dt, kind="ExternalOutput").ap())
    program(nc, _INS, args[:-1], args[-1])
    r = _run(nc, [arrays], core_ids=[0])
    got = tuple(r.results[0][f"out_{i}_dram"] for i in range(len(_OUTS)))
    return got[0]
```

```python
from contextlib import ExitStack

import numpy as np

import concourse.bass as bass
from concourse import mybir

F32 = mybir.dt.float32
BF16 = mybir.dt.bfloat16
I32 = mybir.dt.int32
U32 = mybir.dt.uint32
ALU = mybir.AluOpType
ACT = mybir.ActivationFunctionType
X_AXIS = mybir.AxisListType.X

P = 128
B, S, D = 8, 512, 128
T = B * S
NT = T // P
NH = 16
HD = D // NH
MH = 4
MD = D // MH
E = 8
DF = 512
HID = 352
QT = S // P
GH = 4
NG = NH // GH
ROWS = 2 * P
TILES = (T // ROWS + E - 1, 2 * T // ROWS + E - 1)
POS = P // B
LN_EPS = 1e-5
AMP_EPS = 1e-6
NEG = -1e30
PI = float(np.pi)

Q_PARTS = (0, 1, 0, 2, 0, 1)
K_PARTS = (0, 0, 1, 0, 2, 1)
SLOTS = len(Q_PARTS)
K0, K1 = SLOTS * 2 * HD, SLOTS * HD

(W_QA, W_KA, W_QP, W_KP, W_V0, W_O0, W_MQ, W_MK, W_MV, W_MO, W_Q1, W_K1, W_V1, W_O1) = range(14)
C_MQ, C_MK, C_Q1, C_K1, C_HS, C_PIH, C_EPS = range(7)
R_MV, R_MO, R_G1, R_BE1, R_G2, R_BE2, R_V1, R_O1 = range(8)


class Kept:
    pass


class Signal:

    def __init__(self, sem, per=1, by=1):
        self.sem, self.per, self.by = sem, per, by

    def after(self, unit, k=0):
        return (n_of(unit) * self.per + k + 1) * self.by

    def done(self, unit):
        return (n_of(unit) + 1) * self.per * self.by


def n_of(unit):
    return unit.n if isinstance(unit, Unit) else unit


class Unit:

    def __init__(self, turn, phase, cycle=2):
        self.turn, self.phase, self.cycle = turn, phase, cycle

    @property
    def n(self):
        return self.turn * self.cycle + self.phase

    @property
    def par(self):
        return self.phase % 2

    @property
    def pair(self):
        return self.turn * (self.cycle // 2) + self.phase // 2

    @property
    def group(self):
        return self.phase % NG

    @property
    def row(self):
        return self.turn * (self.cycle // NG) + self.phase // NG

    @property
    def row_par(self):
        return self.phase // NG % 2

    def __sub__(self, k):
        return Unit(self.turn + (self.phase - k) // self.cycle, (self.phase - k) % self.cycle, self.cycle)

    def __add__(self, k):
        return self - (-k)

    def past(self, k):
        return not isinstance(self.turn, int) or self.n >= k


def in_steps(eng, units, depth, step, cycle=2, first=4):
    turns = (units - first) // cycle
    for t in range(first):
        step(Unit(t // cycle, t % cycle, cycle))
    with eng.Fori(0, turns) as i:
        for phase in range(cycle):
            step(Unit(i + first // cycle, phase, cycle))
    for t in range(first + cycle * turns, units + depth - 1):
        step(Unit(t // cycle, t % cycle, cycle))


def active(t, k, units):
    return not isinstance(t.turn, int) or 0 <= t.n - k < units


def wide(row):
    return row.unsqueeze(1).broadcast_to([P, QT, D])


def phase_resources(nc, ctx, phase):
    def sb(name, shape, dtype=F32):
        return ctx.enter_context(nc.sbuf_tensor(f"{phase}_{name}", shape, dtype))

    def banks(name, n):
        return ctx.enter_context(nc.psum_tensor(f"{phase}_{name}", [P, n, 512], F32))

    numbers = []

    def clear():
        with nc.Block() as block:
            @block.sync
            def _(sp):
                for n in sorted(numbers):
                    if n - 1 not in numbers:
                        end = n
                        while end in numbers:
                            end += 1
                        sp.sem_clear(range(n, end))

    ctx.callback(clear)

    def signal(name, per=1, by=1):
        sem = ctx.enter_context(nc.semaphore(f"{phase}_{name}"))
        numbers.append(sem.num)
        return Signal(sem, per, by)

    return sb, banks, signal




def setup(nc, k):
    with ExitStack() as ctx:
        sb, banks, signal = phase_resources(nc, ctx, "setup")
        wraw = sb("wraw", [P, 14, D])
        graw = sb("graw", [E, 2, D])
        zeros = sb("zeros", [P, 2, ROWS * D // P])
        turned_ps = banks("turned_ps", 4)
        raw_in = [signal(f"raw_in{i}", by=16) for i in range(14)]
        gate_in = signal("gate_in", per=2, by=16)
        rows_in = signal("rows_in", per=8, by=16)
        cols_in = signal("cols_in", per=6, by=16)
        base_set = signal("base_set")
        ident_ready = signal("ident_ready")
        turned = signal("turned")
        copied = signal("copied")
        zero_set = signal("zero_set")
        zero_out = signal("zero_out", by=16)
        scale_exp = signal("scale_exp")
        scale_ready = signal("scale_ready")
        block = ctx.enter_context(nc.Block())
        squares = [k.arg["L0_attn_Wq_amp"], k.arg["L0_attn_Wk_amp"], k.arg["L0_attn_Wq_phi"], k.arg["L0_attn_Wk_phi"], k.arg["L0_attn_Wv"],
                   k.arg["L0_attn_Wo"], k.arg["L0_ffn_Wqkv"][0:D], k.arg["L0_ffn_Wqkv"][D:2 * D], k.arg["L0_ffn_Wqkv"][2 * D:3 * D],
                   k.arg["L0_ffn_Wo"], k.arg["L1_attn_Wq"], k.arg["L1_attn_Wk"], k.arg["L1_attn_Wv"], k.arg["L1_attn_Wo"]]

        @block.sync
        def _(sp):
            for n in range(0, 14, 2):
                sp.dma_start(wraw[:, n, :], squares[n]).then_inc(raw_in[n].sem, 16)
            sp.dma_start(graw[:, 0, :], k.arg["L0_ffn_Wg"]).then_inc(gate_in.sem, 16)
            sp.dma_start(graw[:, 1, :], k.arg["L1_ffn_gate_w"]).then_inc(gate_in.sem, 16)
            sp.wait_ge(zero_set.sem, 1)
            n = 0
            for layer, dst in enumerate((k.sorted0, k.sorted1)):
                for a in range(0, TILES[layer], 2):
                    m = min(2, TILES[layer] - a)
                    sp.dma_start(dst[a * ROWS:(a + m) * ROWS, :].rearrange("(a p r) d -> p a (r d)", a=m, p=P),
                                 zeros[:, 0:m, :]).then_inc(zero_out.sem, 16)
                    n += 1
            sp.wait_ge(zero_out.sem, 16 * n)

        @block.scalar
        def _(act):
            for n in range(1, 14, 2):
                act.dma_start(wraw[:, n, :], squares[n]).then_inc(raw_in[n].sem, 16)
            rows = [k.arg["L0_ffn_bqkv"][2 * D:3 * D], k.arg["L0_ffn_bo"], k.arg["L0_ffn_g1"], k.arg["L0_ffn_be1"], k.arg["L0_ffn_g2"],
                    k.arg["L0_ffn_be2"], k.arg["L1_attn_bv"], k.arg["L1_attn_bo"]]
            for n, row in enumerate(rows):
                act.dma_start(k.row[:, n, :], row.rearrange("(o d) -> o d", o=1).partition_broadcast(P))\
                   .then_inc(rows_in.sem, 16)
            cols = [k.arg["L0_ffn_bqkv"][0:D], k.arg["L0_ffn_bqkv"][D:2 * D], k.arg["L1_attn_bq"], k.arg["L1_attn_bk"]]
            for n, col in enumerate(cols):
                act.dma_start(k.col[:, n:n + 1], col.rearrange("(d o) -> d o", o=1)).then_inc(cols_in.sem, 16)
            act.dma_start(k.col[:, C_HS:C_HS + 1],
                          k.arg["L0_attn_score_log_scale"].rearrange("(h o) -> h o", o=1).broadcast_to([NH, HD]))\
               .then_inc(cols_in.sem, 16)
            act.wait_ge(cols_in.sem, 5 * 16)
            act.activation(k.hscale[:, :], k.col[:, C_HS:C_HS + 1], ACT.Exp).then_inc(scale_exp.sem, 1)
            for n in range(4):
                act.wait_ge(turned.sem, min(4 * n + 4, 14))
                m = min(4, 14 - 4 * n)
                act.copy(k.wT[:, 4 * n:4 * n + m, :], turned_ps[:, n, 0:m * D]).then_inc(copied.sem, 1)
            act.wait_ge(turned.sem, 15)
            act.copy(k.gateT[:, :, :], turned_ps[:, 3, 256:256 + 2 * E]).then_inc(copied.sem, 1)
            act.wait_ge(rows_in.sem, 8 * 16)

        @block.gpsimd
        def _(pool):
            pool.memset(k.ident[:, :], 0.0).then_inc(base_set.sem, 1)
            pool.wait_ge(base_set.sem, 1)
            pool.affine_select(out=k.ident[:, :], in_=k.ident[:, :], compare_op=ALU.not_equal, fill=1.0, base=0,
                               pattern=[[-1, P]], channel_multiplier=1).then_inc(ident_ready.sem, 1)
            pool.memset(zeros[:, :, :], 0.0).then_inc(zero_set.sem, 1)
            pool.memset(k.causal_q[:, :], 0.0).then_inc(base_set.sem, 1)
            pool.memset(k.causal_k[:, :], 0.0).then_inc(base_set.sem, 1)
            pool.memset(k.batch_mask[:, :], NEG).then_inc(base_set.sem, 1)
            pool.memset(k.before[:, :], 1.0).then_inc(base_set.sem, 1)
            pool.memset(k.ones[:, :], 1.0).then_inc(base_set.sem, 1)
            pool.memset(k.head_mean[:, :], 1.0 / HD).then_inc(base_set.sem, 1)
            pool.memset(k.half[:, :], -0.5).then_inc(base_set.sem, 1)
            pool.memset(k.ln_eps[:, :], LN_EPS).then_inc(base_set.sem, 1)
            pool.memset(k.col[:, C_PIH:C_PIH + 1], PI / 2).then_inc(base_set.sem, 1)
            pool.memset(k.col[:, C_EPS:C_EPS + 1], AMP_EPS).then_inc(base_set.sem, 1)
            pool.wait_ge(ident_ready.sem, 1)
            pool.tensor_copy(k.identb[:, :], k.ident[:, :]).then_inc(ident_ready.sem, 1)
            pool.wait_ge(base_set.sem, 11)
            pool.affine_select(out=k.causal_q[:, :], in_=k.causal_q[:, :], compare_op=ALU.is_ge, fill=NEG, base=0,
                               pattern=[[-1, P]], channel_multiplier=1).then_inc(base_set.sem, 1)
            pool.affine_select(out=k.causal_k[:, :], in_=k.causal_k[:, :], compare_op=ALU.is_ge, fill=NEG, base=0,
                               pattern=[[1, P]], channel_multiplier=-1).then_inc(base_set.sem, 1)
            pool.affine_select(out=k.before[:, :], in_=k.before[:, :], compare_op=ALU.is_gt, fill=0.0, base=0,
                               pattern=[[1, P]], channel_multiplier=-1).then_inc(base_set.sem, 1)
            head = k.head_mean[:, :].rearrange("p (h d) -> p h d", d=HD)
            pool.affine_select(out=head, in_=head, compare_op=ALU.is_ge, fill=0.0, base=0,
                               pattern=[[-HD, NH], [0, HD]], channel_multiplier=1).then_inc(base_set.sem, 1)
            pool.wait_ge(base_set.sem, 15)
            pool.affine_select(out=head, in_=head, compare_op=ALU.is_ge, fill=0.0, base=HD - 1,
                               pattern=[[HD, NH], [0, HD]], channel_multiplier=-1).then_inc(base_set.sem, 1)
            for n, m in enumerate(range(-(B - 1), B)):
                pool.wait_ge(base_set.sem, 16 + n)
                pool.affine_select(out=k.batch_mask[:, :], in_=k.batch_mask[:, :], compare_op=ALU.not_equal,
                                   fill=0.0, base=-POS * m, pattern=[[-1, P]], channel_multiplier=1)\
                    .then_inc(base_set.sem, 1)
            pool.iota(k.counted_i[:, :], pattern=[[1, 64]], base=0, channel_multiplier=0)\
                .then_inc(base_set.sem, 1)
            pool.wait_ge(base_set.sem, 32)
            pool.tensor_copy(k.counted[:, :], k.counted_i[:, :]).then_inc(base_set.sem, 1)
            pool.wait_ge(base_set.sem, 33)

        @block.tensor
        def _(pe):
            pe.wait_ge(ident_ready.sem, 1)
            for n in range(14):
                pe.wait_ge(raw_in[n].sem, 16)
                pe.transpose(turned_ps[:, n // 4, n % 4 * D:(n % 4 + 1) * D], wraw[:, n, :], k.ident[:, :])\
                  .then_inc(turned.sem, 1)
            pe.wait_ge(gate_in.sem, 32)
            pe.wait_ge(copied.sem, 4)
            pe.transpose(turned_ps[:, 3, 256:256 + E], graw[:, 0, :], k.ident[0:E, 0:E])
            pe.transpose(turned_ps[:, 3, 256 + E:256 + 2 * E], graw[:, 1, :], k.ident[0:E, 0:E])\
              .then_inc(turned.sem, 1)

        @block.vector
        def _(dve):
            dve.wait_ge(scale_exp.sem, 1)
            dve.tensor_scalar(k.hscale[:, :], k.hscale[:, :], float(HD) ** -0.5, None, ALU.mult)\
               .then_inc(scale_ready.sem, 1)
            dve.wait_ge(scale_ready.sem, 1)




def ln_stats(dve, src, stats, mv, stats_done, mv_done, unit, src_ready=None):
    if src_ready:
        dve.wait_ge(src_ready.sem, src_ready.done(unit))
    for j in range(QT):
        dve.bn_stats(stats[:, j, 0:6], src[:, j, :]).then_inc(stats_done.sem, 1)
    dve.wait_ge(stats_done.sem, stats_done.done(unit))
    dve.tensor_copy(stats[:, 0, 6:7], stats[:, 0, 0:1])
    for j in range(QT):
        dve.bn_aggr(mv[:, j, :], stats[:, j, 0:6]).then_inc(mv_done.sem, 1)


def ln_rstd(pool, k, mv, var_eps, rstd, mv_done, eps_done, rstd_done, unit):
    pool.wait_ge(mv_done.sem, mv_done.done(unit))
    pool.tensor_tensor(var_eps[:, :], mv[:, :, 1], k.ln_eps[:, :], ALU.add).then_inc(eps_done.sem, 1)
    pool.wait_ge(eps_done.sem, eps_done.done(unit))
    pool.tensor_tensor(rstd[:, :], var_eps[:, :], k.half[:, :], ALU.pow).then_inc(rstd_done.sem, 1)


def ln_apply(dve, dst, src, mv, rstd, rstd_done, xn_done, unit):
    dve.wait_ge(rstd_done.sem, rstd_done.done(unit))
    for j in range(QT):
        dve.tensor_scalar(dst[:, j, :], src[:, j, :], mv[:, j, 0:1], rstd[:, j:j + 1], ALU.subtract, ALU.mult)\
           .then_inc(xn_done.sem, 1)




def mix0(nc, k):
    UNITS = T // (QT * P)
    with ExitStack() as ctx:
        sb, banks, signal = phase_resources(nc, ctx, "mix0")
        x_tile = sb("x_tile", [P, 2, QT, D])
        xn = sb("xn", [P, 2, QT, D])
        xnT = sb("xnT", [P, QT * P])
        qT = sb("qT", [P, 2, QT * P])
        k_heads = sb("k_heads", [P, 2, QT, MH, P])
        v = sb("v", [P, 2, QT, D])
        probs = sb("probs", [P, 2, MH, P])
        probsT = sb("probsT", [P, 2, MH, P])
        neg_max = sb("neg_max", [P, 2, MH])
        sums = sb("sums", [P, 2, MH])
        rsums = sb("rsums", [P, 2, MH])
        mixedT = sb("mixedT", [P, QT * P])
        res = sb("res", [P, 2, QT, D])
        res_n = sb("res_n", [P, QT, D])
        res_g = sb("res_g", [P, QT, D])
        y = sb("y", [P, 2, QT, D])
        yT = sb("yT", [P, QT * P])
        stats_a, stats_c = sb("stats_a", [P, QT, 7]), sb("stats_c", [P, QT, 7])
        mv_a, mv_c = sb("mv_a", [P, QT, 2]), sb("mv_c", [P, QT, 2])
        ve_a, ve_c = sb("ve_a", [P, QT]), sb("ve_c", [P, QT])
        rstd_a, rstd_c = sb("rstd_a", [P, QT]), sb("rstd_c", [P, QT])
        ps = banks("mix_ps", 8)
        XV, Q, K_, SC, PT, MX, OUT = 0, 1, 2, 3, 5, 6, 7

        x_in = [signal(f"x_in{i}", B, 16) for i in range(2)]
        heads_zero = signal("heads_zero")
        stats_a_done, mv_a_done = signal("stats_a_done", QT), signal("mv_a_done", QT)
        eps_a_done, rstd_a_done = signal("eps_a_done"), signal("rstd_a_done")
        xn_done = signal("xn_done", QT)
        x_turned, xT_ready = signal("x_turned"), signal("xT_ready")
        q_proj, k_proj, v_proj = signal("q_proj"), signal("k_proj"), signal("v_proj")
        q_ready, v_ready = signal("q_ready"), signal("v_ready")
        k_ready_act, k_ready_dve = signal("k_ready_act", 2), signal("k_ready_dve", 2)
        scored, maxed = signal("scored", QT), signal("maxed", QT)
        exped, sums_inv, normed = signal("exped", QT * MH), signal("sums_inv", QT), signal("normed", QT)
        p_turned, pT_ready, mixed = signal("p_turned", QT), signal("pT_ready", QT), signal("mixed", QT)
        mixT_ready, projected, res_done, res_bias = (signal(x) for x in ("mixT_ready", "projected", "res_done", "res_bias"))
        stats_c_done, mv_c_done = signal("stats_c_done", QT), signal("mv_c_done", QT)
        eps_c_done, rstd_c_done = signal("eps_c_done"), signal("rstd_c_done")
        res_n_done, res_g_done, y_ready = signal("res_n_done", QT), signal("res_g_done"), signal("y_ready")
        y_kept = [signal(f"y_kept{i}", 1, 16) for i in range(2)]
        y_turned, yT_ready, logits_ps, logits_done = (signal(x) for x in ("y_turned", "yT_ready", "logits_ps", "logits_done"))
        DEPTH = 4
        block = ctx.enter_context(nc.Block())

        @block.sync
        def _(sp):
            def load(u):
                if u.past(2):
                    sp.wait_ge(xn_done.sem, xn_done.done(u - 2))
                for b in range(B):
                    src = k.x_flat[b, bass.ds(u.n * (QT * POS), QT * POS), :]
                    sp.dma_start(x_tile[b * POS:(b + 1) * POS, u.par, :, :],
                                 src.rearrange("(j s) d -> s j d", j=QT)).then_inc(x_in[u.par].sem, 16)

            def keep(u):
                sp.wait_ge(y_ready.sem, y_ready.done(u))
                sp.dma_start(k.y[:, bass.ds(u.n * QT, QT), :], y[:, u.par, :, :]).then_inc(y_kept[u.par].sem, 16)

            def step(t):
                if active(t, 0, UNITS):
                    load(t)
                if active(t, 3, UNITS):
                    keep(t - 3)

            in_steps(sp, UNITS, DEPTH, step)
            for i in range(2):
                sp.wait_ge(y_kept[i].sem, 16 * UNITS // 2)

        @block.gpsimd
        def _(pool):
            for half in range(2):
                pool.memset(k_heads[:, half, :, :, :], 0.0).then_inc(heads_zero.sem, 1)

            def step(t):
                if active(t, 2, UNITS):
                    u = t - 2
                    pool.wait_ge(res_done.sem, res_done.done(u))
                    pool.tensor_tensor(res[:, u.par, :, :], res[:, u.par, :, :], wide(k.row[:, R_MO, :]), ALU.add)\
                        .then_inc(res_bias.sem, 1)
                if active(t, 0, UNITS):
                    ln_rstd(pool, k, mv_a, ve_a, rstd_a, mv_a_done, eps_a_done, rstd_a_done, t)
                if active(t, 2, UNITS):
                    ln_rstd(pool, k, mv_c, ve_c, rstd_c, mv_c_done, eps_c_done, rstd_c_done, u)
                    pool.wait_ge(res_n_done.sem, res_n_done.done(u))
                    pool.tensor_tensor(res_g[:, :, :], res_n[:, :, :], wide(k.row[:, R_G1, :]), ALU.mult)\
                        .then_inc(res_g_done.sem, 1)
                    pool.wait_ge(res_g_done.sem, res_g_done.done(u))
                    if u.past(2):
                        pool.wait_ge(y_turned.sem, y_turned.done(u - 2))
                        pool.wait_ge(y_kept[u.par].sem, (u - 2).pair * 16 + 16)
                    pool.tensor_tensor(y[:, u.par, :, :], res_g[:, :, :], wide(k.row[:, R_BE1, :]), ALU.add)\
                        .then_inc(y_ready.sem, 1)
                if active(t, 1, UNITS):
                    u = t - 1
                    for j in range(QT):
                        pool.wait_ge(sums_inv.sem, sums_inv.after(u, j))
                        p = probs[:, j % 2, :, :]
                        pool.tensor_tensor(p, p, rsums[:, j % 2, :].unsqueeze(2).broadcast_to([P, MH, P]), ALU.mult)\
                            .then_inc(normed.sem, 1)

            in_steps(pool, UNITS, DEPTH, step)

        @block.scalar
        def _(act):
            def step(t):
                if active(t, 3, UNITS):
                    u = t - 3
                    act.wait_ge(y_turned.sem, y_turned.done(u))
                    if u.past(1):
                        act.wait_ge(logits_ps.sem, logits_ps.done(u - 1))
                    act.copy(yT[:, :], ps[:, PT, :]).then_inc(yT_ready.sem, 1)
                if active(t, 0, UNITS):
                    act.wait_ge(x_turned.sem, x_turned.done(t))
                    if t.past(1):
                        act.wait_ge(v_proj.sem, v_proj.done(t - 1))
                    act.copy(xnT[:, :], ps[:, XV, :]).then_inc(xT_ready.sem, 1)
                    act.wait_ge(k_proj.sem, k_proj.done(t))
                    act.wait_ge(heads_zero.sem, 2)
                    for h in range(2):
                        rows = slice(MD * h, MD * (h + 1))
                        act.activation(k_heads[rows, t.par, :, h, :],
                                       ps[rows, K_, :].rearrange("p (j t) -> p j t", j=QT), ACT.Identity,
                                       bias=k.col[rows, C_MK:C_MK + 1]).then_inc(k_ready_act.sem, 1)
                if active(t, 1, UNITS):
                    u = t - 1
                    for j in range(QT + 1):
                        if j < QT:
                            act.wait_ge(maxed.sem, maxed.after(u, j))
                            if u.past(1) or j >= 2:
                                act.wait_ge(p_turned.sem, p_turned.after(u, j - 2))
                            for h in range(MH):
                                act.activation(probs[:, j % 2, h, :], ps[:, SC + j % 2, h * P:(h + 1) * P], ACT.Exp,
                                               bias=neg_max[:, j % 2, h:h + 1], accum_out=sums[:, j % 2, h:h + 1])\
                                   .then_inc(exped.sem, 1)
                        if j >= 1:
                            act.wait_ge(p_turned.sem, p_turned.after(u, j - 1))
                            if u.past(1) or j >= 3:
                                act.wait_ge(mixed.sem, mixed.after(u, j - 3))
                            act.copy(probsT[:, (j - 1) % 2, :, :], ps[:, PT, :]).then_inc(pT_ready.sem, 1)
                    act.wait_ge(mixed.sem, mixed.done(u))
                    if u.past(1):
                        act.wait_ge(projected.sem, projected.done(u - 1))
                    act.copy(mixedT[:, :], ps[:, MX, :]).then_inc(mixT_ready.sem, 1)

            in_steps(act, UNITS, DEPTH, step)

        @block.tensor
        def _(pe):
            def turn_y(u):
                pe.wait_ge(y_ready.sem, y_ready.done(u))
                after = u + 1 if active(u, -1, UNITS) else u
                pe.wait_ge(pT_ready.sem, pT_ready.done(after))
                if u.past(1):
                    pe.wait_ge(logits_done.sem, logits_done.done(u - 1))
                for j in range(QT):
                    mm = pe.transpose(ps[:, PT, j * P:(j + 1) * P], y[:, u.par, j, :], k.ident[:, :])
                mm.then_inc(y_turned.sem, 1)

            def logits(u):
                pe.wait_ge(yT_ready.sem, yT_ready.done(u))
                for j in range(QT):
                    mm = pe.matmul(ps[:, PT, j * E:(j + 1) * E], yT[:, j * P:(j + 1) * P], k.gateT[:, 0, :],
                                   start=True, stop=True)
                mm.then_inc(logits_ps.sem, 1)

            def project_out(u):
                pe.wait_ge(mixT_ready.sem, mixT_ready.done(u))
                if u.past(1):
                    pe.wait_ge(res_done.sem, res_done.done(u - 1))
                for j in range(QT):
                    mm = pe.matmul(ps[:, OUT, j * P:(j + 1) * P], mixedT[:, j * P:(j + 1) * P], k.wT[:, W_MO, :],
                                   start=True, stop=True)
                mm.then_inc(projected.sem, 1)

            def turn_x(u):
                pe.wait_ge(xn_done.sem, xn_done.done(u))
                if u.past(1):
                    pe.wait_ge(v_ready.sem, v_ready.done(u - 1))
                for j in range(QT):
                    mm = pe.transpose(ps[:, XV, j * P:(j + 1) * P], xn[:, u.par, j, :], k.ident[:, :])
                mm.then_inc(x_turned.sem, 1)

            def project_qkv(u):
                pe.wait_ge(xT_ready.sem, xT_ready.done(u))
                if u.past(1):
                    pe.wait_ge(q_ready.sem, q_ready.done(u - 1))
                    pe.wait_ge(k_ready_act.sem, k_ready_act.done(u - 1))
                    pe.wait_ge(k_ready_dve.sem, k_ready_dve.done(u - 1))
                pe.matmul(ps[:, K_, :], k.wT[:, W_MK, :], xnT[:, :], start=True, stop=True).then_inc(k_proj.sem, 1)
                pe.matmul(ps[:, Q, :], k.wT[:, W_MQ, :], xnT[:, :], start=True, stop=True).then_inc(q_proj.sem, 1)
                for j in range(QT):
                    mm = pe.matmul(ps[:, XV, j * P:(j + 1) * P], xnT[:, j * P:(j + 1) * P], k.wT[:, W_MV, :],
                                   start=True, stop=True)
                mm.then_inc(v_proj.sem, 1)

            def attend(u):
                pe.wait_ge(q_ready.sem, q_ready.done(u))
                pe.wait_ge(k_ready_act.sem, k_ready_act.done(u))
                pe.wait_ge(k_ready_dve.sem, k_ready_dve.done(u))
                pe.wait_ge(v_ready.sem, v_ready.done(u))
                for j in range(QT + 2):
                    if j < QT:
                        if u.past(1) or j >= 2:
                            pe.wait_ge(exped.sem, exped.after(u, MH * (j - 1) - 1))
                        pe.matmul(ps[:, SC + j % 2, :], qT[:, u.par, j * P:(j + 1) * P], k_heads[:, u.par, j, :, :],
                                  start=True, stop=False)
                        pe.matmul(ps[:, SC + j % 2, :], k.identb[:, :],
                                  k.batch_mask[:, :].unsqueeze(1).broadcast_to([P, MH, P]), start=False, stop=True)\
                          .then_inc(scored.sem, 1)
                    if 1 <= j <= QT:
                        i = j - 1
                        pe.wait_ge(normed.sem, normed.after(u, i))
                        if i >= 1:
                            pe.wait_ge(pT_ready.sem, pT_ready.after(u, i - 1))
                        elif u.past(1):
                            pe.wait_ge(pT_ready.sem, pT_ready.done(u - 1))
                            if u.past(2):
                                pe.wait_ge(logits_done.sem, logits_done.done(u - 2))
                        for h in range(MH):
                            mm = pe.transpose(ps[:, PT, h * P:(h + 1) * P], probs[:, i % 2, h, :], k.ident[:, :])
                        mm.then_inc(p_turned.sem, 1)
                    if j >= 2:
                        i = j - 2
                        pe.wait_ge(pT_ready.sem, pT_ready.after(u, i))
                        if i == 0 and (u.past(1)):
                            pe.wait_ge(mixT_ready.sem, mixT_ready.done(u - 1))
                        for h in range(MH):
                            mm = pe.matmul(ps[MD * h:MD * (h + 1), MX, i * P:(i + 1) * P],
                                           v[:, u.par, i, MD * h:MD * (h + 1)], probsT[:, i % 2, h, :],
                                           start=True, stop=True)
                        mm.then_inc(mixed.sem, 1)

            def step(t):
                if active(t, 3, UNITS):
                    turn_y(t - 3)
                if active(t, 2, UNITS):
                    project_out(t - 2)
                if active(t, 0, UNITS):
                    turn_x(t)
                if active(t, 3, UNITS):
                    logits(t - 3)
                if active(t, 0, UNITS):
                    project_qkv(t)
                if active(t, 1, UNITS):
                    attend(t - 1)

            in_steps(pe, UNITS, DEPTH, step)

        @block.vector
        def _(dve):
            def evacuate(u):
                dve.wait_ge(k_proj.sem, k_proj.done(u))
                for h in range(2, MH):
                    rows = slice(MD * h, MD * (h + 1))
                    dve.wait_ge(heads_zero.sem, 2)
                    dve.tensor_scalar(k_heads[rows, u.par, :, h, :], ps[rows, K_, :].rearrange("p (j t) -> p j t", j=QT),
                                      k.col[rows, C_MK:C_MK + 1], None, ALU.add).then_inc(k_ready_dve.sem, 1)
                dve.wait_ge(q_proj.sem, q_proj.done(u))
                dve.tensor_scalar(qT[:, u.par, :], ps[:, Q, :], k.col[:, C_MQ:C_MQ + 1], float(MD) ** -0.5,
                                  ALU.add, ALU.mult).then_inc(q_ready.sem, 1)
                dve.wait_ge(v_proj.sem, v_proj.done(u))
                if u.past(2):
                    dve.wait_ge(mixed.sem, mixed.done(u - 2))
                dve.tensor_tensor(v[:, u.par, :, :], ps[:, XV, :].rearrange("p (j d) -> p j d", j=QT),
                                  wide(k.row[:, R_MV, :]), ALU.add).then_inc(v_ready.sem, 1)

            def softmax(u):
                for j in range(QT + 1):
                    if j < QT:
                        dve.wait_ge(scored.sem, scored.after(u, j))
                        dve.tensor_reduce(neg_max[:, j % 2, :], ps[:, SC + j % 2, :].rearrange("p (h t) -> p h t", h=MH),
                                          X_AXIS, ALU.max, negate=True).then_inc(maxed.sem, 1)
                    if j >= 1:
                        i = j - 1
                        dve.wait_ge(exped.sem, exped.after(u, MH * j - 1))
                        dve.reciprocal(rsums[:, i % 2, :], sums[:, i % 2, :]).then_inc(sums_inv.sem, 1)

            def step(t):
                if active(t, 2, UNITS):
                    u = t - 2
                    dve.wait_ge(projected.sem, projected.done(u))
                    dve.tensor_tensor(res[:, u.par, :, :], ps[:, OUT, :].rearrange("p (j d) -> p j d", j=QT),
                                      xn[:, u.par, :, :], ALU.add).then_inc(res_done.sem, 1)
                if active(t, 0, UNITS):
                    dve.wait_ge(x_in[t.par].sem, (t.pair + 1) * (16 * B))
                    ln_stats(dve, x_tile[:, t.par, :, :], stats_a, mv_a, stats_a_done, mv_a_done, t)
                if active(t, 2, UNITS):
                    dve.wait_ge(res_bias.sem, res_bias.done(u))
                    ln_stats(dve, res[:, u.par, :, :], stats_c, mv_c, stats_c_done, mv_c_done, u)
                if active(t, 0, UNITS):
                    ln_apply(dve, xn[:, t.par, :, :], x_tile[:, t.par, :, :], mv_a, rstd_a, rstd_a_done, xn_done, t)
                if active(t, 2, UNITS):
                    if u.past(1):
                        dve.wait_ge(res_g_done.sem, res_g_done.done(u - 1))
                    ln_apply(dve, res_n, res[:, u.par, :, :], mv_c, rstd_c, rstd_c_done, res_n_done, u)
                if active(t, 3, UNITS):
                    dve.wait_ge(logits_ps.sem, logits_ps.done(t - 3))
                    dve.tensor_copy(k.logits[:, bass.ds((t - 3).n * QT, QT), :],
                                    ps[:, PT, 0:QT * E].rearrange("p (j e) -> p j e", j=QT))\
                       .then_inc(logits_done.sem, 1)
                if active(t, 0, UNITS):
                    evacuate(t)
                if active(t, 1, UNITS):
                    softmax(t - 1)

            in_steps(dve, UNITS, DEPTH, step)




def prepare(nc, k, layer):
    COMP = 2 - layer
    x_in_dram = (k.x_flat, k.z)[layer]
    stacks = ((k.q_stack, k.k_stack), (k.q_stack1, k.k_stack1))[layer]
    w_q, w_k, w_v = ((W_QA, W_KA, W_V0), (W_Q1, W_K1, W_V1))[layer]
    SPLIT = 3 if layer == 0 else 1
    DEPTH = SPLIT + 1
    FIRST = 6 if layer == 0 else 4
    with ExitStack() as ctx:
        sb, banks, signal = phase_resources(nc, ctx, f"prepare{layer}")
        x_tile = sb("x_tile", [P, 2, QT, D])
        xn = sb("xn", [P, 2, QT, D])
        xnT = sb("xnT", [P, QT * P])
        stats, mv = sb("stats", [P, QT, 7]), sb("mv", [P, QT, 2])
        var_eps, rstd = sb("var_eps", [P, QT]), sb("rstd", [P, QT])
        vals = sb("vals", [P, 2, COMP, S])
        rest = sb("rest", [P, 2, COMP, S])
        parts = sb("parts", [P, 2, 2, 3, COMP, S], BF16)
        if layer == 0:
            turn = sb("turn", [P, 2, S])
            turn_abs = sb("turn_abs", [P, 2, S])
            sine, cosine = sb("sine", [P, 2, 2, S]), sb("cosine", [P, 2, 2, S])
            mag, logs = sb("mag", [P, 2, S]), sb("logs", [P, 2, S])
            amp, square = sb("amp", [P, 2, 2, S]), sb("square", [P, 2, S])
            inv, amp_n = sb("inv", [P, 2, S]), sb("amp_n", [P, 2, S])
        ps = banks("prep_ps", 8)
        XV, AMP, PHI, MS, LOG = 0, 1, 3, 5, 7

        x_in = [signal(f"x_in{i}", by=16) for i in range(2)]
        stats_done, mv_done, eps_done, rstd_done = signal("stats_done", QT), signal("mv_done", QT), signal("eps_done"), signal("rstd_done")
        xn_done = signal("xn_done", QT)
        x_turned, xT_ready = signal("x_turned"), signal("xT_ready")
        projected, v_proj, v_ready = signal("projected"), signal("v_proj"), signal("v_ready")
        phases_ps, tanh_done, sine_done, turn_abs_done, cosine_done = (signal(x) for x in ("phases_ps", "tanh_done", "sine_done", "turn_abs_done", "cosine_done"))
        mag_done, exp_done, log_done, amp_done, square_done = (signal(x) for x in ("mag_done", "exp_done", "log_done", "amp_done", "square_done"))
        mean_ps, mean_log, inv_done, amp_n_done = signal("mean_ps"), signal("mean_log"), signal("inv_done"), signal("amp_n_done", 2)
        vals_done, high_done, rest_done, mid_done, low_done = signal("vals_done", 2 if layer == 0 else 1), signal("high_done"), signal("rest_done"), signal("mid_done"), signal("low_done")
        stacked = [signal(f"stacked{i}", 2 * SLOTS, 16) for i in range(2)]
        logits_ps, logits_done = signal("logits_ps"), signal("logits_done")
        xn_kept = [signal(f"xn_kept{i}", by=16) for i in range(2)]
        q_vals_done, summed = signal("q_vals_done"), signal("summed")
        sum_kept = [signal(f"sum_kept{i}", by=16) for i in range(2)]
        block = ctx.enter_context(nc.Block())

        @block.sync
        def _(sp):
            def load(u):
                if u.past(2):
                    sp.wait_ge(xn_done.sem, xn_done.done(u - 2))
                    if layer == 1:
                        sp.wait_ge(sum_kept[u.par].sem, u.pair * 16)
                sp.dma_start(x_tile[:, u.par, :, :], x_in_dram[bass.ds(u.n, 1), :, :].rearrange("b (j p) d -> p (b j) d", p=P))\
                  .then_inc(x_in[u.par].sem, 16)

            def store(u):
                for side, which in enumerate((Q_PARTS, K_PARTS)):
                    for slot in sorted(range(SLOTS), key=lambda s: which[s]):
                        done = (high_done, mid_done, low_done)[which[slot]]
                        sp.wait_ge(done.sem, done.done(u))
                        rows = stacks[side][bass.ds(u.n, 1), :, slot * COMP * HD:(slot + 1) * COMP * HD, :]
                        sp.dma_start(rows.rearrange("b h (d c) t -> (b h) d (c t)", d=HD), parts[:, u.par, side, which[slot], :, :].rearrange("p c t -> p (c t)"))\
                          .then_inc(stacked[u.par].sem, 16)

            def step(t):
                if active(t, 0, B):
                    load(t)
                if layer == 1 and active(t, 1, B):
                    u = t - 1
                    sp.wait_ge(xn_done.sem, xn_done.done(u))
                    sp.dma_start(k.x_sum[:, bass.ds(u.n * QT, QT), :], x_tile[:, u.par, :, :])\
                      .then_inc(sum_kept[u.par].sem, 16)
                    sp.dma_start(k.y[:, bass.ds(u.n * QT, QT), :], xn[:, u.par, :, :]).then_inc(xn_kept[u.par].sem, 16)
                if active(t, DEPTH, B):
                    store(t - DEPTH)

            in_steps(sp, B, DEPTH + 1, step, 2, FIRST)
            for i in range(2):
                sp.wait_ge(stacked[i].sem, stacked[i].done(B // 2 - 1))
                if layer == 1:
                    sp.wait_ge(xn_kept[i].sem, 16 * B // 2)
                    sp.wait_ge(sum_kept[i].sem, 16 * B // 2)

        @block.gpsimd
        def _(pool):
            def step(t):
                if active(t, 0, B):
                    ln_rstd(pool, k, mv, var_eps, rstd, mv_done, eps_done, rstd_done, t)
                if layer == 0 and active(t, 3, B):
                    u = t - 3
                    pool.wait_ge(amp_n_done.sem, amp_n_done.done(u))
                    if u.past(1):
                        pool.wait_ge(rest_done.sem, rest_done.done(u - 1))
                    pool.tensor_tensor(vals[:, :, 0, :], amp_n[:, :, :], cosine[:, u.par, :, :], ALU.mult).then_inc(vals_done.sem, 1)
                    pool.tensor_tensor(vals[:, :, 1, :], amp_n[:, :, :], sine[:, u.par, :, :], ALU.mult).then_inc(vals_done.sem, 1)
                if layer == 0 and active(t, 1, B):
                    u = t - 1
                    pool.wait_ge(amp_done.sem, amp_done.done(u))
                    if u.past(1):
                        pool.wait_ge(mean_ps.sem, mean_ps.done(u - 1))
                    pool.tensor_tensor(square[:, :, :], amp[:, u.par, :, :], amp[:, u.par, :, :], ALU.mult)\
                        .then_inc(square_done.sem, 1)

            in_steps(pool, B, DEPTH, step, 2, FIRST)

        @block.scalar
        def _(act):
            def inverse(u):
                act.activation(inv[:, :, :], inv[:, :, :], ACT.Exp, scale=-0.5).then_inc(inv_done.sem, 1)

            def tanh_and_exp(u):
                act.wait_ge(phases_ps.sem, phases_ps.done(u))
                if u.past(1):
                    act.wait_ge(sine_done.sem, sine_done.done(u - 1))
                    act.wait_ge(turn_abs_done.sem, turn_abs_done.done(u - 1))
                act.activation(turn[:, :, :], ps[:, PHI:PHI + 2, :], ACT.Tanh).then_inc(tanh_done.sem, 1)
                act.wait_ge(projected.sem, projected.done(u))
                if u.past(1):
                    act.wait_ge(log_done.sem, log_done.done(u - 1))
                act.activation(mag[:, :, :], ps[:, AMP:AMP + 2, :], ACT.Abs).then_inc(mag_done.sem, 1)
                act.wait_ge(mag_done.sem, mag_done.done(u))
                act.activation(mag[:, :, :], mag[:, :, :], ACT.Exp, scale=-1.0).then_inc(exp_done.sem, 1)

            def sine_and_cosine(u):
                act.wait_ge(tanh_done.sem, tanh_done.done(u))
                if u.past(2):
                    act.wait_ge(vals_done.sem, vals_done.done(u - 2))
                act.activation(sine[:, u.par, :, :], turn[:, :, :], ACT.Sin, scale=PI).then_inc(sine_done.sem, 1)
                act.wait_ge(turn_abs_done.sem, turn_abs_done.done(u))
                act.activation(cosine[:, u.par, :, :], turn_abs[:, :, :], ACT.Sin, bias=k.col[:, C_PIH:C_PIH + 1], scale=-PI)\
                   .then_inc(cosine_done.sem, 1)

            def log_amplitude(u):
                act.wait_ge(exp_done.sem, exp_done.done(u))
                if u.past(1):
                    act.wait_ge(amp_done.sem, amp_done.done(u - 1))
                act.activation(logs[:, :, :], mag[:, :, :], ACT.Ln, bias=1.0).then_inc(log_done.sem, 1)

            def log_mean(u):
                act.wait_ge(mean_ps.sem, mean_ps.done(u))
                if u.past(1):
                    act.wait_ge(amp_n_done.sem, amp_n_done.done(u - 1))
                act.activation(inv[:, :, :], ps[:, MS:MS + 2, :], ACT.Ln, bias=k.col[:, C_EPS:C_EPS + 1])\
                   .then_inc(mean_log.sem, 1)

            def copy_turned(t):
                act.wait_ge(x_turned.sem, x_turned.done(t))
                if t.past(1):
                    act.wait_ge(v_proj.sem, v_proj.done(t - 1))
                    if layer == 1:
                        act.wait_ge(logits_ps.sem, logits_ps.done(t - 1))
                act.copy(xnT[:, :], ps[:, XV, :]).then_inc(xT_ready.sem, 1)

            def step(t):
                if layer == 1:
                    if active(t, 0, B):
                        copy_turned(t)
                    if active(t, 1, B):
                        u = t - 1
                        act.wait_ge(projected.sem, projected.done(u))
                        if u.past(1):
                            act.wait_ge(rest_done.sem, rest_done.done(u - 1))
                        act.activation(vals[:, 1, 0, :], ps[:, AMP + 1, :], ACT.Identity, bias=k.col[:, C_K1:C_K1 + 1])\
                           .then_inc(vals_done.sem, 1)
                    return
                if active(t, 3, B):
                    act.wait_ge(mean_log.sem, mean_log.done(t - 3))
                    inverse(t - 3)
                if active(t, 1, B):
                    tanh_and_exp(t - 1)
                if active(t, 0, B):
                    copy_turned(t)
                if active(t, 1, B):
                    sine_and_cosine(t - 1)
                    log_amplitude(t - 1)
                if active(t, 2, B):
                    log_mean(t - 2)

            in_steps(act, B, DEPTH, step, 2, FIRST)

        @block.tensor
        def _(pe):
            def step(t):
                if active(t, 0, B):
                    pe.wait_ge(xn_done.sem, xn_done.done(t))
                    if t.past(1):
                        pe.wait_ge(v_ready.sem, v_ready.done(t - 1))
                    for j in range(QT):
                        mm = pe.transpose(ps[:, XV, j * P:(j + 1) * P], xn[:, t.par, j, :], k.ident[:, :])
                    mm.then_inc(x_turned.sem, 1)
                    pe.wait_ge(xT_ready.sem, xT_ready.done(t))
                    for j in range(QT):
                        mm = pe.matmul(ps[:, XV, j * P:(j + 1) * P], xnT[:, j * P:(j + 1) * P], k.wT[:, w_v, :],
                                       start=True, stop=True)
                    mm.then_inc(v_proj.sem, 1)
                    if layer == 0:
                        if t.past(1):
                            pe.wait_ge(tanh_done.sem, tanh_done.done(t - 1))
                        pe.matmul(ps[:, PHI, :], k.wT[:, W_QP, :], xnT[:, :], start=True, stop=True)
                        pe.matmul(ps[:, PHI + 1, :], k.wT[:, W_KP, :], xnT[:, :], start=True, stop=True)\
                          .then_inc(phases_ps.sem, 1)
                    else:
                        if t.past(1):
                            pe.wait_ge(logits_done.sem, logits_done.done(t - 1))
                        for j in range(QT):
                            mm = pe.matmul(ps[:, LOG, j * E:(j + 1) * E], xnT[:, j * P:(j + 1) * P], k.gateT[:, 1, :],
                                           start=True, stop=True)
                        mm.then_inc(logits_ps.sem, 1)
                if active(t, 0, B):
                    if t.past(1):
                        if layer == 0:
                            pe.wait_ge(amp_done.sem, amp_done.done(t - 1))
                        else:
                            pe.wait_ge(vals_done.sem, vals_done.done(t - 1))
                            pe.wait_ge(q_vals_done.sem, q_vals_done.done(t - 1))
                    pe.matmul(ps[:, AMP, :], k.wT[:, w_q, :], xnT[:, :], start=True, stop=True)
                    pe.matmul(ps[:, AMP + 1, :], k.wT[:, w_k, :], xnT[:, :], start=True, stop=True)\
                      .then_inc(projected.sem, 1)
                if active(t, 1, B) and layer == 0:
                    u = t - 1
                    pe.wait_ge(square_done.sem, square_done.done(u))
                    if u.past(1):
                        pe.wait_ge(mean_log.sem, mean_log.done(u - 1))
                    for side in range(2):
                        mm = pe.matmul(ps[:, MS + side, :], k.head_mean[:, :], square[:, side, :], start=True, stop=True)
                    mm.then_inc(mean_ps.sem, 1)

            in_steps(pe, B, DEPTH, step, 2, FIRST)

        @block.vector
        def _(dve):
            def absolute_turn(u):
                dve.wait_ge(tanh_done.sem, tanh_done.done(u))
                if u.past(1):
                    dve.wait_ge(cosine_done.sem, cosine_done.done(u - 1))
                dve.scalar_tensor_tensor(out=turn_abs[:, :, :], in0=turn[:, :, :], scalar=-1.0, in1=turn[:, :, :],
                                         op0=ALU.mult, op1=ALU.max).then_inc(turn_abs_done.sem, 1)

            def amplitude(u):
                dve.wait_ge(log_done.sem, log_done.done(u))
                dve.scalar_tensor_tensor(out=amp[:, u.par, :, :], in0=ps[:, AMP:AMP + 2, :], scalar=0.0, in1=logs[:, :, :],
                                         op0=ALU.max, op1=ALU.add).then_inc(amp_done.sem, 1)

            def normalise(u):
                dve.wait_ge(inv_done.sem, inv_done.done(u))
                if u.past(1):
                    dve.wait_ge(vals_done.sem, vals_done.done(u - 1))
                dve.scalar_tensor_tensor(out=amp_n[:, 0, :], in0=amp[:, u.par, 0, :], scalar=k.hscale[:, :], in1=inv[:, 0, :],
                                         op0=ALU.mult, op1=ALU.mult).then_inc(amp_n_done.sem, 1)
                dve.tensor_tensor(amp_n[:, 1, :], amp[:, u.par, 1, :], inv[:, 1, :], ALU.mult).then_inc(amp_n_done.sem, 1)

            def split(u):
                def flat(which):
                    return parts[:, u.par, :, which, :, :].rearrange("p s c t -> p s (c t)")

                value = vals[:, :, :, :].rearrange("p s c t -> p s (c t)")
                left = rest[:, :, :, :].rearrange("p s c t -> p s (c t)")
                dve.wait_ge(vals_done.sem, vals_done.done(u))
                if layer == 1:
                    dve.wait_ge(q_vals_done.sem, q_vals_done.done(u))
                if u.past(2):
                    dve.wait_ge(stacked[u.par].sem, stacked[u.par].done((u - 2).pair))
                dve.tensor_copy(flat(0), value).then_inc(high_done.sem, 1)
                dve.wait_ge(high_done.sem, high_done.done(u))
                dve.tensor_tensor(left, value, flat(0), ALU.subtract).then_inc(rest_done.sem, 1)
                dve.wait_ge(rest_done.sem, rest_done.done(u))
                dve.tensor_copy(flat(1), left).then_inc(mid_done.sem, 1)
                dve.wait_ge(mid_done.sem, mid_done.done(u))
                dve.tensor_tensor(flat(2), left, flat(1), ALU.subtract).then_inc(low_done.sem, 1)

            def step(t):
                if layer == 0 and active(t, 3, B):
                    normalise(t - 3)
                if active(t, 0, B):
                    dve.wait_ge(x_in[t.par].sem, (t.pair + 1) * 16)
                    if layer == 1:
                        here = bass.ds(t.n * QT, QT)
                        dve.tensor_tensor(x_tile[:, t.par, :, :], x_tile[:, t.par, :, :], k.x_sum[:, here, :], ALU.add)\
                           .then_inc(summed.sem, 1)
                        dve.wait_ge(summed.sem, summed.done(t))
                    ln_stats(dve, x_tile[:, t.par, :, :], stats, mv, stats_done, mv_done, t)
                    if layer == 1 and t.past(2):
                        dve.wait_ge(xn_kept[t.par].sem, t.pair * 16)
                    ln_apply(dve, xn[:, t.par, :, :], x_tile[:, t.par, :, :], mv, rstd, rstd_done, xn_done, t)
                if active(t, 1, B):
                    if layer == 0:
                        absolute_turn(t - 1)
                    else:
                        dve.wait_ge(projected.sem, projected.done(t - 1))
                        dve.tensor_scalar(vals[:, 0, 0, :], ps[:, AMP, :], k.col[:, C_Q1:C_Q1 + 1], float(HD) ** -0.5,
                                          ALU.add, ALU.mult).then_inc(q_vals_done.sem, 1)
                if active(t, 0, B):
                    dve.wait_ge(v_proj.sem, v_proj.done(t))
                    v_out = k.v_all[:, bass.ds(t.n, 1), :, :].rearrange("p b j d -> p (b j) d")
                    v_ps = ps[:, XV, :].rearrange("p (j d) -> p j d", j=QT)
                    if layer == 0:
                        dve.tensor_copy(v_out, v_ps).then_inc(v_ready.sem, 1)
                    else:
                        dve.tensor_tensor(v_out, v_ps, wide(k.row[:, R_V1, :]), ALU.add).then_inc(v_ready.sem, 1)
                        dve.wait_ge(logits_ps.sem, logits_ps.done(t))
                        dve.tensor_copy(k.logits[:, bass.ds(t.n * QT, QT), :],
                                        ps[:, LOG, 0:QT * E].rearrange("p (j e) -> p j e", j=QT))\
                           .then_inc(logits_done.sem, 1)
                if active(t, SPLIT, B):
                    split(t - SPLIT)
                if layer == 0 and active(t, 1, B):
                    amplitude(t - 1)

            in_steps(dve, B, DEPTH, step, 2, FIRST)


def prepare0(nc, k):
    prepare(nc, k, 0)


def prepare1(nc, k):
    prepare(nc, k, 1)




def route(nc, k, layer):
    COPIES = layer + 1
    W = COPIES * NT
    TL = TILES[layer]
    MOST = T // ROWS
    dst = (k.sorted0, k.sorted1)[layer]
    with ExitStack() as ctx:
        sb, banks, signal = phase_resources(nc, ctx, f"route{layer}")
        best = sb("best", [P, NT])
        ties = sb("ties", [P, NT, E])
        first = sb("first", [P, NT])
        left = sb("left", [P, NT, E])
        second = sb("second", [P, NT])
        onehot = sb("onehot", [P, W, E])
        weight = sb("weight", [P, E])
        counts = sb("counts", [P, E, W])
        keep = sb("keep", [P, E, W])
        prefix = sb("prefix", [P, E, W])
        total = sb("total", [P, E])
        filled = sb("filled", [P, E, MOST])
        tiles = sb("tiles", [P, E])
        tiles_to = sb("tiles_to", [P, E])
        start = sb("start", [P, E])
        offset = sb("offset", [P, E, W])
        row_of = sb("row_of", [P, W, E])
        row_f = sb("row_f", [P, W])
        passed = sb("passed", [P, TL, E])
        expert_f = sb("expert_f", [P, TL])
        probs = sb("probs", [P, NT, E])
        denom = sb("denom", [P, NT])
        share = sb("share", [P, COPIES, NT])
        scaled = sb("scaled", [P, 2, NT, D]) if layer == 1 else None
        ps = banks("route_ps", 2)
        exp_ready, dve_step = signal("exp_ready"), signal("dve_step")
        onehot_done, ranked, rows_ready = signal("onehot_done"), signal("ranked"), signal("rows_ready")
        scaled_done = signal("scaled_done")
        scattered = k.scattered[layer]
        minus_best, probs_exp = signal("minus_best"), signal("probs_exp")
        block = ctx.enter_context(nc.Block())

        def per_token(column):
            return column.unsqueeze(2).broadcast_to([P, NT, E])

        @block.tensor
        def _(pe):
            pe.wait_ge(onehot_done.sem, 1)
            flat = onehot[:, :, :].rearrange("p w e -> p (w e)")
            pe.matmul(ps[:, 0, 0:W * E], k.before[:, :], flat, start=True, stop=True)
            pe.matmul(ps[:, 1, 0:W * E], k.ones[:, :], flat, start=True, stop=True).then_inc(ranked.sem, 1)

        @block.scalar
        def _(act):
            if layer == 1:
                act.wait_ge(minus_best.sem, 1)
                act.activation(probs[:, :, :], probs[:, :, :], ACT.Exp).then_inc(probs_exp.sem, 1)

        @block.vector
        def _(dve):
            steps = [0]

            def then(instruction):
                steps[0] += 1
                instruction.then_inc(dve_step.sem, 1)
                dve.wait_ge(dve_step.sem, steps[0])

            def choose(logits, best_, hot):
                then(dve.tensor_reduce(best_, logits, X_AXIS, ALU.max))
                then(dve.tensor_tensor(ties[:, :, :], logits, per_token(best_), ALU.is_equal))
                then(dve.tensor_tensor(ties[:, :, :], ties[:, :, :], weight[:, :].unsqueeze(1).broadcast_to([P, NT, E]),
                                       ALU.mult))
                then(dve.tensor_reduce(first[:, :], ties[:, :, :], X_AXIS, ALU.max))
                return dve.tensor_tensor(hot, ties[:, :, :], per_token(first[:, :]), ALU.is_equal)

            then(dve.tensor_scalar(weight[:, :], k.counted[:, 0:E], -1.0, float(E), ALU.mult, ALU.add))
            if layer == 0:
                choose(k.logits[:, :, :], best[:, :], onehot[:, 0:NT, :]).then_inc(onehot_done.sem, 1)
                dve.wait_ge(onehot_done.sem, 1)
            else:
                then(choose(k.logits[:, :, :], best[:, :], onehot[:, 0:NT, :]))
                dve.tensor_tensor(probs[:, :, :], k.logits[:, :, :], per_token(best[:, :]), ALU.subtract)\
                   .then_inc(minus_best.sem, 1)
                then(dve.scalar_tensor_tensor(out=left[:, :, :], in0=onehot[:, 0:NT, :], scalar=NEG, in1=k.logits[:, :, :],
                                              op0=ALU.mult, op1=ALU.add))
                choose(left[:, :, :], second[:, :], onehot[:, NT:W, :]).then_inc(onehot_done.sem, 1)
                dve.wait_ge(probs_exp.sem, 1)
                dve.wait_ge(onehot_done.sem, 1)
                then(dve.tensor_reduce(denom[:, :], probs[:, :, :], X_AXIS, ALU.add))
                then(dve.reciprocal(denom[:, :], denom[:, :]))
                for c in range(2):
                    then(dve.tensor_tensor(ties[:, :, :], probs[:, :, :], onehot[:, c * NT:(c + 1) * NT, :], ALU.mult))
                    then(dve.tensor_reduce(share[:, c, :], ties[:, :, :], X_AXIS, ALU.add))
                    then(dve.tensor_tensor(share[:, c, :], share[:, c, :], denom[:, :], ALU.mult))
            then(dve.memset(keep[:, :, :], 1.0))
            then(dve.memset(keep[:, :, 0:1], 0.0))
            dve.wait_ge(ranked.sem, 1)
            then(dve.tensor_copy(counts[:, :, :], ps[:, 1, 0:W * E].rearrange("p (w e) -> p e w", e=E)))
            then(dve.tensor_tensor_scan(prefix[:, :, :].rearrange("p e w -> p (e w)"),
                                        keep[:, :, :].rearrange("p e w -> p (e w)"),
                                        counts[:, :, :].rearrange("p e w -> p (e w)"), 0.0, ALU.mult, ALU.add))
            then(dve.tensor_copy(total[:, :], prefix[:, :, W - 1]))
            then(dve.scalar_tensor_tensor(out=filled[:, :, :], in0=k.counted[:, 0:MOST].unsqueeze(1).broadcast_to([P, E, MOST]),
                                          scalar=float(ROWS), in1=total[:, :].unsqueeze(2).broadcast_to([P, E, MOST]),
                                          op0=ALU.mult, op1=ALU.is_lt))
            then(dve.tensor_reduce(tiles[:, :], filled[:, :, :], X_AXIS, ALU.add))
            then(dve.tensor_tensor_scan(tiles_to[:, :], k.ones[:, 0:E], tiles[:, :], 0.0, ALU.mult, ALU.add))
            then(dve.tensor_tensor(start[:, :], tiles_to[:, :], tiles[:, :], ALU.subtract))
            then(dve.tensor_tensor(offset[:, :, :], prefix[:, :, :], counts[:, :, :], ALU.subtract))
            then(dve.scalar_tensor_tensor(out=offset[:, :, :], in0=start[:, :].unsqueeze(2).broadcast_to([P, E, W]),
                                          scalar=float(ROWS), in1=offset[:, :, :], op0=ALU.mult, op1=ALU.add))
            then(dve.tensor_tensor(row_of[:, :, :], ps[:, 0, 0:W * E].rearrange("p (w e) -> p w e", e=E),
                                   offset[:, :, :].rearrange("p e w -> p w e"), ALU.add))
            then(dve.tensor_tensor(row_of[:, :, :], row_of[:, :, :], onehot[:, :, :], ALU.mult))
            then(dve.tensor_reduce(row_f[:, :], row_of[:, :, :], X_AXIS, ALU.add))
            dve.tensor_copy(k.rank_row[:, 0:W], row_f[:, :]).then_inc(rows_ready.sem, 1)
            if layer == 1:
                for c in range(2):
                    dve.tensor_tensor(scaled[:, c, :, :], k.y[:, :, :], share[:, c, :].unsqueeze(2).broadcast_to([P, NT, D]),
                                      ALU.mult).then_inc(scaled_done.sem, 1)
            then(dve.tensor_tensor(passed[:, :, :], tiles_to[:, :].unsqueeze(1).broadcast_to([P, TL, E]),
                                   k.counted[:, 0:TL].unsqueeze(2).broadcast_to([P, TL, E]), ALU.is_le))
            then(dve.tensor_reduce(expert_f[:, :], passed[:, :, :], X_AXIS, ALU.add))
            then(dve.tensor_scalar(expert_f[:, :], expert_f[:, :], float(E - 1), None, ALU.min))
            then(dve.tensor_copy(k.tile_expert[:, 0:TL], expert_f[:, :]))

        @block.gpsimd
        def _(pool):
            pool.wait_ge(rows_ready.sem, 1)
            for c in range(COPIES):
                if layer == 1:
                    pool.wait_ge(scaled_done.sem, c + 1)
                for t in range(NT):
                    n = c * NT + t
                    src = k.y[:, t, :] if layer == 0 else scaled[:, c, t, :]
                    if n >= 4:
                        pool.wait_ge(scattered[n % 4].sem, n // 4 * 16)
                    pool.indirect_dma_start(dst, bass.IndirectOffsetOnAxis(ap=k.rank_row[:, n:n + 1], axis=0), src, None)\
                        .then_inc(scattered[n % 4].sem, 16)
            for i in range(4):
                pool.wait_ge(scattered[i].sem, W // 4 * 16)


def route0(nc, k):
    route(nc, k, 0)


def route1(nc, k):
    route(nc, k, 1)




def experts(nc, k, layer):
    TL = TILES[layer]
    HC = DF // P if layer == 0 else 3
    size = [P] * HC if layer == 0 else [P, P, HID - 2 * P]
    src, dst = ((k.sorted0, k.done0), (k.sorted1, k.done1))[layer]
    LOADS = 5
    RING = 4
    with ExitStack() as ctx:
        sb, banks, signal = phase_resources(nc, ctx, f"experts{layer}")
        rows = sb("rows", [P, RING, 2, D])
        rowsT = sb("rowsT", [P, 2, ROWS])
        w_in = sb("w_in", [P, RING, DF if layer == 0 else 2 * HID])
        w_out = sb("w_out", [P, RING, HC, D])
        b_in = sb("b_in", [P, RING, HC])
        b_out = sb("b_out", [P, RING, D])
        hidden = sb("hidden", [P, 2, HC, ROWS])
        gate = sb("gate", [P, HC, ROWS])
        result = sb("result", [P, RING, 2, D])
        ps = banks("experts_ps", 8)
        TURN, OUT = 0, 7

        def hidden_bank(u, n):
            return 1 + 3 * u.par + n

        loaded = [signal(f"loaded{i}", LOADS, 16) for i in range(RING)]
        turned, rowsT_ready, hidden_ps, out_ps, result_done = (signal(x) for x in ("turned", "rowsT_ready", "hidden_ps", "out_ps", "result_done"))
        hidden_act, hidden_dve = signal("hidden_act", 2), signal("hidden_dve", 2)
        stored = [signal(f"stored{i}", by=16) for i in range(RING)]
        DEPTH = 3
        block = ctx.enter_context(nc.Block())

        @block.sync
        def _(sp):
            def load(u):
                if u.past(RING):
                    sp.wait_ge(out_ps.sem, out_ps.done(u - RING))
                    if layer == 0:
                        sp.wait_ge(result_done.sem, result_done.done(u - RING))
                e = sp.value_load(k.tile_expert[0:1, bass.ds(u.n, 1)], min_val=0, max_val=E - 1)
                done = loaded[u.phase].sem
                sp.dma_start(rows[:, u.phase, :, :], src[bass.ds(u.n * ROWS, ROWS), :].rearrange("(a p) d -> p a d", p=P))\
                  .then_inc(done, 16)
                one = bass.ds(e, 1)
                if layer == 0:
                    sp.dma_start(w_in[:, u.phase, :], k.arg["L0_ffn_W1"][one, :, :].rearrange("e d f -> (e d) f")).then_inc(done, 16)
                    sp.dma_start(b_in[:, u.phase, :], k.arg["L0_ffn_b1"][one, :].rearrange("e (p c) -> (e p) c", p=P))\
                      .then_inc(done, 16)
                    sp.dma_start(w_out[:, u.phase, :, :], k.arg["L0_ffn_W2"][one, :, :].rearrange("e (p c) d -> (e p) c d", p=P))\
                      .then_inc(done, 16)
                    sp.dma_start(b_out[:, u.phase, :], k.arg["L0_ffn_b2"][one, :].rearrange("e d -> (e d)").rearrange("(o d) -> o d", o=1)
                                 .partition_broadcast(P)).then_inc(done, 16)
                else:
                    sp.dma_start(w_in[:, u.phase, 0:HID], k.arg["L1_ffn_w1"][one, :, :].rearrange("e d f -> (e d) f")).then_inc(done, 16)
                    sp.dma_start(w_in[:, u.phase, HID:2 * HID], k.arg["L1_ffn_w3"][one, :, :].rearrange("e d f -> (e d) f"))\
                      .then_inc(done, 16)
                    sp.dma_start(w_out[:, u.phase, 0:2, :], k.arg["L1_ffn_w2"][one, 0:2 * P, :].rearrange("e (c p) d -> p (e c) d", p=P))\
                      .then_inc(done, 16)
                    sp.dma_start(w_out[0:size[2], u.phase, 2, :], k.arg["L1_ffn_w2"][one, 2 * P:HID, :].rearrange("e f d -> (e f) d"))\
                      .then_inc(done, 16)

            def store(u):
                sp.wait_ge(result_done.sem, result_done.done(u))
                sp.dma_start(dst[bass.ds(u.n * ROWS, ROWS), :].rearrange("(a p) d -> p a d", p=P), result[:, u.phase, :, :])\
                  .then_inc(stored[u.phase].sem, 16)

            def step(t):
                if active(t, 0, TL):
                    load(t)
                if active(t, 5, TL):
                    store(t - 5)

            in_steps(sp, TL, 6, step, RING, 2 * RING)
            for i in range(RING):
                sp.wait_ge(stored[i].sem, (TL + RING - 1 - i) // RING * 16)

        @block.scalar
        def _(act):
            def step(t):
                if active(t, 1, TL):
                    u = t - 1
                    act.wait_ge(hidden_ps.sem, hidden_ps.done(u))
                    if layer == 0:
                        if u.past(2):
                            act.wait_ge(out_ps.sem, out_ps.done(u - 2))
                        for c in range(2):
                            act.activation(hidden[:, u.par, c, :], ps[:, hidden_bank(u, 0), c * ROWS:(c + 1) * ROWS], ACT.Relu,
                                           bias=b_in[:, u.phase, c:c + 1]).then_inc(hidden_act.sem, 1)
                    else:
                        if u.past(1):
                            act.wait_ge(hidden_dve.sem, hidden_dve.done(u - 1))
                        act.activation(gate[:, 0:2, :], ps[:, hidden_bank(u, 0), :].rearrange("p (c r) -> p c r", c=2), ACT.Silu)\
                           .then_inc(hidden_act.sem, 1)
                        act.activation(gate[0:size[2], 2, :], ps[0:size[2], hidden_bank(u, 2), 0:ROWS], ACT.Silu)\
                           .then_inc(hidden_act.sem, 1)
                if active(t, 0, TL):
                    act.wait_ge(turned.sem, turned.done(t))
                    if t.past(2):
                        act.wait_ge(hidden_ps.sem, hidden_ps.done(t - 2))
                    act.copy(rowsT[:, t.par, :], ps[:, TURN, 0:ROWS]).then_inc(rowsT_ready.sem, 1)

            in_steps(act, TL, DEPTH, step, RING, 2 * RING)

        @block.vector
        def _(dve):
            def step(t):
                if active(t, 1, TL):
                    u = t - 1
                    dve.wait_ge(hidden_ps.sem, hidden_ps.done(u))
                    if u.past(2):
                        dve.wait_ge(out_ps.sem, out_ps.done(u - 2))
                    if layer == 0:
                        for c in range(2, 4):
                            dve.tensor_scalar(hidden[:, u.par, c, :], ps[:, hidden_bank(u, 1), (c - 2) * ROWS:(c - 1) * ROWS],
                                              b_in[:, u.phase, c:c + 1], 0.0, ALU.add, ALU.max).then_inc(hidden_dve.sem, 1)
                    else:
                        dve.wait_ge(hidden_act.sem, hidden_act.after(u, 0))
                        dve.tensor_tensor(hidden[:, u.par, 0:2, :], ps[:, hidden_bank(u, 1), :].rearrange("p (c r) -> p c r", c=2),
                                          gate[:, 0:2, :], ALU.mult).then_inc(hidden_dve.sem, 1)
                        dve.wait_ge(hidden_act.sem, hidden_act.after(u, 1))
                        dve.tensor_tensor(hidden[0:size[2], u.par, 2, :], ps[0:size[2], hidden_bank(u, 2), ROWS:2 * ROWS],
                                          gate[0:size[2], 2, :], ALU.mult).then_inc(hidden_dve.sem, 1)
                if active(t, 2, TL):
                    u = t - 2
                    dve.wait_ge(out_ps.sem, out_ps.done(u))
                    if u.past(RING):
                        dve.wait_ge(stored[u.phase].sem, u.turn * 16)
                    out = ps[:, OUT, 0:2 * D].rearrange("p (a d) -> p a d", a=2)
                    if layer == 0:
                        dve.tensor_tensor(result[:, u.phase, :, :], out, b_out[:, u.phase, :].unsqueeze(1).broadcast_to([P, 2, D]),
                                          ALU.add).then_inc(result_done.sem, 1)
                    else:
                        dve.tensor_copy(result[:, u.phase, :, :], out).then_inc(result_done.sem, 1)

            in_steps(dve, TL, DEPTH, step, RING, 2 * RING)

        @block.tensor
        def _(pe):
            def turn(u):
                pe.wait_ge(loaded[u.phase].sem, (u.turn + 1) * (LOADS * 16))
                if u.past(1):
                    pe.wait_ge(rowsT_ready.sem, rowsT_ready.done(u - 1))
                for a in range(2):
                    mm = pe.transpose(ps[:, TURN, a * P:(a + 1) * P], rows[:, u.phase, a, :], k.ident[:, :])
                mm.then_inc(turned.sem, 1)

            def into_hidden(u):
                pe.wait_ge(rowsT_ready.sem, rowsT_ready.done(u))
                if u.past(2):
                    pe.wait_ge(hidden_act.sem, hidden_act.done(u - 2))
                    pe.wait_ge(hidden_dve.sem, hidden_dve.done(u - 2))
                if layer == 0:
                    for c in range(HC):
                        mm = pe.matmul(ps[:, hidden_bank(u, c // 2), c % 2 * ROWS:(c % 2 + 1) * ROWS],
                                       w_in[:, u.phase, c:DF:HC], rowsT[:, u.par, :], start=True, stop=True)
                else:
                    for side, w in enumerate((0, HID)):
                        for c in range(HC):
                            bank, half = (side, c) if c < 2 else (2, side)
                            mm = pe.matmul(ps[0:size[c], hidden_bank(u, bank), half * ROWS:(half + 1) * ROWS],
                                           w_in[:, u.phase, w + c * P:w + c * P + size[c]], rowsT[:, u.par, :],
                                           start=True, stop=True)
                mm.then_inc(hidden_ps.sem, 1)

            def out_of_hidden(u):
                pe.wait_ge(hidden_act.sem, hidden_act.done(u))
                pe.wait_ge(hidden_dve.sem, hidden_dve.done(u))
                if u.past(1):
                    pe.wait_ge(result_done.sem, result_done.done(u - 1))
                for a in range(2):
                    for c in range(HC):
                        mm = pe.matmul(ps[:, OUT, a * D:(a + 1) * D], hidden[0:size[c], u.par, c, a * P:(a + 1) * P],
                                       w_out[0:size[c], u.phase, c, :], start=(c == 0), stop=(c == HC - 1))
                mm.then_inc(out_ps.sem, 1)

            def step(t):
                if active(t, 1, TL):
                    into_hidden(t - 1)
                if active(t, 0, TL):
                    turn(t)
                if active(t, 2, TL):
                    out_of_hidden(t - 2)

            in_steps(pe, TL, DEPTH, step, RING, 2 * RING)


def experts0(nc, k):
    experts(nc, k, 0)


def experts1(nc, k):
    experts(nc, k, 1)




def attend(nc, k, layer):
    ROWS_S = (K0, K1)[layer]
    ROWS_K = K0
    ROWS_A = ROWS_K + 3
    UNITS = B * NG
    RING = 4
    MCH, SCH = 10, 5
    stacks = ((k.q_stack, k.k_stack), (k.q_stack1, k.k_stack1))[layer]
    w_o = (W_O0, W_O1)[layer]
    with ExitStack() as ctx:
        sb, banks, signal = phase_resources(nc, ctx, f"attend{layer}")
        q = sb("q", [P, RING, GH, S], BF16)
        ks = sb("ks", [P, RING, GH, S], BF16)
        moe = sb("moe", [P, (layer + 1) * NT, D])
        neg_max = sb("neg_max", [P, 2, GH, QT])
        rest = sb("rest", [P, GH * QT])
        max_parts = sb("max_parts", [P, 2, 3, GH * QT], BF16)
        maxT = sb("maxT", [3 * GH * QT, 2, P], BF16)
        probs = sb("probs", [P, 2, 2 * SCH, S])
        vals = sb("vals", [P, 2, QT * GH, 32])
        mixT = sb("mixT", [P, S])
        inv = sb("inv", [P, QT * GH])
        context = sb("context", [P, 2, QT, D])
        contextT = sb("contextT", [P, S])
        x_tile = sb("x_tile", [P, 2, QT, D]) if layer == 0 else None
        ps = banks("attend_ps", 8)
        MAXB, PROB, MIX, TURN = 0, 2, 6, 7

        loaded = [signal(f"loaded{i}", 2, 16) for i in range(RING)]
        preset, filled = signal("preset"), signal("filled")
        vals_ready = signal("vals_ready")
        scored, maxed = signal("scored", MCH), signal("maxed", MCH)
        high_done, rest_done, mid_done, parts_done = (signal(x) for x in ("high_done", "rest_done", "mid_done", "parts_done"))
        max_turned, maxT_ready = signal("max_turned"), signal("maxT_ready")
        max_in = [signal(f"max_in{i}", by=16) for i in range(2)]
        prob_ps, exped = signal("prob_ps", SCH), signal("exped", SCH)
        mixed, mixT_ready, mix_turned, inv_done, context_done = (signal(x) for x in ("mixed", "mixT_ready", "mix_turned", "inv_done", "context_done"))
        context_turned, contextT_ready, projected, added = (signal(x) for x in ("context_turned", "contextT_ready", "projected", "added"))
        x_in = [signal(f"x_in{i}", by=16) for i in range(2)]
        biased, first_added, summed = signal("biased"), signal("first_added"), signal("summed")
        if layer == 0:
            z_sum, z_norm, z_gain = sb("z_sum", [P, QT, D]), sb("z_norm", [P, QT, D]), sb("z_gain", [P, QT, D])
            z_tile = sb("z_tile", [P, QT, D])
            z_stats, z_mv, z_ve, z_rstd = sb("z_stats", [P, QT, 7]), sb("z_mv", [P, QT, 2]), sb("z_ve", [P, QT]), sb("z_rstd", [P, QT])
            z_summed, z_stats_done, z_mv_done, z_eps_done = signal("z_summed"), signal("z_stats_done", QT), signal("z_mv_done", QT), signal("z_eps_done")
            z_rstd_done, z_normed, z_scaled, z_ready = signal("z_rstd_done"), signal("z_normed", QT), signal("z_scaled"), signal("z_ready")
            z_stored = signal("z_stored", B, 16)
        gathered = k.gathered[layer]
        stored = [signal(f"stored{i}", by=16) for i in range(2)]
        DEPTH = 6
        block = ctx.enter_context(nc.Block())

        def max_chunk(c):
            pair, kind = divmod(c, 5)
            h = 2 * pair + kind // 2
            if kind == 4:
                return [(2 * pair, 1, 0), (2 * pair + 1, 1, 256)]
            return [(h, 3, 0)] if kind % 2 == 0 else [(h, 2, 0), (h, 0, 384)]

        def prob_bank(n):
            pair, kind = divmod(n, 5)
            h = 2 * pair + kind // 2
            if kind == 4:
                return [(2 * pair, 2, 0), (2 * pair + 1, 2, 256)]
            return [(h, 0, 0)] if kind % 2 == 0 else [(h, 1, 0), (h, 3, 384)]

        prob_place = {(h, kt): (n, col) for n in range(2 * SCH) for h, kt, col in prob_bank(n)}

        @block.sync
        def _(sp):
            def step(t):
                if active(t, 0, UNITS):
                    if t.past(RING):
                        sp.wait_ge(prob_ps.sem, prob_ps.done(t - RING))
                    else:
                        sp.wait_ge(filled.sem, t.n + 1)
                    for side, dst in enumerate((q, ks)):
                        src = stacks[side][bass.ds(t.row, 1), t.group * GH:(t.group + 1) * GH, :, :]
                        sp.dma_start(dst[0:ROWS_S, t.group, :, :], src.rearrange("b h r t -> r (b h) t"))\
                          .then_inc(loaded[t.group].sem, 16)
                    if t.group == 2 and layer == 0:
                        if t.past(2 * NG):
                            sp.wait_ge(added.sem, added.done(t.row - 2))
                        sp.dma_start(x_tile[:, t.row_par, :, :],
                                     k.x_flat[bass.ds(t.row, 1), :, :].rearrange("b (j p) d -> p (b j) d", p=P))\
                          .then_inc(x_in[t.row_par].sem, 16)
                if active(t, 2, UNITS):
                    u = t - 2
                    sp.wait_ge(maxT_ready.sem, maxT_ready.done(u))
                    sp.dma_start(q[ROWS_K:ROWS_A, u.group, :, :], maxT[:, u.par, :]).then_inc(max_in[u.par].sem, 16)
                if active(t, 6, UNITS) and (t - 6).group == NG - 1 and layer == 0:
                    r = (t - 6).row
                    sp.wait_ge(z_ready.sem, z_ready.done(r))
                    for b in range(B):
                        sp.dma_start(k.z[b, bass.ds(r * (QT * POS), QT * POS), :].rearrange("(j s) d -> s j d", j=QT),
                                     z_tile[b * POS:(b + 1) * POS, :, :]).then_inc(z_stored.sem, 16)
                if layer == 1 and active(t, 6, UNITS) and (t - 6).group == NG - 1:
                    u = t - 6
                    sp.wait_ge(summed.sem, summed.done(u.row))
                    sp.dma_start(k.out[bass.ds(u.row, 1), :, :].rearrange("b (j p) d -> p (b j) d", p=P),
                                 k.x_sum[:, bass.ds(u.row * QT, QT), :]).then_inc(stored[u.row_par].sem, 16)

            in_steps(sp, UNITS, DEPTH + 1, step, 2 * NG, 2 * NG)
            if layer == 1:
                for i in range(2):
                    sp.wait_ge(stored[i].sem, B // 2 * 16)
            else:
                sp.wait_ge(z_stored.sem, z_stored.done(B - 1))

        @block.gpsimd
        def _(pool):
            pool.memset(vals[:, :, :, :], 0.0).then_inc(preset.sem, 1)
            pool.wait_ge(preset.sem, 1)
            pool.memset(vals[:, :, :, HD:HD + 1], 1.0).then_inc(preset.sem, 1)
            pool.wait_ge(preset.sem, 2)
            src = (k.done0, k.done1)[layer]

            def second_norm(r):
                here = slice(r * QT, (r + 1) * QT)
                for i in range(4):
                    pool.wait_ge(gathered[i].sem, (r + 1) * 16)
                if r >= 1:
                    pool.wait_ge(z_normed.sem, z_normed.done(r - 1))
                pool.tensor_tensor(z_sum[:, :, :], k.y[:, here, :], moe[:, here, :], ALU.add).then_inc(z_summed.sem, 1)
                ln_rstd(pool, k, z_mv, z_ve, z_rstd, z_mv_done, z_eps_done, z_rstd_done, r)
                pool.wait_ge(z_normed.sem, z_normed.done(r))
                pool.tensor_tensor(z_gain[:, :, :], z_norm[:, :, :], wide(k.row[:, R_G2, :]), ALU.mult).then_inc(z_scaled.sem, 1)
                pool.wait_ge(z_scaled.sem, z_scaled.done(r))
                if r >= 1:
                    pool.wait_ge(z_stored.sem, z_stored.done(r - 1))
                pool.tensor_tensor(z_tile[:, :, :], z_gain[:, :, :], wide(k.row[:, R_BE2, :]), ALU.add).then_inc(z_ready.sem, 1)

            for n in range(UNITS + NG):
                if layer == 0 and n >= 7 and (n - 7) % NG == 0:
                    second_norm((n - 7) // NG)
                if n >= UNITS:
                    continue
                if n >= 2:
                    pool.wait_ge(mixed.sem, mixed.done(n - 2))
                b, g = divmod(n, NG)
                pool.tensor_copy(vals[:, n % 2, :, 0:HD].rearrange("p (j h) d -> p j h d", j=QT),
                                 k.v_all[:, b, :, g * GH * HD:(g + 1) * GH * HD].rearrange("p j (h d) -> p j h d", h=GH))\
                    .then_inc(vals_ready.sem, 1)
                for c in range(layer + 1):
                    m = n * (layer + 1) + c
                    if m >= 4:
                        pool.wait_ge(gathered[m % 4].sem, m // 4 * 16)
                    pool.indirect_dma_start(moe[:, c * NT + n, :], None, src,
                                            bass.IndirectOffsetOnAxis(ap=k.rank_row[:, c * NT + n:c * NT + n + 1], axis=0))\
                        .then_inc(gathered[m % 4].sem, 16)
            for i in range(4):
                pool.wait_ge(gathered[i].sem, UNITS * (layer + 1) // 4 * 16)

        @block.scalar
        def _(act):
            def exponentials(u, c):
                act.wait_ge(prob_ps.sem, prob_ps.after(u, c))
                if c == 0 and u.past(2):
                    act.wait_ge(mixed.sem, mixed.done(u - 2))
                bank = PROB + 2 * ((u.par + c) % 2)
                act.activation(probs[:, u.par, 2 * c:2 * c + 2, :], ps[:, bank:bank + 2, :], ACT.Exp)\
                   .then_inc(exped.sem, 1)

            def step(t):
                row_ends = active(t, 5, UNITS) and (t - 5).group == NG - 1
                for c in range(SCH):
                    if active(t, 2, UNITS):
                        exponentials(t - 2, c)
                    if c == 3 and active(t, 3, UNITS):
                        u = t - 3
                        act.wait_ge(mixed.sem, mixed.done(u))
                        if u.past(1):
                            act.wait_ge(mix_turned.sem, mix_turned.done(u - 1))
                        act.copy(mixT[:, :], ps[:, MIX, :]).then_inc(mixT_ready.sem, 1)
                    if c == 2 and row_ends:
                        r = (t - 5).row
                        act.wait_ge(context_turned.sem, context_turned.done(r))
                        act.copy(contextT[:, :], ps[:, TURN, :]).then_inc(contextT_ready.sem, 1)

            in_steps(act, UNITS, DEPTH, step, 2 * NG, 2 * NG)

        @block.tensor
        def _(pe):
            def maxima(u, c):
                if c == 0:
                    pe.wait_ge(loaded[u.group].sem, (u.row + 1) * 32)
                if u.past(1) or c >= 2:
                    pe.wait_ge(maxed.sem, maxed.after(u, c - 2))
                g = u.group
                for h, qt, col in max_chunk(c):
                    last = col + (qt + 1) * P
                    pe.matmul(ps[:, MAXB + c % 2, col:last], q[0:ROWS_K, g, h, qt * P:(qt + 1) * P],
                              ks[0:ROWS_K, g, h, 0:(qt + 1) * P], start=True, stop=False)
                    mm = pe.matmul(ps[:, MAXB + c % 2, last - P:last], k.identb[:, :], k.causal_q[:, :],
                                   start=False, stop=True)
                mm.then_inc(scored.sem, 1)

            def turn_maxima(u):
                pe.wait_ge(parts_done.sem, parts_done.done(u))
                pe.matmul(ps[0:3 * GH * QT, TURN, 0:P], max_parts[:, u.par, :, :].rearrange("p a b -> p (a b)"), k.identb[:, :],
                          start=True, stop=True)\
                  .then_inc(max_turned.sem, 1)

            def probabilities(u, c):
                if c == 0:
                    pe.wait_ge(max_in[u.par].sem, (u.pair + 1) * 16)
                if u.past(1) or c >= 2:
                    pe.wait_ge(exped.sem, exped.after(u, c - 2))
                g = u.group
                for n in (2 * c, 2 * c + 1):
                    bank = PROB + 2 * ((u.par + c) % 2) + n % 2
                    for h, kt, col in prob_bank(n):
                        pe.matmul(ps[:, bank, col:col + S - kt * P], ks[0:ROWS_A, g, h, kt * P:(kt + 1) * P],
                                  q[0:ROWS_A, g, h, kt * P:S], start=True, stop=False)
                        mm = pe.matmul(ps[:, bank, col:col + P], k.identb[:, :], k.causal_k[:, :], start=False, stop=True)
                mm.then_inc(prob_ps.sem, 1)

            def mix(u, kt):
                if kt == 0:
                    pe.wait_ge(exped.sem, exped.done(u))
                    pe.wait_ge(vals_ready.sem, vals_ready.done(u))
                    if u.past(1):
                        pe.wait_ge(mixT_ready.sem, mixT_ready.done(u - 1))
                for h in range(GH):
                    n, col = prob_place[h, kt]
                    mm = pe.matmul(ps[32 * h:32 * h + 32, MIX, kt * P:S], vals[:, u.par, kt * GH + h, :],
                                   probs[:, u.par, n, col:col + S - kt * P], start=(kt == 0), stop=(kt == QT - 1))
                if kt == QT - 1:
                    mm.then_inc(mixed.sem, 1)

            def turn_mix(u):
                pe.wait_ge(mixT_ready.sem, mixT_ready.done(u))
                for j in range(QT):
                    mm = pe.transpose(ps[:, TURN, j * P:(j + 1) * P], mixT[:, j * P:(j + 1) * P], k.ident[:, :])
                mm.then_inc(mix_turned.sem, 1)

            def turn_context(u):
                pe.wait_ge(context_done.sem, context_done.done(u))
                for j in range(QT):
                    mm = pe.transpose(ps[:, TURN, j * P:(j + 1) * P], context[:, u.row_par, j, :], k.ident[:, :])
                mm.then_inc(context_turned.sem, 1)

            def project(u):
                pe.wait_ge(contextT_ready.sem, contextT_ready.done(u.row))
                for j in range(QT):
                    mm = pe.matmul(ps[:, TURN, j * P:(j + 1) * P], contextT[:, j * P:(j + 1) * P], k.wT[:, w_o, :],
                                   start=True, stop=True)
                mm.then_inc(projected.sem, 1)

            def turn_free(t, use):
                if use == 0:
                    if active(t, 2, UNITS):
                        pe.wait_ge(maxT_ready.sem, maxT_ready.done(t - 2))
                    elif active(t, 5, UNITS):
                        pe.wait_ge(context_done.sem, context_done.done(t - 5))
                    if active(t, 6, UNITS) and (t - 6).group == NG - 1:
                        pe.wait_ge(added.sem, added.done((t - 6).row))
                elif active(t, 4, UNITS):
                    pe.wait_ge(context_done.sem, context_done.done(t - 4))
                elif use == 1 and active(t, 2, UNITS):
                    pe.wait_ge(maxT_ready.sem, maxT_ready.done(t - 2))
                if use == 2 and active(t, 1, UNITS):
                    pe.wait_ge(maxT_ready.sem, maxT_ready.done(t - 1))

            def step(t):
                row_ends = active(t, 5, UNITS) and (t - 5).group == NG - 1
                for c in range(MCH):
                    if active(t, 0, UNITS):
                        maxima(t, c)
                    if c % 2 and active(t, 2, UNITS):
                        probabilities(t - 2, c // 2)
                    if c % 2 == 0 and c < 2 * QT and active(t, 3, UNITS):
                        mix(t - 3, c // 2)
                    if c == 1 and active(t, 4, UNITS):
                        turn_free(t, 0)
                        turn_mix(t - 4)
                    if c == 3 and active(t, 1, UNITS):
                        turn_free(t, 1)
                        turn_maxima(t - 1)
                    if c == 7 and row_ends:
                        turn_free(t, 2)
                        turn_context(t - 5)
                    if c == 9 and row_ends:
                        project(t - 5)

            in_steps(pe, UNITS, DEPTH, step, 2 * NG, 2 * NG)

        @block.vector
        def _(dve):
            for i in range(RING):
                if layer == 1:
                    dve.memset(q[0:ROWS_A, i, :, :], 0.0)
                dve.memset(ks[0:ROWS_A, i, :, :], 1.0).then_inc(filled.sem, 1)

            def reduce(u, c):
                dve.wait_ge(scored.sem, scored.after(u, c))
                bank = ps[:, MAXB + c % 2, :]
                blocks = max_chunk(c)
                if c % 5 == 4:
                    h, qt, _ = blocks[0]
                    out = neg_max[:, u.par, h:h + 2, qt]
                    dve.tensor_reduce(out, bank.rearrange("p (h t) -> p h t", h=2), X_AXIS, ALU.max, negate=True)\
                       .then_inc(maxed.sem, 1)
                    return
                for n, (h, qt, col) in enumerate(blocks):
                    ins = dve.tensor_reduce(neg_max[:, u.par, h, qt:qt + 1], bank[:, col:col + (qt + 1) * P], X_AXIS,
                                            ALU.max, negate=True)
                ins.then_inc(maxed.sem, 1)

            def split_maxima(u, part):
                flat = neg_max[:, u.par, :, :].rearrange("p h j -> p (h j)")
                parts = max_parts[:, u.par, :, :]
                if part == 0:
                    if u.past(2):
                        dve.wait_ge(max_turned.sem, max_turned.done(u - 2))
                    dve.wait_ge(maxed.sem, maxed.done(u))
                    dve.tensor_copy(parts[:, 0, :], flat).then_inc(high_done.sem, 1)
                elif part == 1:
                    dve.wait_ge(high_done.sem, high_done.done(u))
                    dve.tensor_tensor(rest[:, :], flat, parts[:, 0, :], ALU.subtract).then_inc(rest_done.sem, 1)
                elif part == 2:
                    dve.wait_ge(rest_done.sem, rest_done.done(u))
                    dve.tensor_copy(parts[:, 1, :], rest[:, :]).then_inc(mid_done.sem, 1)
                else:
                    dve.wait_ge(mid_done.sem, mid_done.done(u))
                    dve.tensor_tensor(parts[:, 2, :], rest[:, :], parts[:, 1, :], ALU.subtract).then_inc(parts_done.sem, 1)

            def copy_maxima(u):
                dve.wait_ge(max_turned.sem, max_turned.done(u))
                if u.past(2):
                    dve.wait_ge(max_in[u.par].sem, u.pair * 16)
                dve.tensor_copy(maxT[:, u.par, :], ps[0:3 * GH * QT, TURN, 0:P])\
                   .then_inc(maxT_ready.sem, 1)

            def divide(u):
                dve.wait_ge(mix_turned.sem, mix_turned.done(u))
                turned = ps[:, TURN, :].rearrange("p (n f) -> p n f", f=32)
                dve.reciprocal(inv[:, :], turned[:, :, HD]).then_inc(inv_done.sem, 1)
                dve.wait_ge(inv_done.sem, inv_done.done(u))
                out = context[:, u.row_par, :, u.group * GH * HD:(u.group + 1) * GH * HD]
                dve.tensor_tensor(out.rearrange("p j (h d) -> p j h d", h=GH),
                                  turned[:, :, 0:HD].rearrange("p (j h) d -> p j h d", h=GH),
                                  inv[:, :].rearrange("p (j h) -> p j h", h=GH).unsqueeze(3).broadcast_to([P, QT, GH, HD]),
                                  ALU.mult).then_inc(context_done.sem, 1)

            def add_row(u):
                r = u.row
                dve.wait_ge(projected.sem, projected.done(r))
                proj = ps[:, TURN, :].rearrange("p (j d) -> p j d", j=QT)
                here = bass.ds(r * QT, QT)
                if layer == 0:
                    dve.wait_ge(x_in[u.row_par].sem, (r - u.row_par) * 8 + 16)
                    dve.tensor_tensor(k.x_sum[:, here, :], proj, x_tile[:, u.row_par, :, :], ALU.add).then_inc(added.sem, 1)
                    return
                out = k.x_sum[:, here, :]
                dve.tensor_tensor(out, proj, out, ALU.add).then_inc(added.sem, 1)
                dve.wait_ge(added.sem, added.done(r))
                dve.tensor_tensor(out, out, wide(k.row[:, R_O1, :]), ALU.add).then_inc(biased.sem, 1)
                for i in range(4):
                    dve.wait_ge(gathered[i].sem, (r + 1) * 32)
                dve.wait_ge(biased.sem, biased.done(r))
                dve.tensor_tensor(out, out, moe[:, here, :], ALU.add).then_inc(first_added.sem, 1)
                dve.wait_ge(first_added.sem, first_added.done(r))
                dve.tensor_tensor(out, out, moe[:, bass.ds(r * QT + NT, QT), :], ALU.add).then_inc(summed.sem, 1)

            def step(t):
                row_ends = active(t, 5, UNITS) and (t - 5).group == NG - 1
                for c in range(MCH):
                    if active(t, 0, UNITS):
                        reduce(t, c)
                    if c < 2 and active(t, 1, UNITS):
                        split_maxima(t - 1, 2 * c)
                        split_maxima(t - 1, 2 * c + 1)
                    if c == 4 and active(t, 1, UNITS):
                        copy_maxima(t - 1)
                    if c == 3 and layer == 0 and row_ends:
                        ln_stats(dve, z_sum, z_stats, z_mv, z_stats_done, z_mv_done, (t - 5).row, z_summed)
                    if c == 2 and active(t, 4, UNITS):
                        divide(t - 4)
                    if c == 7 and layer == 0 and row_ends:
                        ln_apply(dve, z_norm, z_sum, z_mv, z_rstd, z_rstd_done, z_normed, (t - 5).row)
                if row_ends:
                    add_row(t - 5)

            in_steps(dve, UNITS, DEPTH, step, 2 * NG, 2 * NG)


def attend0(nc, k):
    attend(nc, k, 0)


def attend1(nc, k):
    attend(nc, k, 1)




def program(nc, names, args, out, phases=None):
    k = Kept()
    k.arg, k.out = dict(zip(names, args)), out
    with ExitStack() as ctx:
        def dram(name, shape, dtype=F32):
            return nc.dram_tensor(name, shape, dtype).ap()

        def sb(name, shape, dtype=F32):
            return ctx.enter_context(nc.sbuf_tensor(name, shape, dtype))

        k.x_flat = k.arg["L0_attn_x"]
        k.sorted0, k.sorted1 = (dram(f"sorted{i}", [TILES[i] * ROWS, D]) for i in range(2))
        k.done0, k.done1 = (dram(f"done{i}", [TILES[i] * ROWS, D]) for i in range(2))
        k.z = dram("z", [B, S, D])
        k.q_stack, k.k_stack = (dram(f"{n}_stack", [B, NH, K0, S], BF16) for n in "qk")
        k.q_stack1, k.k_stack1 = (dram(f"{n}_stack1", [B, NH, K1, S], BF16) for n in "qk")
        k.wT = sb("wT", [P, 14, D])
        k.gateT = sb("gateT", [P, 2, E])
        k.row = sb("row", [P, 8, D])
        k.col = sb("col", [P, 7])
        k.hscale = sb("hscale", [P, 1])
        k.ident, k.identb = sb("ident", [P, P]), sb("identb", [P, P], BF16)
        k.causal_q, k.causal_k = sb("causal_q", [P, P], BF16), sb("causal_k", [P, P], BF16)
        k.batch_mask = sb("batch_mask", [P, P], BF16)
        k.before, k.ones, k.head_mean = sb("before", [P, P]), sb("ones", [P, P]), sb("head_mean", [P, P])
        k.half, k.ln_eps = sb("half", [P, QT]), sb("ln_eps", [P, QT])
        k.counted_i, k.counted = sb("counted_i", [P, 64], I32), sb("counted", [P, 64])
        k.logits = sb("logits", [P, NT, E])
        k.v_all = sb("v_all", [P, B, QT, D])
        k.rank_row = sb("rank_row", [P, 2 * NT], U32)
        k.tile_expert = sb("tile_expert", [P, 64], I32)
        k.y = sb("y_all", [P, NT, D])
        k.x_sum = sb("x_sum", [P, NT, D])
        k.scattered, k.gathered = ([[Signal(ctx.enter_context(nc.semaphore(f"{name}{layer}_{i}")), by=16) for i in range(4)]
                                    for layer in range(2)] for name in ("scattered", "gathered"))
        for phase in phases or PHASES:
            phase(nc, k)


PHASES = (setup, mix0, route0, prepare0, experts0, attend0, prepare1, route1, experts1, attend1)

_INS = ['L0_attn_x', 'L0_attn_Wq_amp', 'L0_attn_Wk_amp', 'L0_attn_Wq_phi', 'L0_attn_Wk_phi', 'L0_attn_Wv',
        'L0_attn_Wo', 'L0_attn_score_log_scale', 'L0_ffn_Wqkv', 'L0_ffn_bqkv', 'L0_ffn_Wo', 'L0_ffn_bo',
        'L0_ffn_g1', 'L0_ffn_be1', 'L0_ffn_g2', 'L0_ffn_be2', 'L0_ffn_Wg', 'L0_ffn_W1', 'L0_ffn_b1', 'L0_ffn_W2',
        'L0_ffn_b2', 'L1_attn_Wq', 'L1_attn_bq', 'L1_attn_Wk', 'L1_attn_bk', 'L1_attn_Wv', 'L1_attn_bv',
        'L1_attn_Wo', 'L1_attn_bo', 'L1_ffn_gate_w', 'L1_ffn_w1', 'L1_ffn_w2', 'L1_ffn_w3']
_OUTS = [((8, 512, 128), 'float32')]


def kernel(**inputs):
    import numpy as _np
    import concourse.bacc as _bacc
    from concourse import mybir as _mybir
    from concourse.bass_utils import run_bass_kernel_spmd as _run

    nc = _bacc.Bacc("TRN2", target_bir_lowering=False, num_devices=1)
    arrays, args = {}, []
    for name in _INS:
        a = _np.ascontiguousarray(inputs[name])
        arrays[f"in_{name}_dram"] = a
        args.append(nc.dram_tensor(f"in_{name}_dram", a.shape, _mybir.dt.from_np(a.dtype), kind="ExternalInput").ap())
    for i, (shape, dtype) in enumerate(_OUTS):
        dt = _mybir.dt.from_np(_np.dtype(dtype))
        args.append(nc.dram_tensor(f"out_{i}_dram", shape, dt, kind="ExternalOutput").ap())
    program(nc, _INS, args[:-1], args[-1])
    r = _run(nc, [arrays], core_ids=[0])
    got = tuple(r.results[0][f"out_{i}_dram"] for i in range(len(_OUTS)))
    return got[0]
```

```python
from contextlib import ExitStack

import numpy as np

import concourse.bass as bass
from concourse import mybir

F32 = mybir.dt.float32
BF16 = mybir.dt.bfloat16
I32 = mybir.dt.int32
U32 = mybir.dt.uint32
ALU = mybir.AluOpType
ACT = mybir.ActivationFunctionType
X_AXIS = mybir.AxisListType.X

P = 128
B, S, D = 8, 512, 128
T = B * S
NT = T // P
NH = 16
HD = D // NH
MH = 4
MD = D // MH
E = 8
DF = 512
HID = 352
QT = S // P
GH = 4
NG = NH // GH
ROWS = 2 * P
TILES = (T // ROWS + E - 1, 2 * T // ROWS + E - 1)
POS = P // B
LN_EPS = 1e-5
AMP_EPS = 1e-6
NEG = -1e30
PI = float(np.pi)

Q_PARTS = (0, 1, 0, 2, 0, 1)
K_PARTS = (0, 0, 1, 0, 2, 1)
SLOTS = len(Q_PARTS)
K0, K1 = SLOTS * 2 * HD, SLOTS * HD

(W_QA, W_KA, W_QP, W_KP, W_V0, W_O0, W_MQ, W_MK, W_MV, W_MO, W_Q1, W_K1, W_V1, W_O1) = range(14)
C_MQ, C_MK, C_Q1, C_K1, C_HS, C_PIH, C_EPS = range(7)
R_MV, R_MO, R_G1, R_BE1, R_G2, R_BE2, R_V1, R_O1 = range(8)


class Kept:
    pass


class Signal:

    def __init__(self, sem, per=1, by=1):
        self.sem, self.per, self.by = sem, per, by

    def after(self, unit, k=0):
        return (n_of(unit) * self.per + k + 1) * self.by

    def done(self, unit):
        return (n_of(unit) + 1) * self.per * self.by


def n_of(unit):
    return unit.n if isinstance(unit, Unit) else unit


class Unit:

    def __init__(self, turn, phase, cycle=2):
        self.turn, self.phase, self.cycle = turn, phase, cycle

    @property
    def n(self):
        return self.turn * self.cycle + self.phase

    @property
    def par(self):
        return self.phase % 2

    @property
    def pair(self):
        return self.turn * (self.cycle // 2) + self.phase // 2

    @property
    def group(self):
        return self.phase % NG

    @property
    def row(self):
        return self.turn * (self.cycle // NG) + self.phase // NG

    @property
    def row_par(self):
        return self.phase // NG % 2

    def __sub__(self, k):
        return Unit(self.turn + (self.phase - k) // self.cycle, (self.phase - k) % self.cycle, self.cycle)

    def __add__(self, k):
        return self - (-k)

    def past(self, k):
        return not isinstance(self.turn, int) or self.n >= k


def in_steps(eng, units, depth, step, cycle=2, first=4):
    turns = (units - first) // cycle
    for t in range(first):
        step(Unit(t // cycle, t % cycle, cycle))
    with eng.Fori(0, turns) as i:
        for phase in range(cycle):
            step(Unit(i + first // cycle, phase, cycle))
    for t in range(first + cycle * turns, units + depth - 1):
        step(Unit(t // cycle, t % cycle, cycle))


def active(t, k, units):
    return not isinstance(t.turn, int) or 0 <= t.n - k < units


def wide(row):
    return row.unsqueeze(1).broadcast_to([P, QT, D])


def phase_resources(nc, ctx, phase):
    def sb(name, shape, dtype=F32):
        return ctx.enter_context(nc.sbuf_tensor(f"{phase}_{name}", shape, dtype))

    def banks(name, n):
        return ctx.enter_context(nc.psum_tensor(f"{phase}_{name}", [P, n, 512], F32))

    numbers = []

    def clear():
        with nc.Block() as block:
            @block.sync
            def _(sp):
                for n in sorted(numbers):
                    if n - 1 not in numbers:
                        end = n
                        while end in numbers:
                            end += 1
                        sp.sem_clear(range(n, end))

    ctx.callback(clear)

    def signal(name, per=1, by=1):
        sem = ctx.enter_context(nc.semaphore(f"{phase}_{name}"))
        numbers.append(sem.num)
        return Signal(sem, per, by)

    return sb, banks, signal




def setup(nc, k):
    with ExitStack() as ctx:
        sb, banks, signal = phase_resources(nc, ctx, "setup")
        wraw = sb("wraw", [P, 14, D])
        graw = sb("graw", [E, 2, D])
        turned_ps = banks("turned_ps", 4)
        raw_in = [signal(f"raw_in{i}", by=16) for i in range(14)]
        gate_in = signal("gate_in", per=2, by=16)
        rows_in = signal("rows_in", per=8, by=16)
        cols_in = signal("cols_in", per=5, by=16)
        base_set = signal("base_set")
        ident_ready = signal("ident_ready")
        turned = signal("turned")
        copied = signal("copied")
        scale_exp = signal("scale_exp")
        scale_ready = signal("scale_ready")
        block = ctx.enter_context(nc.Block())
        squares = [k.arg["L0_attn_Wq_amp"], k.arg["L0_attn_Wk_amp"], k.arg["L0_attn_Wq_phi"], k.arg["L0_attn_Wk_phi"], k.arg["L0_attn_Wv"],
                   k.arg["L0_attn_Wo"], k.arg["L0_ffn_Wqkv"][0:D], k.arg["L0_ffn_Wqkv"][D:2 * D], k.arg["L0_ffn_Wqkv"][2 * D:3 * D],
                   k.arg["L0_ffn_Wo"], k.arg["L1_attn_Wq"], k.arg["L1_attn_Wk"], k.arg["L1_attn_Wv"], k.arg["L1_attn_Wo"]]

        @block.sync
        def _(sp):
            for n in range(0, 14, 2):
                sp.dma_start(wraw[:, n, :], squares[n]).then_inc(raw_in[n].sem, 16)
            sp.dma_start(graw[:, 0, :], k.arg["L0_ffn_Wg"]).then_inc(gate_in.sem, 16)
            sp.dma_start(graw[:, 1, :], k.arg["L1_ffn_gate_w"]).then_inc(gate_in.sem, 16)
            rows = [k.arg["L0_ffn_bqkv"][2 * D:3 * D], k.arg["L0_ffn_bo"], k.arg["L0_ffn_g1"], k.arg["L0_ffn_be1"], k.arg["L0_ffn_g2"],
                    k.arg["L0_ffn_be2"], k.arg["L1_attn_bv"], k.arg["L1_attn_bo"]]
            for n, row in enumerate(rows):
                sp.dma_start(k.row[:, n, :], row.rearrange("(o d) -> o d", o=1).partition_broadcast(P))\
                   .then_inc(rows_in.sem, 16)
            sp.wait_ge(rows_in.sem, rows_in.done(0))

        @block.scalar
        def _(act):
            for n in range(1, 14, 2):
                act.dma_start(wraw[:, n, :], squares[n]).then_inc(raw_in[n].sem, 16)
            cols = [k.arg["L0_ffn_bqkv"][0:D], k.arg["L0_ffn_bqkv"][D:2 * D], k.arg["L1_attn_bq"], k.arg["L1_attn_bk"]]
            for n, col in enumerate(cols):
                act.dma_start(k.col[:, n:n + 1], col.rearrange("(d o) -> d o", o=1)).then_inc(cols_in.sem, 16)
            act.dma_start(k.col[:, C_HS:C_HS + 1],
                          k.arg["L0_attn_score_log_scale"].rearrange("(h o) -> h o", o=1).broadcast_to([NH, HD]))\
               .then_inc(cols_in.sem, 16)
            act.wait_ge(cols_in.sem, cols_in.done(0))
            act.activation(k.hscale[:, :], k.col[:, C_HS:C_HS + 1], ACT.Exp).then_inc(scale_exp.sem, 1)
            for n in range(4):
                act.wait_ge(turned.sem, min(4 * n + 4, 14))
                m = min(4, 14 - 4 * n)
                act.copy(k.wT[:, 4 * n:4 * n + m, :], turned_ps[:, n, 0:m * D]).then_inc(copied.sem, 1)
            act.wait_ge(turned.sem, 15)
            act.copy(k.gateT[:, :, :], turned_ps[:, 3, 256:256 + 2 * E]).then_inc(copied.sem, 1)

        @block.gpsimd
        def _(pool):
            pool.memset(k.ident[:, :], 0.0).then_inc(base_set.sem, 1)
            pool.wait_ge(base_set.sem, 1)
            pool.affine_select(out=k.ident[:, :], in_=k.ident[:, :], compare_op=ALU.not_equal, fill=1.0, base=0,
                               pattern=[[-1, P]], channel_multiplier=1).then_inc(ident_ready.sem, 1)
            pool.memset(k.causal_q[:, :], 0.0).then_inc(base_set.sem, 1)
            pool.memset(k.causal_k[:, :], 0.0).then_inc(base_set.sem, 1)
            pool.memset(k.batch_mask[:, :], NEG).then_inc(base_set.sem, 1)
            pool.memset(k.before[:, :], 1.0).then_inc(base_set.sem, 1)
            pool.memset(k.ones[:, :], 1.0).then_inc(base_set.sem, 1)
            pool.memset(k.head_mean[:, :], 1.0 / HD).then_inc(base_set.sem, 1)
            pool.memset(k.half[:, :], -0.5).then_inc(base_set.sem, 1)
            pool.memset(k.ln_eps[:, :], LN_EPS).then_inc(base_set.sem, 1)
            pool.memset(k.col[:, C_PIH:C_PIH + 1], PI / 2).then_inc(base_set.sem, 1)
            pool.memset(k.col[:, C_EPS:C_EPS + 1], AMP_EPS).then_inc(base_set.sem, 1)
            pool.wait_ge(ident_ready.sem, 1)
            pool.tensor_copy(k.identb[:, :], k.ident[:, :]).then_inc(ident_ready.sem, 1)
            pool.wait_ge(base_set.sem, 11)
            pool.affine_select(out=k.causal_q[:, :], in_=k.causal_q[:, :], compare_op=ALU.is_ge, fill=NEG, base=0,
                               pattern=[[-1, P]], channel_multiplier=1).then_inc(base_set.sem, 1)
            pool.affine_select(out=k.causal_k[:, :], in_=k.causal_k[:, :], compare_op=ALU.is_ge, fill=NEG, base=0,
                               pattern=[[1, P]], channel_multiplier=-1).then_inc(base_set.sem, 1)
            pool.affine_select(out=k.before[:, :], in_=k.before[:, :], compare_op=ALU.is_gt, fill=0.0, base=0,
                               pattern=[[1, P]], channel_multiplier=-1).then_inc(base_set.sem, 1)
            head = k.head_mean[:, :].rearrange("p (h d) -> p h d", d=HD)
            pool.affine_select(out=head, in_=head, compare_op=ALU.is_ge, fill=0.0, base=0,
                               pattern=[[-HD, NH], [0, HD]], channel_multiplier=1).then_inc(base_set.sem, 1)
            pool.wait_ge(base_set.sem, 15)
            pool.affine_select(out=head, in_=head, compare_op=ALU.is_ge, fill=0.0, base=HD - 1,
                               pattern=[[HD, NH], [0, HD]], channel_multiplier=-1).then_inc(base_set.sem, 1)
            for n, m in enumerate(range(-(B - 1), B)):
                pool.wait_ge(base_set.sem, 16 + n)
                pool.affine_select(out=k.batch_mask[:, :], in_=k.batch_mask[:, :], compare_op=ALU.not_equal,
                                   fill=0.0, base=-POS * m, pattern=[[-1, P]], channel_multiplier=1)\
                    .then_inc(base_set.sem, 1)
            pool.iota(k.counted_i[:, :], pattern=[[1, 64]], base=0, channel_multiplier=0)\
                .then_inc(base_set.sem, 1)
            pool.wait_ge(base_set.sem, 32)
            pool.tensor_copy(k.counted[:, :], k.counted_i[:, :]).then_inc(base_set.sem, 1)
            pool.wait_ge(base_set.sem, 33)

        @block.tensor
        def _(pe):
            pe.wait_ge(ident_ready.sem, 1)
            for n in range(14):
                pe.wait_ge(raw_in[n].sem, 16)
                pe.transpose(turned_ps[:, n // 4, n % 4 * D:(n % 4 + 1) * D], wraw[:, n, :], k.ident[:, :])\
                  .then_inc(turned.sem, 1)
            pe.wait_ge(gate_in.sem, gate_in.done(0))
            pe.wait_ge(copied.sem, 4)
            pe.transpose(turned_ps[:, 3, 256:256 + E], graw[:, 0, :], k.ident[0:E, 0:E])
            pe.transpose(turned_ps[:, 3, 256 + E:256 + 2 * E], graw[:, 1, :], k.ident[0:E, 0:E])\
              .then_inc(turned.sem, 1)

        @block.vector
        def _(dve):
            dve.wait_ge(scale_exp.sem, 1)
            dve.tensor_scalar(k.hscale[:, :], k.hscale[:, :], float(HD) ** -0.5, None, ALU.mult)\
               .then_inc(scale_ready.sem, 1)
            dve.wait_ge(scale_ready.sem, 1)




def ln_stats(dve, src, stats, mv, stats_done, mv_done, unit, src_ready=None):
    if src_ready:
        dve.wait_ge(src_ready.sem, src_ready.done(unit))
    for j in range(QT):
        dve.bn_stats(stats[:, j, 0:6], src[:, j, :]).then_inc(stats_done.sem, 1)
    dve.wait_ge(stats_done.sem, stats_done.done(unit))
    dve.tensor_copy(stats[:, 0, 6:7], stats[:, 0, 0:1])
    for j in range(QT):
        dve.bn_aggr(mv[:, j, :], stats[:, j, 0:6]).then_inc(mv_done.sem, 1)


def ln_rstd(pool, k, mv, var_eps, rstd, mv_done, eps_done, rstd_done, unit):
    pool.wait_ge(mv_done.sem, mv_done.done(unit))
    pool.tensor_tensor(var_eps[:, :], mv[:, :, 1], k.ln_eps[:, :], ALU.add).then_inc(eps_done.sem, 1)
    pool.wait_ge(eps_done.sem, eps_done.done(unit))
    pool.tensor_tensor(rstd[:, :], var_eps[:, :], k.half[:, :], ALU.pow).then_inc(rstd_done.sem, 1)


def ln_apply(dve, dst, src, mv, rstd, rstd_done, xn_done, unit):
    dve.wait_ge(rstd_done.sem, rstd_done.done(unit))
    for j in range(QT):
        dve.tensor_scalar(dst[:, j, :], src[:, j, :], mv[:, j, 0:1], rstd[:, j:j + 1], ALU.subtract, ALU.mult)\
           .then_inc(xn_done.sem, 1)




def mix0(nc, k):
    UNITS = T // (QT * P)
    with ExitStack() as ctx:
        sb, banks, signal = phase_resources(nc, ctx, "mix0")
        zeros = sb("zeros", [P, ROWS * D // P])
        x_tile = sb("x_tile", [P, 2, QT, D])
        xn = sb("xn", [P, 2, QT, D])
        xnT = sb("xnT", [P, QT * P])
        qT = sb("qT", [P, 2, QT * P])
        k_heads = sb("k_heads", [P, 2, QT, MH, P])
        v = sb("v", [P, 2, QT, D])
        probs = sb("probs", [P, 2, MH, P])
        probsT = sb("probsT", [P, 2, MH, P])
        neg_max = sb("neg_max", [P, 2, MH])
        sums = sb("sums", [P, 2, MH])
        rsums = sb("rsums", [P, 2, MH])
        mixedT = sb("mixedT", [P, QT * P])
        res = sb("res", [P, 2, QT, D])
        res_n = sb("res_n", [P, QT, D])
        res_g = sb("res_g", [P, QT, D])
        y = sb("y", [P, 2, QT, D])
        yT = sb("yT", [P, QT * P])
        stats_a, stats_c = sb("stats_a", [P, QT, 7]), sb("stats_c", [P, QT, 7])
        mv_a, mv_c = sb("mv_a", [P, QT, 2]), sb("mv_c", [P, QT, 2])
        ve_a, ve_c = sb("ve_a", [P, QT]), sb("ve_c", [P, QT])
        rstd_a, rstd_c = sb("rstd_a", [P, QT]), sb("rstd_c", [P, QT])
        ps = banks("mix_ps", 8)
        XV, Q, K_, SC, PT, MX, OUT = 0, 1, 2, 3, 5, 6, 7

        x_in = [signal(f"x_in{i}", B, 16) for i in range(2)]
        heads_zero = signal("heads_zero")
        zero_set, zero_out = signal("zero_set"), signal("zero_out", by=16)
        stats_a_done, mv_a_done = signal("stats_a_done", QT), signal("mv_a_done", QT)
        eps_a_done, rstd_a_done = signal("eps_a_done"), signal("rstd_a_done")
        xn_done = signal("xn_done", QT)
        x_turned, xT_ready = signal("x_turned"), signal("xT_ready")
        q_proj, k_proj, v_proj = signal("q_proj"), signal("k_proj"), signal("v_proj")
        q_ready, v_ready = signal("q_ready"), signal("v_ready")
        k_ready_act, k_ready_dve = signal("k_ready_act", 2), signal("k_ready_dve", 2)
        scored, maxed = signal("scored", QT), signal("maxed", QT)
        exped, sums_inv, normed = signal("exped", QT * MH), signal("sums_inv", QT), signal("normed", QT)
        p_turned, pT_ready, mixed = signal("p_turned", QT), signal("pT_ready", QT), signal("mixed", QT)
        mixT_ready, projected, res_done, res_bias = (signal(x) for x in ("mixT_ready", "projected", "res_done", "res_bias"))
        stats_c_done, mv_c_done = signal("stats_c_done", QT), signal("mv_c_done", QT)
        eps_c_done, rstd_c_done = signal("eps_c_done"), signal("rstd_c_done")
        res_n_done, res_g_done, y_ready = signal("res_n_done", QT), signal("res_g_done"), signal("y_ready")
        y_kept = [signal(f"y_kept{i}", 1, 16) for i in range(2)]
        y_turned, yT_ready, logits_ps, logits_done = (signal(x) for x in ("y_turned", "yT_ready", "logits_ps", "logits_done"))
        DEPTH = 4
        block = ctx.enter_context(nc.Block())

        @block.sync
        def _(sp):
            def load(u):
                if u.past(2):
                    sp.wait_ge(xn_done.sem, xn_done.done(u - 2))
                for b in range(B):
                    src = k.x_flat[b, bass.ds(u.n * (QT * POS), QT * POS), :]
                    sp.dma_start(x_tile[b * POS:(b + 1) * POS, u.par, :, :],
                                 src.rearrange("(j s) d -> s j d", j=QT)).then_inc(x_in[u.par].sem, 16)

            def keep(u):
                sp.wait_ge(y_ready.sem, y_ready.done(u))
                sp.dma_start(k.y[:, bass.ds(u.n * QT, QT), :], y[:, u.par, :, :]).then_inc(y_kept[u.par].sem, 16)

            fills = [(dst, a, min(8, TILES[layer] - a)) for layer, dst in enumerate((k.sorted0, k.sorted1))
                     for a in range(0, TILES[layer], 8)]

            def fill(dst, a, m):
                sp.dma_start(dst[a * ROWS:(a + m) * ROWS, :].rearrange("(a p r) d -> p a (r d)", a=m, p=P),
                             zeros[:, :].unsqueeze(1).broadcast_to([P, m, ROWS * D // P])).then_inc(zero_out.sem, 16)

            def step(t):
                if active(t, 0, UNITS):
                    load(t)
                if isinstance(t.turn, int) and 1 <= t.n < 4:
                    sp.wait_ge(zero_set.sem, 1)
                    for f in fills[t.n - 1::3]:
                        fill(*f)
                if active(t, 3, UNITS):
                    keep(t - 3)

            in_steps(sp, UNITS, DEPTH, step)
            for i in range(2):
                sp.wait_ge(y_kept[i].sem, 16 * UNITS // 2)
            sp.wait_ge(zero_out.sem, 16 * len(fills))

        @block.gpsimd
        def _(pool):
            pool.memset(zeros[:, :], 0.0).then_inc(zero_set.sem, 1)
            for half in range(2):
                pool.memset(k_heads[:, half, :, :, :], 0.0).then_inc(heads_zero.sem, 1)

            def add_bias(u):
                pool.wait_ge(res_done.sem, res_done.done(u))
                pool.tensor_tensor(res[:, u.par, :, :], res[:, u.par, :, :], wide(k.row[:, R_MO, :]), ALU.add)\
                    .then_inc(res_bias.sem, 1)

            def gain_and_bias(u):
                pool.wait_ge(res_n_done.sem, res_n_done.done(u))
                pool.tensor_tensor(res_g[:, :, :], res_n[:, :, :], wide(k.row[:, R_G1, :]), ALU.mult)\
                    .then_inc(res_g_done.sem, 1)
                pool.wait_ge(res_g_done.sem, res_g_done.done(u))
                if u.past(2):
                    pool.wait_ge(y_turned.sem, y_turned.done(u - 2))
                    pool.wait_ge(y_kept[u.par].sem, (u - 2).pair * 16 + 16)
                pool.tensor_tensor(y[:, u.par, :, :], res_g[:, :, :], wide(k.row[:, R_BE1, :]), ALU.add)\
                    .then_inc(y_ready.sem, 1)

            def step(t):
                if active(t, 0, UNITS):
                    ln_rstd(pool, k, mv_a, ve_a, rstd_a, mv_a_done, eps_a_done, rstd_a_done, t)
                if active(t, 2, UNITS):
                    add_bias(t - 2)
                    ln_rstd(pool, k, mv_c, ve_c, rstd_c, mv_c_done, eps_c_done, rstd_c_done, t - 2)
                    gain_and_bias(t - 2)

            in_steps(pool, UNITS, DEPTH, step)

        @block.scalar
        def _(act):
            def exponentials(u, j):
                act.wait_ge(maxed.sem, maxed.after(u, j))
                if u.past(1) or j >= 2:
                    act.wait_ge(p_turned.sem, p_turned.after(u, j - 2))
                for h in range(MH):
                    act.activation(probs[:, j % 2, h, :], ps[:, SC + j % 2, h * P:(h + 1) * P], ACT.Exp,
                                   bias=neg_max[:, j % 2, h:h + 1], accum_out=sums[:, j % 2, h:h + 1])\
                       .then_inc(exped.sem, 1)

            def copy_probs(u, j):
                act.wait_ge(p_turned.sem, p_turned.after(u, j))
                if u.past(1) or j >= 2:
                    act.wait_ge(mixed.sem, mixed.after(u, j - 2))
                act.copy(probsT[:, j % 2, :, :], ps[:, PT, :]).then_inc(pT_ready.sem, 1)

            def copy_xT(u):
                act.wait_ge(x_turned.sem, x_turned.done(u))
                if u.past(1):
                    act.wait_ge(v_proj.sem, v_proj.done(u - 1))
                act.copy(xnT[:, :], ps[:, XV, :]).then_inc(xT_ready.sem, 1)

            def keys(u):
                act.wait_ge(k_proj.sem, k_proj.done(u))
                act.wait_ge(heads_zero.sem, 2)
                for h in range(2):
                    rows = slice(MD * h, MD * (h + 1))
                    act.activation(k_heads[rows, u.par, :, h, :],
                                   ps[rows, K_, :].rearrange("p (j t) -> p j t", j=QT), ACT.Identity,
                                   bias=k.col[rows, C_MK:C_MK + 1]).then_inc(k_ready_act.sem, 1)

            def copy_mixed(u):
                act.wait_ge(mixed.sem, mixed.done(u))
                if u.past(1):
                    act.wait_ge(projected.sem, projected.done(u - 1))
                act.copy(mixedT[:, :], ps[:, MX, :]).then_inc(mixT_ready.sem, 1)

            def copy_yT(u):
                act.wait_ge(y_turned.sem, y_turned.done(u))
                if u.past(1):
                    act.wait_ge(logits_ps.sem, logits_ps.done(u - 1))
                act.copy(yT[:, :], ps[:, PT, :]).then_inc(yT_ready.sem, 1)

            def step(t):
                for j in range(QT + 1):
                    if active(t, 1, UNITS):
                        if j < QT:
                            exponentials(t - 1, j)
                        if j >= 1:
                            copy_probs(t - 1, j - 1)
                    if j == 1 and active(t, 0, UNITS):
                        copy_xT(t)
                    if j == 3 and active(t, 0, UNITS):
                        keys(t)
                if active(t, 1, UNITS):
                    copy_mixed(t - 1)
                if active(t, 3, UNITS):
                    copy_yT(t - 3)

            in_steps(act, UNITS, DEPTH, step)

        @block.tensor
        def _(pe):
            def turn_y(u):
                pe.wait_ge(y_ready.sem, y_ready.done(u))
                if active(u, -2, UNITS):
                    pe.wait_ge(pT_ready.sem, pT_ready.done(u + 2))
                if u.past(1):
                    pe.wait_ge(logits_done.sem, logits_done.done(u - 1))
                for j in range(QT):
                    mm = pe.transpose(ps[:, PT, j * P:(j + 1) * P], y[:, u.par, j, :], k.ident[:, :])
                mm.then_inc(y_turned.sem, 1)

            def logits(u):
                pe.wait_ge(yT_ready.sem, yT_ready.done(u))
                for j in range(QT):
                    mm = pe.matmul(ps[:, PT, j * E:(j + 1) * E], yT[:, j * P:(j + 1) * P], k.gateT[:, 0, :],
                                   start=True, stop=True)
                mm.then_inc(logits_ps.sem, 1)

            def project_out(u):
                pe.wait_ge(mixT_ready.sem, mixT_ready.done(u))
                if u.past(1):
                    pe.wait_ge(res_done.sem, res_done.done(u - 1))
                for j in range(QT):
                    mm = pe.matmul(ps[:, OUT, j * P:(j + 1) * P], mixedT[:, j * P:(j + 1) * P], k.wT[:, W_MO, :],
                                   start=True, stop=True)
                mm.then_inc(projected.sem, 1)

            def turn_x(u):
                pe.wait_ge(xn_done.sem, xn_done.done(u))
                if u.past(1):
                    pe.wait_ge(v_ready.sem, v_ready.done(u - 1))
                for j in range(QT):
                    mm = pe.transpose(ps[:, XV, j * P:(j + 1) * P], xn[:, u.par, j, :], k.ident[:, :])
                mm.then_inc(x_turned.sem, 1)

            def project_qk(u):
                pe.wait_ge(xT_ready.sem, xT_ready.done(u))
                if u.past(1):
                    pe.wait_ge(q_ready.sem, q_ready.done(u - 1))
                    pe.wait_ge(k_ready_act.sem, k_ready_act.done(u - 1))
                    pe.wait_ge(k_ready_dve.sem, k_ready_dve.done(u - 1))
                pe.matmul(ps[:, K_, :], k.wT[:, W_MK, :], xnT[:, :], start=True, stop=True).then_inc(k_proj.sem, 1)
                pe.matmul(ps[:, Q, :], k.wT[:, W_MQ, :], xnT[:, :], start=True, stop=True).then_inc(q_proj.sem, 1)

            def project_v(u):
                for j in range(QT):
                    mm = pe.matmul(ps[:, XV, j * P:(j + 1) * P], xnT[:, j * P:(j + 1) * P], k.wT[:, W_MV, :],
                                   start=True, stop=True)
                mm.then_inc(v_proj.sem, 1)

            def scores(u, j):
                if j == 0:
                    pe.wait_ge(q_ready.sem, q_ready.done(u))
                    pe.wait_ge(k_ready_act.sem, k_ready_act.done(u))
                    pe.wait_ge(k_ready_dve.sem, k_ready_dve.done(u))
                if u.past(1) or j >= 2:
                    pe.wait_ge(exped.sem, exped.after(u, MH * (j - 1) - 1))
                pe.matmul(ps[:, SC + j % 2, :], qT[:, u.par, j * P:(j + 1) * P], k_heads[:, u.par, j, :, :],
                          start=True, stop=False)
                pe.matmul(ps[:, SC + j % 2, :], k.identb[:, :],
                          k.batch_mask[:, :].unsqueeze(1).broadcast_to([P, MH, P]), start=False, stop=True)\
                  .then_inc(scored.sem, 1)

            def turn_probs(u, j):
                pe.wait_ge(normed.sem, normed.after(u, j))
                if j >= 1:
                    pe.wait_ge(pT_ready.sem, pT_ready.after(u, j - 1))
                elif u.past(3):
                    pe.wait_ge(logits_done.sem, logits_done.done(u - 3))
                elif u.past(1):
                    pe.wait_ge(pT_ready.sem, pT_ready.done(u - 1))
                for h in range(MH):
                    mm = pe.transpose(ps[:, PT, h * P:(h + 1) * P], probs[:, j % 2, h, :], k.ident[:, :])
                mm.then_inc(p_turned.sem, 1)

            def mix(u, j):
                pe.wait_ge(pT_ready.sem, pT_ready.after(u, j))
                if j == 0:
                    pe.wait_ge(v_ready.sem, v_ready.done(u))
                    if u.past(1):
                        pe.wait_ge(mixT_ready.sem, mixT_ready.done(u - 1))
                for h in range(MH):
                    mm = pe.matmul(ps[MD * h:MD * (h + 1), MX, j * P:(j + 1) * P],
                                   v[:, u.par, j, MD * h:MD * (h + 1)], probsT[:, j % 2, h, :],
                                   start=True, stop=True)
                mm.then_inc(mixed.sem, 1)

            def step(t):
                for j in range(QT + 2):
                    if active(t, 1, UNITS):
                        for i in (0, 1) if j == 0 else (j + 1,):
                            if i < QT:
                                scores(t - 1, i)
                        if 1 <= j <= QT:
                            turn_probs(t - 1, j - 1)
                        if j >= 2:
                            mix(t - 1, j - 2)
                    if j == 0 and active(t, 2, UNITS):
                        project_out(t - 2)
                    if j == 1 and active(t, 0, UNITS):
                        turn_x(t)
                    if j == 2 and active(t, 0, UNITS):
                        project_qk(t)
                    if j == 3 and active(t, 0, UNITS):
                        project_v(t)
                if active(t, 3, UNITS):
                    turn_y(t - 3)
                    logits(t - 3)

            in_steps(pe, UNITS, DEPTH, step)

        @block.vector
        def _(dve):
            def evacuate(u):
                dve.wait_ge(k_proj.sem, k_proj.done(u))
                for h in range(2, MH):
                    rows = slice(MD * h, MD * (h + 1))
                    dve.wait_ge(heads_zero.sem, 2)
                    dve.tensor_scalar(k_heads[rows, u.par, :, h, :], ps[rows, K_, :].rearrange("p (j t) -> p j t", j=QT),
                                      k.col[rows, C_MK:C_MK + 1], None, ALU.add).then_inc(k_ready_dve.sem, 1)
                dve.wait_ge(q_proj.sem, q_proj.done(u))
                dve.tensor_scalar(qT[:, u.par, :], ps[:, Q, :], k.col[:, C_MQ:C_MQ + 1], float(MD) ** -0.5,
                                  ALU.add, ALU.mult).then_inc(q_ready.sem, 1)
                dve.wait_ge(v_proj.sem, v_proj.done(u))
                if u.past(2):
                    dve.wait_ge(mixed.sem, mixed.done(u - 2))
                dve.tensor_tensor(v[:, u.par, :, :], ps[:, XV, :].rearrange("p (j d) -> p j d", j=QT),
                                  wide(k.row[:, R_MV, :]), ALU.add).then_inc(v_ready.sem, 1)

            def maxima(u, j):
                dve.wait_ge(scored.sem, scored.after(u, j))
                dve.tensor_reduce(neg_max[:, j % 2, :], ps[:, SC + j % 2, :].rearrange("p (h t) -> p h t", h=MH),
                                  X_AXIS, ALU.max, negate=True).then_inc(maxed.sem, 1)

            def normalise(u, j):
                dve.wait_ge(exped.sem, exped.after(u, MH * (j + 1) - 1))
                dve.reciprocal(rsums[:, j % 2, :], sums[:, j % 2, :]).then_inc(sums_inv.sem, 1)
                dve.wait_ge(sums_inv.sem, sums_inv.after(u, j))
                p = probs[:, j % 2, :, :]
                dve.tensor_tensor(p, p, rsums[:, j % 2, :].unsqueeze(2).broadcast_to([P, MH, P]), ALU.mult)\
                   .then_inc(normed.sem, 1)

            def step(t):
                if active(t, 0, UNITS):
                    dve.wait_ge(x_in[t.par].sem, (t.pair + 1) * (16 * B))
                    ln_stats(dve, x_tile[:, t.par, :, :], stats_a, mv_a, stats_a_done, mv_a_done, t)
                for j in range(QT + 1):
                    if active(t, 1, UNITS):
                        if j >= 1:
                            normalise(t - 1, j - 1)
                        for i in (0, 1) if j == 0 else (j + 1,):
                            if i < QT:
                                maxima(t - 1, i)
                    if j == 0 and active(t, 2, UNITS):
                        u = t - 2
                        dve.wait_ge(projected.sem, projected.done(u))
                        dve.tensor_tensor(res[:, u.par, :, :], ps[:, OUT, :].rearrange("p (j d) -> p j d", j=QT),
                                          xn[:, u.par, :, :], ALU.add).then_inc(res_done.sem, 1)
                    if j == 1 and active(t, 0, UNITS):
                        ln_apply(dve, xn[:, t.par, :, :], x_tile[:, t.par, :, :], mv_a, rstd_a, rstd_a_done, xn_done, t)
                    if j == 3 and active(t, 2, UNITS):
                        dve.wait_ge(res_bias.sem, res_bias.done(t - 2))
                        ln_stats(dve, res[:, t.par, :, :], stats_c, mv_c, stats_c_done, mv_c_done, t - 2)
                    if j == 4 and active(t, 2, UNITS):
                        u = t - 2
                        if u.past(1):
                            dve.wait_ge(res_g_done.sem, res_g_done.done(u - 1))
                        ln_apply(dve, res_n, res[:, u.par, :, :], mv_c, rstd_c, rstd_c_done, res_n_done, u)
                if active(t, 0, UNITS):
                    evacuate(t)
                if active(t, 3, UNITS):
                    dve.wait_ge(logits_ps.sem, logits_ps.done(t - 3))
                    dve.tensor_copy(k.logits[:, bass.ds((t - 3).n * QT, QT), :],
                                    ps[:, PT, 0:QT * E].rearrange("p (j e) -> p j e", j=QT))\
                       .then_inc(logits_done.sem, 1)

            in_steps(dve, UNITS, DEPTH, step)




def scatter(pool, k, layer, copies):
    dst = (k.sorted0, k.sorted1)[layer]
    for n in copies:
        c, t = divmod(n, NT)
        src = k.y[:, t, :] if layer == 0 else k.scaled[:, c, t, :]
        done = k.scattered[layer][n % 4]
        if n >= 4:
            pool.wait_ge(done.sem, n // 4 * 16)
        pool.indirect_dma_start(dst, bass.IndirectOffsetOnAxis(ap=k.rank_row[:, n:n + 1], axis=0), src, None)\
            .then_inc(done.sem, 16)


def norm1(nc, k):
    with ExitStack() as ctx:
        sb, banks, signal = phase_resources(nc, ctx, "norm1")
        z_tile = sb("z_tile", [P, 4, QT, D])
        xn = sb("xn", [P, 2, QT, D])
        xnT = sb("xnT", [P, 2, QT * P])
        stats, mv = sb("stats", [P, QT, 7]), sb("mv", [P, 2, QT, 2])
        var_eps, rstd = sb("var_eps", [P, 2, QT]), sb("rstd", [P, 2, QT])
        ps = banks("ps", 4)
        z_in = [signal(f"z_in{i}", by=16) for i in range(4)]
        summed, sum_kept = signal("summed"), signal("sum_kept")
        stats_done, mv_done, eps_done, rstd_done = signal("stats_done", QT), signal("mv_done", QT), signal("eps_done"), signal("rstd_done")
        xn_done, xn_kept, turned, turned_ready = signal("xn_done", QT), signal("xn_kept"), signal("turned"), signal("turned_ready")
        logits_ps, logits_done = signal("logits_ps"), signal("logits_done")
        block = ctx.enter_context(nc.Block())

        def here(u):
            return bass.ds(u.n * QT, QT)

        @block.sync
        def _(sp):
            def step(t):
                if t.past(4):
                    sp.wait_ge(xn_done.sem, xn_done.done(t - 4))
                    sp.wait_ge(sum_kept.sem, sum_kept.done(t - 4))
                sp.dma_start(z_tile[:, t.phase, :, :], k.z[bass.ds(t.n, 1), :, :].rearrange("b (j p) d -> p (b j) d", p=P))\
                  .then_inc(z_in[t.phase].sem, 16)

            in_steps(sp, B, 1, step, 4)

        @block.vector
        def _(dve):
            def step(t):
                if active(t, 0, B):
                    x_tile = z_tile[:, t.phase, :, :]
                    dve.wait_ge(z_in[t.phase].sem, (t.turn + 1) * 16)
                    dve.tensor_tensor(x_tile, x_tile, k.x_sum[:, here(t), :], ALU.add).then_inc(summed.sem, 1)
                    ln_stats(dve, x_tile, stats, mv[:, t.par, :, :], stats_done, mv_done, t, summed)
                if active(t, 1, B):
                    u = t - 1
                    if u.past(2):
                        dve.wait_ge(xn_kept.sem, xn_kept.done(u - 2))
                        dve.wait_ge(turned.sem, turned.done(u - 2))
                    ln_apply(dve, xn[:, u.par, :, :], z_tile[:, u.phase, :, :], mv[:, u.par, :, :], rstd[:, u.par, :],
                             rstd_done, xn_done, u)
                if active(t, 2, B):
                    u = t - 2
                    dve.wait_ge(logits_ps.sem, logits_ps.done(u))
                    dve.tensor_copy(k.logits[:, here(u), :], ps[:, 2 + u.par, 0:QT * E].rearrange("p (j e) -> p j e", j=QT))\
                       .then_inc(logits_done.sem, 1)

            in_steps(dve, B, 3, step, 4)

        @block.gpsimd
        def _(pool):
            def step(t):
                ln_rstd(pool, k, mv[:, t.par, :, :], var_eps[:, t.par, :], rstd[:, t.par, :], mv_done, eps_done, rstd_done, t)

            in_steps(pool, B, 1, step, 4)

        @block.scalar
        def _(act):
            def step(t):
                act.wait_ge(summed.sem, summed.done(t))
                act.copy(k.x_sum[:, here(t), :], z_tile[:, t.phase, :, :]).then_inc(sum_kept.sem, 1)
                act.wait_ge(xn_done.sem, xn_done.done(t))
                act.copy(k.y[:, here(t), :], xn[:, t.par, :, :]).then_inc(xn_kept.sem, 1)
                act.wait_ge(turned.sem, turned.done(t))
                if t.past(2):
                    act.wait_ge(logits_ps.sem, logits_ps.done(t - 2))
                act.copy(xnT[:, t.par, :], ps[:, t.par, :]).then_inc(turned_ready.sem, 1)

            in_steps(act, B, 1, step, 4)

        @block.tensor
        def _(pe):
            def step(t):
                if active(t, 1, B):
                    u = t - 1
                    pe.wait_ge(turned_ready.sem, turned_ready.done(u))
                    if u.past(2):
                        pe.wait_ge(logits_done.sem, logits_done.done(u - 2))
                    for j in range(QT):
                        mm = pe.matmul(ps[:, 2 + u.par, j * E:(j + 1) * E], xnT[:, u.par, j * P:(j + 1) * P], k.gateT[:, 1, :],
                                       start=True, stop=True)
                    mm.then_inc(logits_ps.sem, 1)
                if active(t, 0, B):
                    pe.wait_ge(xn_done.sem, xn_done.done(t))
                    if t.past(2):
                        pe.wait_ge(turned_ready.sem, turned_ready.done(t - 2))
                    for j in range(QT):
                        mm = pe.transpose(ps[:, t.par, j * P:(j + 1) * P], xn[:, t.par, j, :], k.ident[:, :])
                    mm.then_inc(turned.sem, 1)

            in_steps(pe, B, 2, step, 4)


def prepare(nc, k, layer):
    COMP = 2 - layer
    stacks = ((k.q_stack, k.k_stack), (k.q_stack1, k.k_stack1))[layer]
    w_q, w_k, w_v = ((W_QA, W_KA, W_V0), (W_Q1, W_K1, W_V1))[layer]
    SPLIT = 3 if layer == 0 else 1
    DEPTH = SPLIT + 1
    FIRST = 6 if layer == 0 else 4
    with ExitStack() as ctx:
        sb, banks, signal = phase_resources(nc, ctx, f"prepare{layer}")
        x_tile = sb("x_tile", [P, 2, QT, D]) if layer == 0 else None
        xn = sb("xn", [P, 2, QT, D])
        xnT = sb("xnT", [P, QT * P])
        stats, mv = sb("stats", [P, QT, 7]), sb("mv", [P, QT, 2])
        var_eps, rstd = sb("var_eps", [P, QT]), sb("rstd", [P, QT])
        vals = sb("vals", [P, 2, COMP, S])
        rest = sb("rest", [P, 2, COMP, S])
        parts = sb("parts", [P, 2, 2, 3, COMP, S], BF16)
        if layer == 0:
            turn = sb("turn", [P, 2, S])
            turn_abs = sb("turn_abs", [P, 2, S])
            sine, cosine = sb("sine", [P, 2, 2, S]), sb("cosine", [P, 2, 2, S])
            mag, logs = sb("mag", [P, 2, S]), sb("logs", [P, 2, S])
            amp, square = sb("amp", [P, 2, 2, S]), sb("square", [P, 2, S])
            inv, amp_n = sb("inv", [P, 2, S]), sb("amp_n", [P, 2, S])
        ps = banks("prep_ps", 7)
        XV, AMP, PHI, MS = 0, 1, 3, 5

        x_in = [signal(f"x_in{i}", by=16) for i in range(2)]
        stats_done, mv_done, eps_done, rstd_done = signal("stats_done", QT), signal("mv_done", QT), signal("eps_done"), signal("rstd_done")
        xn_done = signal("xn_done", QT if layer == 0 else 1)
        x_turned, xT_ready = signal("x_turned"), signal("xT_ready")
        projected, v_proj, v_ready = signal("projected"), signal("v_proj"), signal("v_ready")
        phases_ps, tanh_done, sine_done, turn_abs_done, cosine_done = (signal(x) for x in ("phases_ps", "tanh_done", "sine_done", "turn_abs_done", "cosine_done"))
        mag_done, exp_done, log_done, amp_done, square_done = (signal(x) for x in ("mag_done", "exp_done", "log_done", "amp_done", "square_done"))
        mean_ps, mean_log, inv_done, amp_n_done = signal("mean_ps"), signal("mean_log"), signal("inv_done"), signal("amp_n_done", 2)
        vals_done, high_done, rest_done, mid_done, low_done = signal("vals_done"), signal("high_done"), signal("rest_done"), signal("mid_done"), signal("low_done")
        stacked = [signal(f"stacked{i}", 2 * SLOTS, 16) for i in range(2)]
        vals_dve_done = signal("vals_dve_done")
        block = ctx.enter_context(nc.Block())

        @block.sync
        def _(sp):
            def load(u):
                if u.past(2):
                    sp.wait_ge(xn_done.sem, xn_done.done(u - 2))
                sp.dma_start(x_tile[:, u.par, :, :], k.x_flat[bass.ds(u.n, 1), :, :].rearrange("b (j p) d -> p (b j) d", p=P))\
                  .then_inc(x_in[u.par].sem, 16)

            def store(u):
                for side, which in enumerate((Q_PARTS, K_PARTS)):
                    for slot in sorted(range(SLOTS), key=lambda s: which[s]):
                        done = (high_done, mid_done, low_done)[which[slot]]
                        sp.wait_ge(done.sem, done.done(u))
                        rows = stacks[side][bass.ds(u.n, 1), :, slot * COMP * HD:(slot + 1) * COMP * HD, :]
                        sp.dma_start(rows.rearrange("b h (d c) t -> (b h) d (c t)", d=HD), parts[:, u.par, side, which[slot], :, :].rearrange("p c t -> p (c t)"))\
                          .then_inc(stacked[u.par].sem, 16)

            def step(t):
                if layer == 0 and active(t, 0, B):
                    load(t)
                if active(t, DEPTH, B):
                    store(t - DEPTH)

            in_steps(sp, B, DEPTH + 1, step, 2, FIRST)
            for i in range(2):
                sp.wait_ge(stacked[i].sem, stacked[i].done(B // 2 - 1))

        @block.gpsimd
        def _(pool):
            def step(t):
                if active(t, 0, B):
                    ln_rstd(pool, k, mv, var_eps, rstd, mv_done, eps_done, rstd_done, t)
                if active(t, 3, B):
                    u = t - 3
                    pool.wait_ge(amp_n_done.sem, amp_n_done.done(u))
                    if u.past(1):
                        pool.wait_ge(rest_done.sem, rest_done.done(u - 1))
                    pool.tensor_tensor(vals[:, :, 1, :], amp_n[:, :, :], sine[:, u.par, :, :], ALU.mult).then_inc(vals_done.sem, 1)
                if isinstance(t.turn, int) and t.n < FIRST:
                    scatter(pool, k, 0, range(t.n * PER_STEP, min((t.n + 1) * PER_STEP, NT)))

            if layer == 0:
                PER_STEP = -(-NT // FIRST)
                in_steps(pool, B, DEPTH, step, 2, FIRST)
            else:
                scatter(pool, k, 1, range(2 * NT))
            for done in k.scattered[layer]:
                pool.wait_ge(done.sem, (layer + 1) * NT // 4 * 16)

        @block.scalar
        def _(act):
            def inverse(u):
                act.activation(inv[:, :, :], inv[:, :, :], ACT.Exp, scale=-0.5).then_inc(inv_done.sem, 1)

            def square_amplitude(u):
                act.wait_ge(amp_done.sem, amp_done.done(u))
                if u.past(1):
                    act.wait_ge(mean_ps.sem, mean_ps.done(u - 1))
                act.activation(square[:, :, :], amp[:, u.par, :, :], ACT.Square).then_inc(square_done.sem, 1)

            def tanh_and_exp(u):
                act.wait_ge(phases_ps.sem, phases_ps.done(u))
                if u.past(1):
                    act.wait_ge(sine_done.sem, sine_done.done(u - 1))
                    act.wait_ge(turn_abs_done.sem, turn_abs_done.done(u - 1))
                act.activation(turn[:, :, :], ps[:, PHI:PHI + 2, :], ACT.Tanh).then_inc(tanh_done.sem, 1)
                act.wait_ge(projected.sem, projected.done(u))
                if u.past(1):
                    act.wait_ge(log_done.sem, log_done.done(u - 1))
                act.activation(mag[:, :, :], ps[:, AMP:AMP + 2, :], ACT.Abs).then_inc(mag_done.sem, 1)
                act.wait_ge(mag_done.sem, mag_done.done(u))
                act.activation(mag[:, :, :], mag[:, :, :], ACT.Exp, scale=-1.0).then_inc(exp_done.sem, 1)

            def sine_and_cosine(u):
                act.wait_ge(tanh_done.sem, tanh_done.done(u))
                if u.past(2):
                    act.wait_ge(vals_done.sem, vals_done.done(u - 2))
                    act.wait_ge(vals_dve_done.sem, vals_dve_done.done(u - 2))
                act.activation(sine[:, u.par, :, :], turn[:, :, :], ACT.Sin, scale=PI).then_inc(sine_done.sem, 1)
                act.wait_ge(turn_abs_done.sem, turn_abs_done.done(u))
                act.activation(cosine[:, u.par, :, :], turn_abs[:, :, :], ACT.Sin, bias=k.col[:, C_PIH:C_PIH + 1], scale=-PI)\
                   .then_inc(cosine_done.sem, 1)

            def log_amplitude(u):
                act.wait_ge(exp_done.sem, exp_done.done(u))
                if u.past(1):
                    act.wait_ge(amp_done.sem, amp_done.done(u - 1))
                act.activation(logs[:, :, :], mag[:, :, :], ACT.Ln, bias=1.0).then_inc(log_done.sem, 1)

            def log_mean(u):
                act.wait_ge(mean_ps.sem, mean_ps.done(u))
                if u.past(1):
                    act.wait_ge(amp_n_done.sem, amp_n_done.done(u - 1))
                act.activation(inv[:, :, :], ps[:, MS:MS + 2, :], ACT.Ln, bias=k.col[:, C_EPS:C_EPS + 1])\
                   .then_inc(mean_log.sem, 1)

            def copy_turned(t):
                act.wait_ge(x_turned.sem, x_turned.done(t))
                if t.past(1):
                    act.wait_ge(v_proj.sem, v_proj.done(t - 1))
                    act.wait_ge(projected.sem, projected.done(t - 1))
                act.copy(xnT[:, :], ps[:, XV, :]).then_inc(xT_ready.sem, 1)

            def step(t):
                if layer == 1:
                    if active(t, 0, B):
                        if t.past(2):
                            act.wait_ge(x_turned.sem, x_turned.done(t - 2))
                        act.copy(xn[:, t.par, :, :], k.y[:, bass.ds(t.n * QT, QT), :]).then_inc(xn_done.sem, 1)
                        copy_turned(t)
                    if active(t, 1, B):
                        u = t - 1
                        act.wait_ge(projected.sem, projected.done(u))
                        if u.past(1):
                            act.wait_ge(rest_done.sem, rest_done.done(u - 1))
                        act.activation(vals[:, 1, 0, :], ps[:, AMP + 1, :], ACT.Identity, bias=k.col[:, C_K1:C_K1 + 1])\
                           .then_inc(vals_done.sem, 1)
                    return
                if active(t, 3, B):
                    act.wait_ge(mean_log.sem, mean_log.done(t - 3))
                    inverse(t - 3)
                if active(t, 1, B):
                    tanh_and_exp(t - 1)
                if active(t, 2, B):
                    square_amplitude(t - 2)
                if active(t, 0, B):
                    copy_turned(t)
                if active(t, 1, B):
                    log_amplitude(t - 1)
                if active(t, 2, B):
                    log_mean(t - 2)
                if active(t, 1, B):
                    sine_and_cosine(t - 1)

            in_steps(act, B, DEPTH, step, 2, FIRST)

        @block.tensor
        def _(pe):
            def step(t):
                if active(t, 0, B):
                    pe.wait_ge(xn_done.sem, xn_done.done(t))
                    if t.past(1):
                        pe.wait_ge(v_ready.sem, v_ready.done(t - 1))
                    for j in range(QT):
                        mm = pe.transpose(ps[:, XV, j * P:(j + 1) * P], xn[:, t.par, j, :], k.ident[:, :])
                    mm.then_inc(x_turned.sem, 1)
                if active(t, 2, B) and layer == 0:
                    u = t - 2
                    pe.wait_ge(square_done.sem, square_done.done(u))
                    if u.past(1):
                        pe.wait_ge(mean_log.sem, mean_log.done(u - 1))
                    for side in range(2):
                        mm = pe.matmul(ps[:, MS + side, :], k.head_mean[:, :], square[:, side, :], start=True, stop=True)
                    mm.then_inc(mean_ps.sem, 1)
                if active(t, 0, B):
                    pe.wait_ge(xT_ready.sem, xT_ready.done(t))
                    for j in range(QT):
                        mm = pe.matmul(ps[:, XV, j * P:(j + 1) * P], xnT[:, j * P:(j + 1) * P], k.wT[:, w_v, :],
                                       start=True, stop=True)
                    mm.then_inc(v_proj.sem, 1)
                    if layer == 0:
                        if t.past(1):
                            pe.wait_ge(tanh_done.sem, tanh_done.done(t - 1))
                        pe.matmul(ps[:, PHI, :], k.wT[:, W_QP, :], xnT[:, :], start=True, stop=True)
                        pe.matmul(ps[:, PHI + 1, :], k.wT[:, W_KP, :], xnT[:, :], start=True, stop=True)\
                          .then_inc(phases_ps.sem, 1)
                if active(t, 0, B):
                    if t.past(1):
                        if layer == 0:
                            pe.wait_ge(amp_done.sem, amp_done.done(t - 1))
                        else:
                            pe.wait_ge(vals_done.sem, vals_done.done(t - 1))
                            pe.wait_ge(vals_dve_done.sem, vals_dve_done.done(t - 1))
                    pe.matmul(ps[:, AMP, :], k.wT[:, w_q, :], xnT[:, :], start=True, stop=True)
                    pe.matmul(ps[:, AMP + 1, :], k.wT[:, w_k, :], xnT[:, :], start=True, stop=True)\
                      .then_inc(projected.sem, 1)

            in_steps(pe, B, DEPTH, step, 2, FIRST)

        @block.vector
        def _(dve):
            def absolute_turn(u):
                dve.wait_ge(tanh_done.sem, tanh_done.done(u))
                if u.past(1):
                    dve.wait_ge(cosine_done.sem, cosine_done.done(u - 1))
                dve.scalar_tensor_tensor(out=turn_abs[:, :, :], in0=turn[:, :, :], scalar=-1.0, in1=turn[:, :, :],
                                         op0=ALU.mult, op1=ALU.max).then_inc(turn_abs_done.sem, 1)

            def amplitude(u):
                dve.wait_ge(log_done.sem, log_done.done(u))
                dve.scalar_tensor_tensor(out=amp[:, u.par, :, :], in0=ps[:, AMP:AMP + 2, :], scalar=0.0, in1=logs[:, :, :],
                                         op0=ALU.max, op1=ALU.add).then_inc(amp_done.sem, 1)

            def normalise(u):
                dve.wait_ge(inv_done.sem, inv_done.done(u))
                if u.past(1):
                    dve.wait_ge(vals_done.sem, vals_done.done(u - 1))
                dve.scalar_tensor_tensor(out=amp_n[:, 0, :], in0=amp[:, u.par, 0, :], scalar=k.hscale[:, :], in1=inv[:, 0, :],
                                         op0=ALU.mult, op1=ALU.mult).then_inc(amp_n_done.sem, 1)
                dve.tensor_tensor(amp_n[:, 1, :], amp[:, u.par, 1, :], inv[:, 1, :], ALU.mult).then_inc(amp_n_done.sem, 1)

            def cosine_products(u):
                dve.wait_ge(amp_n_done.sem, amp_n_done.done(u))
                if u.past(1):
                    dve.wait_ge(rest_done.sem, rest_done.done(u - 1))
                dve.tensor_tensor(vals[:, :, 0, :], amp_n[:, :, :], cosine[:, u.par, :, :], ALU.mult).then_inc(vals_dve_done.sem, 1)

            def flat(u, which):
                return parts[:, u.par, :, which, :, :].rearrange("p s c t -> p s (c t)")

            value = vals[:, :, :, :].rearrange("p s c t -> p s (c t)")
            left = rest[:, :, :, :].rearrange("p s c t -> p s (c t)")

            def split_high(u):
                dve.wait_ge(vals_done.sem, vals_done.done(u))
                dve.wait_ge(vals_dve_done.sem, vals_dve_done.done(u))
                if u.past(2):
                    dve.wait_ge(stacked[u.par].sem, stacked[u.par].done((u - 2).pair))
                dve.tensor_copy(flat(u, 0), value).then_inc(high_done.sem, 1)
                dve.wait_ge(high_done.sem, high_done.done(u))
                dve.tensor_tensor(left, value, flat(u, 0), ALU.subtract).then_inc(rest_done.sem, 1)

            def split_rest(u):
                dve.wait_ge(rest_done.sem, rest_done.done(u))
                dve.tensor_copy(flat(u, 1), left).then_inc(mid_done.sem, 1)
                dve.wait_ge(mid_done.sem, mid_done.done(u))
                dve.tensor_tensor(flat(u, 2), left, flat(u, 1), ALU.subtract).then_inc(low_done.sem, 1)

            def keep_values(t):
                dve.wait_ge(v_proj.sem, v_proj.done(t))
                v_out = k.v_all[:, bass.ds(t.n, 1), :, :].rearrange("p b j d -> p (b j) d")
                v_ps = ps[:, XV, :].rearrange("p (j d) -> p j d", j=QT)
                if layer == 0:
                    dve.tensor_copy(v_out, v_ps).then_inc(v_ready.sem, 1)
                else:
                    dve.tensor_tensor(v_out, v_ps, wide(k.row[:, R_V1, :]), ALU.add).then_inc(v_ready.sem, 1)

            def step(t):
                if layer == 0:
                    if active(t, 0, B):
                        dve.wait_ge(x_in[t.par].sem, (t.pair + 1) * 16)
                        ln_stats(dve, x_tile[:, t.par, :, :], stats, mv, stats_done, mv_done, t)
                    if active(t, 3, B):
                        normalise(t - 3)
                    if active(t, 0, B):
                        ln_apply(dve, xn[:, t.par, :, :], x_tile[:, t.par, :, :], mv, rstd, rstd_done, xn_done, t)
                    if active(t, 1, B):
                        absolute_turn(t - 1)
                    if active(t, 3, B):
                        cosine_products(t - 3)
                elif active(t, 1, B):
                    dve.wait_ge(projected.sem, projected.done(t - 1))
                    dve.tensor_scalar(vals[:, 0, 0, :], ps[:, AMP, :], k.col[:, C_Q1:C_Q1 + 1], float(HD) ** -0.5,
                                      ALU.add, ALU.mult).then_inc(vals_dve_done.sem, 1)
                if active(t, SPLIT, B):
                    split_high(t - SPLIT)
                if layer == 0 and active(t, 1, B):
                    amplitude(t - 1)
                if active(t, 0, B):
                    keep_values(t)
                if active(t, SPLIT, B):
                    split_rest(t - SPLIT)

            in_steps(dve, B, DEPTH, step, 2, FIRST)


def prepare0(nc, k):
    prepare(nc, k, 0)


def route_and_prepare1(nc, k):
    with nc.sbuf_tensor("scaled", [P, 2, NT, D], F32) as k.scaled:
        route(nc, k, 1)
        prepare(nc, k, 1)




def route(nc, k, layer):
    COPIES = layer + 1
    W = COPIES * NT
    TL = TILES[layer]
    MOST = T // ROWS
    with ExitStack() as ctx:
        sb, banks, signal = phase_resources(nc, ctx, f"route{layer}")
        best = sb("best", [P, NT])
        ties = sb("ties", [P, NT, E])
        first = sb("first", [P, NT])
        left = sb("left", [P, NT, E])
        second = sb("second", [P, NT])
        onehot = sb("onehot", [P, W, E])
        weight = sb("weight", [P, E])
        counts = sb("counts", [P, E, W])
        keep = sb("keep", [P, E, W])
        prefix = sb("prefix", [P, E, W])
        total = sb("total", [P, E])
        filled = sb("filled", [P, E, MOST])
        tiles = sb("tiles", [P, E])
        tiles_to = sb("tiles_to", [P, E])
        start = sb("start", [P, E])
        offset = sb("offset", [P, E, W])
        row_of = sb("row_of", [P, W, E])
        row_f = sb("row_f", [P, W])
        passed = sb("passed", [P, TL, E])
        expert_f = sb("expert_f", [P, TL])
        probs = sb("probs", [P, NT, E])
        denom = sb("denom", [P, NT])
        share = sb("share", [P, COPIES, NT])
        ps = banks("route_ps", 2)
        dve_step = signal("dve_step")
        onehot_done, ranked = signal("onehot_done"), signal("ranked")
        minus_best, probs_exp, share_ready = signal("minus_best"), signal("probs_exp"), signal("share_ready")
        block = ctx.enter_context(nc.Block())

        def per_token(column):
            return column.unsqueeze(2).broadcast_to([P, NT, E])

        @block.tensor
        def _(pe):
            pe.wait_ge(onehot_done.sem, 1)
            flat = onehot[:, :, :].rearrange("p w e -> p (w e)")
            pe.matmul(ps[:, 0, 0:W * E], k.before[:, :], flat, start=True, stop=True)
            pe.matmul(ps[:, 1, 0:W * E], k.ones[:, :], flat, start=True, stop=True).then_inc(ranked.sem, 1)

        @block.scalar
        def _(act):
            if layer == 1:
                act.wait_ge(minus_best.sem, 1)
                act.activation(probs[:, :, :], probs[:, :, :], ACT.Exp).then_inc(probs_exp.sem, 1)
                act.wait_ge(share_ready.sem, 1)
                for t in range(NT):
                    act.activation(k.scaled[:, 0, t, :], k.y[:, t, :], ACT.Identity, scale=share[:, 0, t:t + 1])

        @block.gpsimd
        def _(pool):
            if layer == 1:
                pool.wait_ge(share_ready.sem, 2)
                pool.tensor_tensor(k.scaled[:, 1, :, :], k.y[:, :, :], share[:, 1, :].unsqueeze(2).broadcast_to([P, NT, D]),
                                   ALU.mult)

        @block.vector
        def _(dve):
            steps = [0]

            def then(instruction):
                steps[0] += 1
                instruction.then_inc(dve_step.sem, 1)
                dve.wait_ge(dve_step.sem, steps[0])

            def choose(logits, best_, hot):
                then(dve.tensor_reduce(best_, logits, X_AXIS, ALU.max))
                then(dve.tensor_tensor(ties[:, :, :], logits, per_token(best_), ALU.is_equal))
                then(dve.tensor_tensor(ties[:, :, :], ties[:, :, :], weight[:, :].unsqueeze(1).broadcast_to([P, NT, E]),
                                       ALU.mult))
                then(dve.tensor_reduce(first[:, :], ties[:, :, :], X_AXIS, ALU.max))
                return dve.tensor_tensor(hot, ties[:, :, :], per_token(first[:, :]), ALU.is_equal)

            then(dve.tensor_scalar(weight[:, :], k.counted[:, 0:E], -1.0, float(E), ALU.mult, ALU.add))
            if layer == 0:
                choose(k.logits[:, :, :], best[:, :], onehot[:, 0:NT, :]).then_inc(onehot_done.sem, 1)
                dve.wait_ge(onehot_done.sem, 1)
            else:
                then(choose(k.logits[:, :, :], best[:, :], onehot[:, 0:NT, :]))
                dve.tensor_tensor(probs[:, :, :], k.logits[:, :, :], per_token(best[:, :]), ALU.subtract)\
                   .then_inc(minus_best.sem, 1)
                then(dve.scalar_tensor_tensor(out=left[:, :, :], in0=onehot[:, 0:NT, :], scalar=NEG, in1=k.logits[:, :, :],
                                              op0=ALU.mult, op1=ALU.add))
                choose(left[:, :, :], second[:, :], onehot[:, NT:W, :]).then_inc(onehot_done.sem, 1)
                dve.wait_ge(probs_exp.sem, 1)
                dve.wait_ge(onehot_done.sem, 1)
                then(dve.tensor_reduce(denom[:, :], probs[:, :, :], X_AXIS, ALU.add))
                then(dve.reciprocal(denom[:, :], denom[:, :]))
                for c in range(2):
                    then(dve.tensor_tensor(ties[:, :, :], probs[:, :, :], onehot[:, c * NT:(c + 1) * NT, :], ALU.mult))
                    then(dve.tensor_reduce(share[:, c, :], ties[:, :, :], X_AXIS, ALU.add))
                    dve.tensor_tensor(share[:, c, :], share[:, c, :], denom[:, :], ALU.mult).then_inc(share_ready.sem, 1)
            then(dve.memset(keep[:, :, :], 1.0))
            then(dve.memset(keep[:, :, 0:1], 0.0))
            dve.wait_ge(ranked.sem, 1)
            then(dve.tensor_copy(counts[:, :, :], ps[:, 1, 0:W * E].rearrange("p (w e) -> p e w", e=E)))
            then(dve.tensor_tensor_scan(prefix[:, :, :].rearrange("p e w -> p (e w)"),
                                        keep[:, :, :].rearrange("p e w -> p (e w)"),
                                        counts[:, :, :].rearrange("p e w -> p (e w)"), 0.0, ALU.mult, ALU.add))
            then(dve.tensor_copy(total[:, :], prefix[:, :, W - 1]))
            then(dve.scalar_tensor_tensor(out=filled[:, :, :], in0=k.counted[:, 0:MOST].unsqueeze(1).broadcast_to([P, E, MOST]),
                                          scalar=float(ROWS), in1=total[:, :].unsqueeze(2).broadcast_to([P, E, MOST]),
                                          op0=ALU.mult, op1=ALU.is_lt))
            then(dve.tensor_reduce(tiles[:, :], filled[:, :, :], X_AXIS, ALU.add))
            then(dve.tensor_tensor_scan(tiles_to[:, :], k.ones[:, 0:E], tiles[:, :], 0.0, ALU.mult, ALU.add))
            then(dve.tensor_tensor(start[:, :], tiles_to[:, :], tiles[:, :], ALU.subtract))
            then(dve.tensor_tensor(offset[:, :, :], prefix[:, :, :], counts[:, :, :], ALU.subtract))
            then(dve.scalar_tensor_tensor(out=offset[:, :, :], in0=start[:, :].unsqueeze(2).broadcast_to([P, E, W]),
                                          scalar=float(ROWS), in1=offset[:, :, :], op0=ALU.mult, op1=ALU.add))
            then(dve.tensor_tensor(row_of[:, :, :], ps[:, 0, 0:W * E].rearrange("p (w e) -> p w e", e=E),
                                   offset[:, :, :].rearrange("p e w -> p w e"), ALU.add))
            then(dve.tensor_tensor(row_of[:, :, :], row_of[:, :, :], onehot[:, :, :], ALU.mult))
            then(dve.tensor_reduce(row_f[:, :], row_of[:, :, :], X_AXIS, ALU.add))
            then(dve.tensor_copy(k.rank_row[:, 0:W], row_f[:, :]))
            then(dve.tensor_tensor(passed[:, :, :], tiles_to[:, :].unsqueeze(1).broadcast_to([P, TL, E]),
                                   k.counted[:, 0:TL].unsqueeze(2).broadcast_to([P, TL, E]), ALU.is_le))
            then(dve.tensor_reduce(expert_f[:, :], passed[:, :, :], X_AXIS, ALU.add))
            then(dve.tensor_scalar(expert_f[:, :], expert_f[:, :], float(E - 1), None, ALU.min))
            then(dve.tensor_copy(k.tile_expert[:, 0:TL], expert_f[:, :]))


def route0(nc, k):
    route(nc, k, 0)




def experts(nc, k, layer):
    TL = TILES[layer]
    HC = DF // P if layer == 0 else 3
    size = [P] * HC if layer == 0 else [P, P, HID - 2 * P]
    src, dst = ((k.sorted0, k.done0), (k.sorted1, k.done1))[layer]
    LOADS = 5
    RING = 4
    with ExitStack() as ctx:
        sb, banks, signal = phase_resources(nc, ctx, f"experts{layer}")
        rows = sb("rows", [P, RING, 2, D])
        rowsT = sb("rowsT", [P, 2, ROWS])
        w_in = sb("w_in", [P, RING, DF if layer == 0 else 2 * HID])
        w_out = sb("w_out", [P, RING, HC, D])
        b_in = sb("b_in", [P, RING, HC])
        b_out = sb("b_out", [P, RING, D])
        hidden = sb("hidden", [P, 2, HC, ROWS])
        gate = sb("gate", [P, HC, ROWS])
        result = sb("result", [P, RING, 2, D])
        ps = banks("experts_ps", 8)
        TURN, OUT = 0, 7

        def hidden_bank(u, n):
            return 1 + 3 * u.par + n

        loaded = [signal(f"loaded{i}", LOADS, 16) for i in range(RING)]
        turned, rowsT_ready, hidden_ps, out_ps, result_done = (signal(x) for x in ("turned", "rowsT_ready", "hidden_ps", "out_ps", "result_done"))
        hidden_act, hidden_dve = signal("hidden_act", 2), signal("hidden_dve", 2)
        stored = [signal(f"stored{i}", by=16) for i in range(RING)]
        DEPTH = 3
        block = ctx.enter_context(nc.Block())

        @block.sync
        def _(sp):
            def load(u):
                if u.past(RING):
                    sp.wait_ge(out_ps.sem, out_ps.done(u - RING))
                    if layer == 0:
                        sp.wait_ge(result_done.sem, result_done.done(u - RING))
                e = sp.value_load(k.tile_expert[0:1, bass.ds(u.n, 1)], min_val=0, max_val=E - 1)
                done = loaded[u.phase].sem
                sp.dma_start(rows[:, u.phase, :, :], src[bass.ds(u.n * ROWS, ROWS), :].rearrange("(a p) d -> p a d", p=P))\
                  .then_inc(done, 16)
                one = bass.ds(e, 1)
                if layer == 0:
                    sp.dma_start(w_in[:, u.phase, :], k.arg["L0_ffn_W1"][one, :, :].rearrange("e d f -> (e d) f")).then_inc(done, 16)
                    sp.dma_start(b_in[:, u.phase, :], k.arg["L0_ffn_b1"][one, :].rearrange("e (p c) -> (e p) c", p=P))\
                      .then_inc(done, 16)
                    sp.dma_start(w_out[:, u.phase, :, :], k.arg["L0_ffn_W2"][one, :, :].rearrange("e (p c) d -> (e p) c d", p=P))\
                      .then_inc(done, 16)
                    sp.dma_start(b_out[:, u.phase, :], k.arg["L0_ffn_b2"][one, :].rearrange("e d -> (e d)").rearrange("(o d) -> o d", o=1)
                                 .partition_broadcast(P)).then_inc(done, 16)
                else:
                    sp.dma_start(w_in[:, u.phase, 0:HID], k.arg["L1_ffn_w1"][one, :, :].rearrange("e d f -> (e d) f")).then_inc(done, 16)
                    sp.dma_start(w_in[:, u.phase, HID:2 * HID], k.arg["L1_ffn_w3"][one, :, :].rearrange("e d f -> (e d) f"))\
                      .then_inc(done, 16)
                    sp.dma_start(w_out[:, u.phase, 0:2, :], k.arg["L1_ffn_w2"][one, 0:2 * P, :].rearrange("e (c p) d -> p (e c) d", p=P))\
                      .then_inc(done, 16)
                    sp.dma_start(w_out[0:size[2], u.phase, 2, :], k.arg["L1_ffn_w2"][one, 2 * P:HID, :].rearrange("e f d -> (e f) d"))\
                      .then_inc(done, 16)

            def store(u):
                sp.wait_ge(result_done.sem, result_done.done(u))
                sp.dma_start(dst[bass.ds(u.n * ROWS, ROWS), :].rearrange("(a p) d -> p a d", p=P), result[:, u.phase, :, :])\
                  .then_inc(stored[u.phase].sem, 16)

            def step(t):
                if active(t, 0, TL):
                    load(t)
                if active(t, 5, TL):
                    store(t - 5)

            in_steps(sp, TL, 6, step, RING, 2 * RING)
            for i in range(RING):
                sp.wait_ge(stored[i].sem, (TL + RING - 1 - i) // RING * 16)

        @block.scalar
        def _(act):
            def step(t):
                if active(t, 1, TL):
                    u = t - 1
                    act.wait_ge(hidden_ps.sem, hidden_ps.done(u))
                    if layer == 0:
                        if u.past(2):
                            act.wait_ge(out_ps.sem, out_ps.done(u - 2))
                        for c in range(2):
                            act.activation(hidden[:, u.par, c, :], ps[:, hidden_bank(u, 0), c * ROWS:(c + 1) * ROWS], ACT.Relu,
                                           bias=b_in[:, u.phase, c:c + 1]).then_inc(hidden_act.sem, 1)
                    else:
                        if u.past(1):
                            act.wait_ge(hidden_dve.sem, hidden_dve.done(u - 1))
                        act.activation(gate[:, 0:2, :], ps[:, hidden_bank(u, 0), :].rearrange("p (c r) -> p c r", c=2), ACT.Silu)\
                           .then_inc(hidden_act.sem, 1)
                        act.activation(gate[0:size[2], 2, :], ps[0:size[2], hidden_bank(u, 2), 0:ROWS], ACT.Silu)\
                           .then_inc(hidden_act.sem, 1)
                if active(t, 0, TL):
                    act.wait_ge(turned.sem, turned.done(t))
                    if t.past(2):
                        act.wait_ge(hidden_ps.sem, hidden_ps.done(t - 2))
                    act.copy(rowsT[:, t.par, :], ps[:, TURN, 0:ROWS]).then_inc(rowsT_ready.sem, 1)

            in_steps(act, TL, DEPTH, step, RING, 2 * RING)

        @block.vector
        def _(dve):
            def step(t):
                if active(t, 1, TL):
                    u = t - 1
                    dve.wait_ge(hidden_ps.sem, hidden_ps.done(u))
                    if u.past(2):
                        dve.wait_ge(out_ps.sem, out_ps.done(u - 2))
                    if layer == 0:
                        for c in range(2, 4):
                            dve.tensor_scalar(hidden[:, u.par, c, :], ps[:, hidden_bank(u, 1), (c - 2) * ROWS:(c - 1) * ROWS],
                                              b_in[:, u.phase, c:c + 1], 0.0, ALU.add, ALU.max).then_inc(hidden_dve.sem, 1)
                    else:
                        dve.wait_ge(hidden_act.sem, hidden_act.after(u, 0))
                        dve.tensor_tensor(hidden[:, u.par, 0:2, :], ps[:, hidden_bank(u, 1), :].rearrange("p (c r) -> p c r", c=2),
                                          gate[:, 0:2, :], ALU.mult).then_inc(hidden_dve.sem, 1)
                        dve.wait_ge(hidden_act.sem, hidden_act.after(u, 1))
                        dve.tensor_tensor(hidden[0:size[2], u.par, 2, :], ps[0:size[2], hidden_bank(u, 2), ROWS:2 * ROWS],
                                          gate[0:size[2], 2, :], ALU.mult).then_inc(hidden_dve.sem, 1)
                if active(t, 2, TL):
                    u = t - 2
                    dve.wait_ge(out_ps.sem, out_ps.done(u))
                    if u.past(RING):
                        dve.wait_ge(stored[u.phase].sem, u.turn * 16)
                    out = ps[:, OUT, 0:2 * D].rearrange("p (a d) -> p a d", a=2)
                    if layer == 0:
                        dve.tensor_tensor(result[:, u.phase, :, :], out, b_out[:, u.phase, :].unsqueeze(1).broadcast_to([P, 2, D]),
                                          ALU.add).then_inc(result_done.sem, 1)
                    else:
                        dve.tensor_copy(result[:, u.phase, :, :], out).then_inc(result_done.sem, 1)

            in_steps(dve, TL, DEPTH, step, RING, 2 * RING)

        @block.tensor
        def _(pe):
            def turn(u):
                pe.wait_ge(loaded[u.phase].sem, (u.turn + 1) * (LOADS * 16))
                if u.past(1):
                    pe.wait_ge(rowsT_ready.sem, rowsT_ready.done(u - 1))
                for a in range(2):
                    mm = pe.transpose(ps[:, TURN, a * P:(a + 1) * P], rows[:, u.phase, a, :], k.ident[:, :])
                mm.then_inc(turned.sem, 1)

            def into_hidden(u):
                pe.wait_ge(rowsT_ready.sem, rowsT_ready.done(u))
                if u.past(2):
                    pe.wait_ge(hidden_act.sem, hidden_act.done(u - 2))
                    pe.wait_ge(hidden_dve.sem, hidden_dve.done(u - 2))
                if layer == 0:
                    for c in range(HC):
                        mm = pe.matmul(ps[:, hidden_bank(u, c // 2), c % 2 * ROWS:(c % 2 + 1) * ROWS],
                                       w_in[:, u.phase, c:DF:HC], rowsT[:, u.par, :], start=True, stop=True)
                else:
                    for side, w in enumerate((0, HID)):
                        for c in range(HC):
                            bank, half = (side, c) if c < 2 else (2, side)
                            mm = pe.matmul(ps[0:size[c], hidden_bank(u, bank), half * ROWS:(half + 1) * ROWS],
                                           w_in[:, u.phase, w + c * P:w + c * P + size[c]], rowsT[:, u.par, :],
                                           start=True, stop=True)
                mm.then_inc(hidden_ps.sem, 1)

            def out_of_hidden(u):
                pe.wait_ge(hidden_act.sem, hidden_act.done(u))
                pe.wait_ge(hidden_dve.sem, hidden_dve.done(u))
                if u.past(1):
                    pe.wait_ge(result_done.sem, result_done.done(u - 1))
                for a in range(2):
                    for c in range(HC):
                        mm = pe.matmul(ps[:, OUT, a * D:(a + 1) * D], hidden[0:size[c], u.par, c, a * P:(a + 1) * P],
                                       w_out[0:size[c], u.phase, c, :], start=(c == 0), stop=(c == HC - 1))
                mm.then_inc(out_ps.sem, 1)

            def step(t):
                if active(t, 1, TL):
                    into_hidden(t - 1)
                if active(t, 0, TL):
                    turn(t)
                if active(t, 2, TL):
                    out_of_hidden(t - 2)

            in_steps(pe, TL, DEPTH, step, RING, 2 * RING)


def experts0(nc, k):
    experts(nc, k, 0)


def experts1(nc, k):
    experts(nc, k, 1)




def attend(nc, k, layer):
    ROWS_S = (K0, K1)[layer]
    ROWS_K = K0
    ROWS_A = ROWS_K + 3
    UNITS = B * NG
    RING = 4
    MCH, SCH = 10, 5
    stacks = ((k.q_stack, k.k_stack), (k.q_stack1, k.k_stack1))[layer]
    w_o = (W_O0, W_O1)[layer]
    with ExitStack() as ctx:
        sb, banks, signal = phase_resources(nc, ctx, f"attend{layer}")
        q = sb("q", [P, RING, GH, S], BF16)
        ks = sb("ks", [P, RING, GH, S], BF16)
        moe = sb("moe", [P, (layer + 1) * NT, D])
        neg_max = sb("neg_max", [P, 2, GH, QT])
        rest = sb("rest", [P, GH * QT])
        max_parts = sb("max_parts", [P, 2, 3, GH * QT], BF16)
        maxT = sb("maxT", [3 * GH * QT, 2, P], BF16)
        probs = sb("probs", [P, 2, 2 * SCH, S])
        vals = sb("vals", [P, 2, QT * GH, 32])
        mixT = sb("mixT", [P, S])
        inv = sb("inv", [P, QT * GH])
        context = sb("context", [P, 2, QT, D])
        contextT = sb("contextT", [P, S])
        x_tile = sb("x_tile", [P, 2, QT, D]) if layer == 0 else None
        ps = banks("attend_ps", 8)
        MAXB, PROB, MIX, TURN = 0, 2, 6, 7

        loaded = [signal(f"loaded{i}", 2, 16) for i in range(RING)]
        preset = signal("preset")
        filled = [signal(f"filled{i}") for i in range(RING)]
        vals_ready = signal("vals_ready")
        scored, maxed = signal("scored", MCH), signal("maxed", MCH)
        high_done, rest_done, mid_done, parts_done = (signal(x) for x in ("high_done", "rest_done", "mid_done", "parts_done"))
        max_turned, maxT_ready = signal("max_turned"), signal("maxT_ready")
        max_in = [signal(f"max_in{i}", by=16) for i in range(2)]
        prob_ps, exped, masked = signal("prob_ps", SCH), signal("exped", SCH), signal("masked", 2 * QT)
        mixed, mixT_ready, mix_turned, inv_done, context_done = (signal(x) for x in ("mixed", "mixT_ready", "mix_turned", "inv_done", "context_done"))
        context_turned, contextT_ready, projected, added = (signal(x) for x in ("context_turned", "contextT_ready", "projected", "added"))
        x_in = [signal(f"x_in{i}", by=16) for i in range(2)]
        joined = signal("joined", 3)
        if layer == 0:
            z_sum, z_norm, z_gain = sb("z_sum", [P, QT, D]), sb("z_norm", [P, QT, D]), sb("z_gain", [P, QT, D])
            z_tile = sb("z_tile", [P, 2, QT, D])
            z_stats, z_mv, z_ve, z_rstd = sb("z_stats", [P, QT, 7]), sb("z_mv", [P, QT, 2]), sb("z_ve", [P, QT]), sb("z_rstd", [P, QT])
            z_summed, z_stats_done, z_mv_done, z_eps_done = signal("z_summed"), signal("z_stats_done", QT), signal("z_mv_done", QT), signal("z_eps_done")
            z_rstd_done, z_normed, z_scaled, z_ready = signal("z_rstd_done"), signal("z_normed", QT), signal("z_scaled"), signal("z_ready")
            z_stored = [signal(f"z_stored{i}", QT, 16) for i in range(2)]
        gathered = k.gathered[layer]
        stored = [signal(f"stored{i}", by=16) for i in range(2)]
        DEPTH = 6
        Z_AFTER = 10
        block = ctx.enter_context(nc.Block())

        def max_chunk(c):
            pair, kind = divmod(c, 5)
            h = 2 * pair + kind // 2
            if kind == 4:
                return [(2 * pair, 1, 0), (2 * pair + 1, 1, 256)]
            return [(h, 3, 0)] if kind % 2 == 0 else [(h, 2, 0), (h, 0, 384)]

        def prob_bank(n):
            pair, kind = divmod(n, 5)
            h = 2 * pair + kind // 2
            if kind == 4:
                return [(2 * pair, 2, 0), (2 * pair + 1, 2, 256)]
            return [(h, 0, 0)] if kind % 2 == 0 else [(h, 1, 0), (h, 3, 384)]

        prob_place = {(h, kt): (n, col) for n in range(2 * SCH) for h, kt, col in prob_bank(n)}

        def fill_slot(eng, i):
            if layer == 1:
                eng.memset(q[0:ROWS_A, i, :, :], 0.0)
            eng.memset(ks[0:ROWS_A, i, :, :], 1.0).then_inc(filled[i].sem, 1)

        @block.sync
        def _(sp):
            def step(t):
                if active(t, 0, UNITS):
                    if t.past(RING):
                        sp.wait_ge(prob_ps.sem, prob_ps.done(t - RING))
                    else:
                        sp.wait_ge(filled[t.phase].sem, 1)
                    for side, dst in enumerate((q, ks)):
                        src = stacks[side][bass.ds(t.row, 1), t.group * GH:(t.group + 1) * GH, :, :]
                        sp.dma_start(dst[0:ROWS_S, t.group, :, :], src.rearrange("b h r t -> r (b h) t"))\
                          .then_inc(loaded[t.group].sem, 16)
                    if t.group == 2 and layer == 0:
                        if t.past(2 * NG):
                            sp.wait_ge(added.sem, added.done(t.row - 2))
                        sp.dma_start(x_tile[:, t.row_par, :, :],
                                     k.x_flat[bass.ds(t.row, 1), :, :].rearrange("b (j p) d -> p (b j) d", p=P))\
                          .then_inc(x_in[t.row_par].sem, 16)
                if active(t, 2, UNITS):
                    u = t - 2
                    sp.wait_ge(maxT_ready.sem, maxT_ready.done(u))
                    sp.dma_start(q[ROWS_K:ROWS_A, u.group, :, :], maxT[:, u.par, :]).then_inc(max_in[u.par].sem, 16)
                if layer == 0 and active(t, Z_AFTER, UNITS):
                    u = t - Z_AFTER
                    if u.group == 0:
                        sp.wait_ge(z_ready.sem, z_ready.done(u.row))
                    sp.dma_start(k.z[:, bass.ds((u.row * QT + u.group) * POS, POS), :], z_tile[:, u.row_par, u.group, :])\
                      .then_inc(z_stored[u.row_par].sem, 16)
                if layer == 1 and active(t, 6, UNITS) and (t - 6).group == NG - 1:
                    u = t - 6
                    sp.wait_ge(added.sem, added.done(u.row))
                    sp.dma_start(k.out[bass.ds(u.row, 1), :, :].rearrange("b (j p) d -> p (b j) d", p=P),
                                 k.x_sum[:, bass.ds(u.row * QT, QT), :]).then_inc(stored[u.row_par].sem, 16)

            if layer == 0:
                in_steps(sp, UNITS, Z_AFTER + 1, step, 2 * NG, 4 * NG)
            else:
                in_steps(sp, UNITS, DEPTH + 1, step, 2 * NG, 2 * NG)
            if layer == 1:
                for i in range(2):
                    sp.wait_ge(stored[i].sem, B // 2 * 16)
            else:
                for done in z_stored:
                    sp.wait_ge(done.sem, done.done(B // 2 - 1))

        @block.gpsimd
        def _(pool):
            for i in range(1, RING):
                fill_slot(pool, i)
            pool.memset(vals[:, :, :, :], 0.0).then_inc(preset.sem, 1)
            pool.wait_ge(preset.sem, 1)
            pool.memset(vals[:, :, :, HD:HD + 1], 1.0).then_inc(preset.sem, 1)
            pool.wait_ge(preset.sem, 2)
            src = (k.done0, k.done1)[layer]

            def second_norm(r):
                here = slice(r * QT, (r + 1) * QT)
                for i in range(4):
                    pool.wait_ge(gathered[i].sem, (r + 1) * 16)
                if r >= 1:
                    pool.wait_ge(z_normed.sem, z_normed.done(r - 1))
                pool.tensor_tensor(z_sum[:, :, :], k.y[:, here, :], moe[:, here, :], ALU.add).then_inc(z_summed.sem, 1)
                ln_rstd(pool, k, z_mv, z_ve, z_rstd, z_mv_done, z_eps_done, z_rstd_done, r)

            def second_gain(r):
                pool.wait_ge(z_normed.sem, z_normed.done(r))
                pool.tensor_tensor(z_gain[:, :, :], z_norm[:, :, :], wide(k.row[:, R_G2, :]), ALU.mult).then_inc(z_scaled.sem, 1)
                pool.wait_ge(z_scaled.sem, z_scaled.done(r))
                if r >= 2:
                    pool.wait_ge(z_stored[r % 2].sem, z_stored[r % 2].done(r // 2 - 1))
                pool.tensor_tensor(z_tile[:, r % 2, :, :], z_gain[:, :, :], wide(k.row[:, R_BE2, :]), ALU.add).then_inc(z_ready.sem, 1)

            def join_branches(r):
                here = slice(r * QT, (r + 1) * QT)
                for i in range(4):
                    pool.wait_ge(gathered[i].sem, (r + 1) * 32)
                for n, term in enumerate((wide(k.row[:, R_O1, :]), moe[:, here, :], moe[:, r * QT + NT:(r + 1) * QT + NT, :])):
                    if n:
                        pool.wait_ge(joined.sem, joined.after(r, n - 1))
                    pool.tensor_tensor(k.x_sum[:, here, :], k.x_sum[:, here, :], term, ALU.add).then_inc(joined.sem, 1)

            def mask(n):
                for pair in range(2):
                    pool.wait_ge(exped.sem, exped.after(n, 2 + 2 * pair))
                    first = 5 * pair
                    for kt in range(QT):
                        if kt == 2:
                            block_ = probs[:, n % 2, first + 4, :].rearrange("p (h t) -> p h t", h=2)[:, :, 0:P]
                        else:
                            bank, col = first + kt % 2, 0 if kt < 2 else S - P
                            block_ = probs[:, n % 2, bank:bank + 3:2, col:col + P]
                        pool.affine_select(out=block_, in_=block_, compare_op=ALU.is_ge, fill=0.0, base=0,
                                           pattern=[[0, 2], [1, P]], channel_multiplier=-1).then_inc(masked.sem, 1)

            for n in range(UNITS + NG):
                if n < UNITS:
                    if n >= 2:
                        pool.wait_ge(mixed.sem, mixed.done(n - 2))
                    b, g = divmod(n, NG)
                    pool.tensor_copy(vals[:, n % 2, :, 0:HD].rearrange("p (j h) d -> p j h d", j=QT),
                                     k.v_all[:, b, :, g * GH * HD:(g + 1) * GH * HD].rearrange("p j (h d) -> p j h d", h=GH))\
                        .then_inc(vals_ready.sem, 1)
                    for c in range(layer + 1):
                        m = n * (layer + 1) + c
                        if m >= 4:
                            pool.wait_ge(gathered[m % 4].sem, m // 4 * 16)
                        pool.indirect_dma_start(moe[:, c * NT + n, :], None, src,
                                                bass.IndirectOffsetOnAxis(ap=k.rank_row[:, c * NT + n:c * NT + n + 1], axis=0))\
                            .then_inc(gathered[m % 4].sem, 16)
                if layer == 0 and n >= 6 and (n - 6) % NG == 0:
                    second_norm((n - 6) // NG)
                if n < UNITS:
                    mask(n)
                if layer == 0 and n >= 6 and (n - 6) % NG == 0:
                    second_gain((n - 6) // NG)
                if layer == 1 and n >= NG and n % NG == 0:
                    join_branches(n // NG - 1)
            for i in range(4):
                pool.wait_ge(gathered[i].sem, UNITS * (layer + 1) // 4 * 16)

        @block.scalar
        def _(act):
            def exponentials(u, c):
                act.wait_ge(prob_ps.sem, prob_ps.after(u, c))
                if c == 0 and u.past(2):
                    act.wait_ge(mixed.sem, mixed.done(u - 2))
                bank = PROB + 2 * ((u.par + c) % 2)
                act.activation(probs[:, u.par, 2 * c:2 * c + 2, :], ps[:, bank:bank + 2, :], ACT.Exp)\
                   .then_inc(exped.sem, 1)

            def step(t):
                row_ends = active(t, 5, UNITS) and (t - 5).group == NG - 1
                for c in range(SCH):
                    if active(t, 2, UNITS):
                        exponentials(t - 2, c)
                    if c == 3 and active(t, 3, UNITS):
                        u = t - 3
                        act.wait_ge(mixed.sem, mixed.done(u))
                        if u.past(1):
                            act.wait_ge(mix_turned.sem, mix_turned.done(u - 1))
                        act.copy(mixT[:, :], ps[:, MIX, :]).then_inc(mixT_ready.sem, 1)
                    if c == 2 and row_ends:
                        r = (t - 5).row
                        act.wait_ge(context_turned.sem, context_turned.done(r))
                        act.copy(contextT[:, :], ps[:, TURN, :]).then_inc(contextT_ready.sem, 1)

            in_steps(act, UNITS, DEPTH, step, 2 * NG, 2 * NG)

        @block.tensor
        def _(pe):
            def maxima(u, c):
                if c == 0:
                    pe.wait_ge(loaded[u.group].sem, (u.row + 1) * 32)
                if u.past(1) or c >= 2:
                    pe.wait_ge(maxed.sem, maxed.after(u, c - 2))
                g = u.group
                for h, qt, col in max_chunk(c):
                    last = col + (qt + 1) * P
                    pe.matmul(ps[:, MAXB + c % 2, col:last], q[0:ROWS_K, g, h, qt * P:(qt + 1) * P],
                              ks[0:ROWS_K, g, h, 0:(qt + 1) * P], start=True, stop=False)
                    mm = pe.matmul(ps[:, MAXB + c % 2, last - P:last], k.identb[:, :], k.causal_q[:, :],
                                   start=False, stop=True)
                mm.then_inc(scored.sem, 1)

            def turn_maxima(u):
                pe.wait_ge(parts_done.sem, parts_done.done(u))
                pe.matmul(ps[0:3 * GH * QT, TURN, 0:P], max_parts[:, u.par, :, :].rearrange("p a b -> p (a b)"), k.identb[:, :],
                          start=True, stop=True)\
                  .then_inc(max_turned.sem, 1)

            def probabilities(u, c):
                if c == 0:
                    pe.wait_ge(max_in[u.par].sem, (u.pair + 1) * 16)
                if u.past(1) or c >= 2:
                    pe.wait_ge(exped.sem, exped.after(u, c - 2))
                g = u.group
                for n in (2 * c, 2 * c + 1):
                    bank = PROB + 2 * ((u.par + c) % 2) + n % 2
                    for h, kt, col in prob_bank(n):
                        mm = pe.matmul(ps[:, bank, col:col + S - kt * P], ks[0:ROWS_A, g, h, kt * P:(kt + 1) * P],
                                       q[0:ROWS_A, g, h, kt * P:S], start=True, stop=True)
                mm.then_inc(prob_ps.sem, 1)

            def mix(u, kt):
                pe.wait_ge(masked.sem, masked.after(u, QT + kt))
                if kt == 0:
                    pe.wait_ge(vals_ready.sem, vals_ready.done(u))
                    if u.past(1):
                        pe.wait_ge(mixT_ready.sem, mixT_ready.done(u - 1))
                for h in range(GH):
                    n, col = prob_place[h, kt]
                    mm = pe.matmul(ps[32 * h:32 * h + 32, MIX, kt * P:S], vals[:, u.par, kt * GH + h, :],
                                   probs[:, u.par, n, col:col + S - kt * P], start=(kt == 0), stop=(kt == QT - 1))
                if kt == QT - 1:
                    mm.then_inc(mixed.sem, 1)

            def turn_mix(u):
                pe.wait_ge(mixT_ready.sem, mixT_ready.done(u))
                for j in range(QT):
                    mm = pe.transpose(ps[:, TURN, j * P:(j + 1) * P], mixT[:, j * P:(j + 1) * P], k.ident[:, :])
                mm.then_inc(mix_turned.sem, 1)

            def turn_context(u):
                pe.wait_ge(context_done.sem, context_done.done(u))
                for j in range(QT):
                    mm = pe.transpose(ps[:, TURN, j * P:(j + 1) * P], context[:, u.row_par, j, :], k.ident[:, :])
                mm.then_inc(context_turned.sem, 1)

            def project(u):
                pe.wait_ge(contextT_ready.sem, contextT_ready.done(u.row))
                for j in range(QT):
                    mm = pe.matmul(ps[:, TURN, j * P:(j + 1) * P], contextT[:, j * P:(j + 1) * P], k.wT[:, w_o, :],
                                   start=True, stop=True)
                mm.then_inc(projected.sem, 1)

            def turn_free(t, use):
                if use == 0:
                    if active(t, 2, UNITS):
                        pe.wait_ge(maxT_ready.sem, maxT_ready.done(t - 2))
                    elif active(t, 5, UNITS):
                        pe.wait_ge(context_done.sem, context_done.done(t - 5))
                    if active(t, 6, UNITS) and (t - 6).group == NG - 1:
                        pe.wait_ge(added.sem, added.done((t - 6).row))
                elif active(t, 4, UNITS):
                    pe.wait_ge(context_done.sem, context_done.done(t - 4))
                elif use == 1 and active(t, 2, UNITS):
                    pe.wait_ge(maxT_ready.sem, maxT_ready.done(t - 2))
                if use == 2 and active(t, 1, UNITS):
                    pe.wait_ge(maxT_ready.sem, maxT_ready.done(t - 1))

            def step(t):
                row_ends = active(t, 5, UNITS) and (t - 5).group == NG - 1
                for c in range(MCH):
                    if active(t, 0, UNITS):
                        maxima(t, c)
                    if c % 2 and active(t, 2, UNITS):
                        probabilities(t - 2, c // 2)
                    if c % 2 == 0 and c >= 2 and active(t, 3, UNITS):
                        mix(t - 3, c // 2 - 1)
                    if c == 1 and active(t, 4, UNITS):
                        turn_free(t, 0)
                        turn_mix(t - 4)
                    if c == 3 and active(t, 1, UNITS):
                        turn_free(t, 1)
                        turn_maxima(t - 1)
                    if c == 7 and row_ends:
                        turn_free(t, 2)
                        turn_context(t - 5)
                    if c == 9 and row_ends:
                        project(t - 5)

            in_steps(pe, UNITS, DEPTH, step, 2 * NG, 2 * NG)

        @block.vector
        def _(dve):
            fill_slot(dve, 0)

            def reduce(u, c):
                dve.wait_ge(scored.sem, scored.after(u, c))
                bank = ps[:, MAXB + c % 2, :]
                blocks = max_chunk(c)
                if c % 5 == 4:
                    h, qt, _ = blocks[0]
                    out = neg_max[:, u.par, h:h + 2, qt]
                    dve.tensor_reduce(out, bank.rearrange("p (h t) -> p h t", h=2), X_AXIS, ALU.max, negate=True)\
                       .then_inc(maxed.sem, 1)
                    return
                for n, (h, qt, col) in enumerate(blocks):
                    ins = dve.tensor_reduce(neg_max[:, u.par, h, qt:qt + 1], bank[:, col:col + (qt + 1) * P], X_AXIS,
                                            ALU.max, negate=True)
                ins.then_inc(maxed.sem, 1)

            def split_maxima(u, part):
                flat = neg_max[:, u.par, :, :].rearrange("p h j -> p (h j)")
                parts = max_parts[:, u.par, :, :]
                if part == 0:
                    if u.past(2):
                        dve.wait_ge(max_turned.sem, max_turned.done(u - 2))
                    dve.wait_ge(maxed.sem, maxed.done(u))
                    dve.tensor_copy(parts[:, 0, :], flat).then_inc(high_done.sem, 1)
                elif part == 1:
                    dve.wait_ge(high_done.sem, high_done.done(u))
                    dve.tensor_tensor(rest[:, :], flat, parts[:, 0, :], ALU.subtract).then_inc(rest_done.sem, 1)
                elif part == 2:
                    dve.wait_ge(rest_done.sem, rest_done.done(u))
                    dve.tensor_copy(parts[:, 1, :], rest[:, :]).then_inc(mid_done.sem, 1)
                else:
                    dve.wait_ge(mid_done.sem, mid_done.done(u))
                    dve.tensor_tensor(parts[:, 2, :], rest[:, :], parts[:, 1, :], ALU.subtract).then_inc(parts_done.sem, 1)

            def copy_maxima(u):
                dve.wait_ge(max_turned.sem, max_turned.done(u))
                if u.past(2):
                    dve.wait_ge(max_in[u.par].sem, u.pair * 16)
                dve.tensor_copy(maxT[:, u.par, :], ps[0:3 * GH * QT, TURN, 0:P])\
                   .then_inc(maxT_ready.sem, 1)

            def divide(u):
                dve.wait_ge(mix_turned.sem, mix_turned.done(u))
                turned = ps[:, TURN, :].rearrange("p (n f) -> p n f", f=32)
                dve.reciprocal(inv[:, :], turned[:, :, HD]).then_inc(inv_done.sem, 1)
                dve.wait_ge(inv_done.sem, inv_done.done(u))
                out = context[:, u.row_par, :, u.group * GH * HD:(u.group + 1) * GH * HD]
                dve.tensor_tensor(out.rearrange("p j (h d) -> p j h d", h=GH),
                                  turned[:, :, 0:HD].rearrange("p (j h) d -> p j h d", h=GH),
                                  inv[:, :].rearrange("p (j h) -> p j h", h=GH).unsqueeze(3).broadcast_to([P, QT, GH, HD]),
                                  ALU.mult).then_inc(context_done.sem, 1)

            def add_row(u):
                r = u.row
                dve.wait_ge(projected.sem, projected.done(r))
                proj = ps[:, TURN, :].rearrange("p (j d) -> p j d", j=QT)
                here = bass.ds(r * QT, QT)
                if layer == 0:
                    dve.wait_ge(x_in[u.row_par].sem, (r - u.row_par) * 8 + 16)
                    dve.tensor_tensor(k.x_sum[:, here, :], proj, x_tile[:, u.row_par, :, :], ALU.add).then_inc(added.sem, 1)
                    return
                dve.wait_ge(joined.sem, joined.done(r))
                out = k.x_sum[:, here, :]
                dve.tensor_tensor(out, proj, out, ALU.add).then_inc(added.sem, 1)

            def step(t):
                row_ends = active(t, 5, UNITS) and (t - 5).group == NG - 1
                for c in range(MCH):
                    if active(t, 0, UNITS):
                        reduce(t, c)
                    if c < 2 and active(t, 1, UNITS):
                        split_maxima(t - 1, 2 * c)
                        split_maxima(t - 1, 2 * c + 1)
                    if c == 4 and active(t, 1, UNITS):
                        copy_maxima(t - 1)
                    if c == 5 and layer == 0 and row_ends:
                        ln_stats(dve, z_sum, z_stats, z_mv, z_stats_done, z_mv_done, (t - 5).row, z_summed)
                    if c == 2 and active(t, 4, UNITS):
                        divide(t - 4)
                    if c == 8 and layer == 0 and row_ends:
                        ln_apply(dve, z_norm, z_sum, z_mv, z_rstd, z_rstd_done, z_normed, (t - 5).row)
                if row_ends:
                    add_row(t - 5)

            in_steps(dve, UNITS, DEPTH, step, 2 * NG, 2 * NG)


def attend0(nc, k):
    attend(nc, k, 0)


def attend1(nc, k):
    attend(nc, k, 1)




def program(nc, names, args, out, phases=None):
    k = Kept()
    k.arg, k.out = dict(zip(names, args)), out
    with ExitStack() as ctx:
        def dram(name, shape, dtype=F32):
            return nc.dram_tensor(name, shape, dtype).ap()

        def sb(name, shape, dtype=F32):
            return ctx.enter_context(nc.sbuf_tensor(name, shape, dtype))

        k.x_flat = k.arg["L0_attn_x"]
        k.sorted0, k.sorted1 = (dram(f"sorted{i}", [TILES[i] * ROWS, D]) for i in range(2))
        k.done0, k.done1 = (dram(f"done{i}", [TILES[i] * ROWS, D]) for i in range(2))
        k.z = dram("z", [B, S, D])
        k.q_stack, k.k_stack = (dram(f"{n}_stack", [B, NH, K0, S], BF16) for n in "qk")
        k.q_stack1, k.k_stack1 = (dram(f"{n}_stack1", [B, NH, K1, S], BF16) for n in "qk")
        k.wT = sb("wT", [P, 14, D])
        k.gateT = sb("gateT", [P, 2, E])
        k.row = sb("row", [P, 8, D])
        k.col = sb("col", [P, 7])
        k.hscale = sb("hscale", [P, 1])
        k.ident, k.identb = sb("ident", [P, P]), sb("identb", [P, P], BF16)
        k.causal_q, k.causal_k = sb("causal_q", [P, P], BF16), sb("causal_k", [P, P], BF16)
        k.batch_mask = sb("batch_mask", [P, P], BF16)
        k.before, k.ones, k.head_mean = sb("before", [P, P]), sb("ones", [P, P]), sb("head_mean", [P, P])
        k.half, k.ln_eps = sb("half", [P, QT]), sb("ln_eps", [P, QT])
        k.counted_i, k.counted = sb("counted_i", [P, 64], I32), sb("counted", [P, 64])
        k.logits = sb("logits", [P, NT, E])
        k.v_all = sb("v_all", [P, B, QT, D])
        k.rank_row = sb("rank_row", [P, 2 * NT], U32)
        k.tile_expert = sb("tile_expert", [P, 64], I32)
        k.y = sb("y_all", [P, NT, D])
        k.x_sum = sb("x_sum", [P, NT, D])
        k.scattered, k.gathered = ([[Signal(ctx.enter_context(nc.semaphore(f"{name}{layer}_{i}")), by=16) for i in range(4)]
                                    for layer in range(2)] for name in ("scattered", "gathered"))
        for phase in phases or PHASES:
            phase(nc, k)


PHASES = (setup, mix0, route0, prepare0, experts0, attend0, norm1, route_and_prepare1, experts1, attend1)

_INS = ['L0_attn_x', 'L0_attn_Wq_amp', 'L0_attn_Wk_amp', 'L0_attn_Wq_phi', 'L0_attn_Wk_phi', 'L0_attn_Wv',
        'L0_attn_Wo', 'L0_attn_score_log_scale', 'L0_ffn_Wqkv', 'L0_ffn_bqkv', 'L0_ffn_Wo', 'L0_ffn_bo',
        'L0_ffn_g1', 'L0_ffn_be1', 'L0_ffn_g2', 'L0_ffn_be2', 'L0_ffn_Wg', 'L0_ffn_W1', 'L0_ffn_b1', 'L0_ffn_W2',
        'L0_ffn_b2', 'L1_attn_Wq', 'L1_attn_bq', 'L1_attn_Wk', 'L1_attn_bk', 'L1_attn_Wv', 'L1_attn_bv',
        'L1_attn_Wo', 'L1_attn_bo', 'L1_ffn_gate_w', 'L1_ffn_w1', 'L1_ffn_w2', 'L1_ffn_w3']
_OUTS = [((8, 512, 128), 'float32')]


def kernel(**inputs):
    import numpy as _np
    import concourse.bacc as _bacc
    from concourse import mybir as _mybir
    from concourse.bass_utils import run_bass_kernel_spmd as _run

    nc = _bacc.Bacc("TRN2", target_bir_lowering=False, num_devices=1)
    arrays, args = {}, []
    for name in _INS:
        a = _np.ascontiguousarray(inputs[name])
        arrays[f"in_{name}_dram"] = a
        args.append(nc.dram_tensor(f"in_{name}_dram", a.shape, _mybir.dt.from_np(a.dtype), kind="ExternalInput").ap())
    for i, (shape, dtype) in enumerate(_OUTS):
        dt = _mybir.dt.from_np(_np.dtype(dtype))
        args.append(nc.dram_tensor(f"out_{i}_dram", shape, dt, kind="ExternalOutput").ap())
    program(nc, _INS, args[:-1], args[-1])
    r = _run(nc, [arrays], core_ids=[0])
    got = tuple(r.results[0][f"out_{i}_dram"] for i in range(len(_OUTS)))
    return got[0]
```
